# Optimizing a Trainium2 kernel written in Bass

```python
import numpy as np
import jax
import jax.numpy as jnp

def _softmax(x, axis=-1):
    return jax.nn.softmax(x, axis=axis)

def _gelu(x):
    return jax.nn.gelu(x, approximate=True)

def _silu(x):
    return jax.nn.silu(x)

def _sigmoid(x):
    return jax.nn.sigmoid(x)

def _layernorm(x, axis=-1, eps=1e-05):
    m = jnp.mean(x, axis=axis, keepdims=True)
    v = jnp.var(x, axis=axis, keepdims=True)
    return (x - m) / jnp.sqrt(v + eps)

def _scatter_add(tgt, idx, src, axis=0):
    return tgt.at[idx].add(src)

def _segment_sum(src, seg, n):
    return jax.ops.segment_sum(src, seg, n)
kernel_name = 'mk_macaron_d1_jaxref_r8_1a96ea'

def setup_inputs(seed: int=0):
    np.random.seed(seed)
    _w = jnp.asarray

    def _L0_attn_setup():
        import jax, jax.numpy as jnp
        import numpy as np
        B, L = (2, 128)
        D_MODEL, D_CKV, D_CQ = (128, 32, 64)
        N_HEAD, D_HEAD, D_ROPE = (8, 64, 32)
        N_IDX_HEAD = 4
        K_TS, LW = (96, 64)
        ROPE_BASE = 10000.0

        def _pope(x, angles):
            cos, sin = (jnp.cos(angles), jnp.sin(angles))
            mu1, mu2 = jnp.split(jax.nn.softplus(x), 2, axis=-1)
            return jnp.concatenate([mu1 * cos - mu2 * sin, mu1 * sin + mu2 * cos], axis=-1)

        def _forward(x, W_dkv, W_uk, W_uv, W_dq, W_uq, W_qr, W_kr, W_out, idx_wq, idx_wk, idx_w, raw_delta):
            B_, L_, _ = x.shape
            c_kv = x @ W_dkv
            q_i = (x @ idx_wq).reshape(B_, L_, N_IDX_HEAD, D_HEAD)
            k_i = x @ idx_wk
            s_i = jax.nn.relu(jnp.einsum('bthd,bsd->bths', q_i, k_i))
            I = jnp.einsum('bths,h->bts', s_i, idx_w)
            qpos = jnp.arange(L_)[:, None]
            kpos = jnp.arange(L_)[None, :]
            local = (kpos >= qpos - LW + 1) & (kpos <= qpos)
            causal = kpos > qpos
            I = jnp.where(local[None], jnp.inf, I)
            I = jnp.where(causal[None], -jnp.inf, I)
            kk = min(K_TS, L_)
            _, idx = jax.lax.top_k(I, kk)
            bi = jnp.arange(B_)[:, None, None]
            key_c = (c_kv @ W_uk)[bi, idx].reshape(B_, L_, kk, N_HEAD, D_HEAD)
            value = (c_kv @ W_uv)[bi, idx].reshape(B_, L_, kk, N_HEAD, D_HEAD)
            c_q = x @ W_dq
            query_c = (c_q @ W_uq).reshape(B_, L_, N_HEAD, D_HEAD)
            half = D_ROPE // 2
            theta = 1.0 / ROPE_BASE ** (2.0 * jnp.arange(half, dtype=jnp.float32) / D_ROPE)
            delta = -2.0 * jnp.pi * jax.nn.sigmoid(raw_delta)
            angles_q = jnp.arange(L_, dtype=jnp.float32)[:, None] * theta[None, :] + delta
            query_r = _pope((c_q @ W_qr).reshape(B_, L_, N_HEAD, D_ROPE), angles_q[None, :, None, :])
            kr_sel = (x @ W_kr)[bi, idx]
            angles_k = jnp.arange(kk, dtype=jnp.float32)[:, None] * theta[None, :] + delta
            key_r = _pope(kr_sel, angles_k[None, None, :, :])
            scale = (D_HEAD + D_ROPE) ** (-0.5)
            q_c = query_c.transpose(0, 2, 1, 3)
            q_r = query_r.transpose(0, 2, 1, 3)
            k_c = key_c.transpose(0, 3, 1, 2, 4)
            v = value.transpose(0, 3, 1, 2, 4)
            scores = (jnp.einsum('bhld,bhlkd->bhlk', q_c, k_c) + jnp.einsum('bhld,blkd->bhlk', q_r, key_r)) * scale
            attn = jax.nn.softmax(scores.astype(jnp.float32), axis=-1).astype(v.dtype)
            out = jnp.einsum('bhlk,bhlkd->bhld', attn, v)
            out = out.transpose(0, 2, 1, 3).reshape(B_, L_, N_HEAD * D_HEAD)
            return out @ W_out
        key = jax.random.key(seed)
        ks = jax.random.split(key, 14)

        def w(k, shape, fan_in):
            return jax.random.normal(k, shape, dtype=jnp.float32) * fan_in ** (-0.5)
        return {'x': jax.random.normal(ks[0], (B, L, D_MODEL), dtype=jnp.float32), 'W_dkv': w(ks[1], (D_MODEL, D_CKV), D_MODEL), 'W_uk': w(ks[2], (D_CKV, N_HEAD * D_HEAD), D_CKV), 'W_uv': w(ks[3], (D_CKV, N_HEAD * D_HEAD), D_CKV), 'W_dq': w(ks[4], (D_MODEL, D_CQ), D_MODEL), 'W_uq': w(ks[5], (D_CQ, N_HEAD * D_HEAD), D_CQ), 'W_qr': w(ks[6], (D_CQ, N_HEAD * D_ROPE), D_CQ), 'W_kr': w(ks[7], (D_MODEL, D_ROPE), D_MODEL), 'W_out': w(ks[8], (N_HEAD * D_HEAD, D_MODEL), N_HEAD * D_HEAD), 'idx_wq': w(ks[9], (D_MODEL, N_IDX_HEAD * D_HEAD), D_MODEL), 'idx_wk': w(ks[10], (D_MODEL, D_HEAD), D_MODEL), 'idx_w': jnp.ones((N_IDX_HEAD,), dtype=jnp.float32), 'raw_delta': jax.random.normal(ks[11], (D_ROPE // 2,), dtype=jnp.float32) * 0.1}
    _L0_attn_in = _L0_attn_setup()

    def _L0_ffn_setup():
        import jax, jax.numpy as jnp
        import numpy as np
        B, S, D, H, E, K, F = (1, 128, 128, 16, 8, 2, 512)

        def layernorm(x, g, b, eps=1e-05):
            m = x.mean(-1, keepdims=True)
            v = ((x - m) ** 2).mean(-1, keepdims=True)
            return (x - m) * jax.lax.rsqrt(v + eps) * g + b
        key = jax.random.key(seed)
        ks = jax.random.split(key, 8)
        n = lambda k, shape, sc: jax.random.normal(k, shape, dtype=jnp.float32) * sc
        return {'x': n(ks[0], (B, S, D), 1.0), 'w_qkv': n(ks[1], (D, 3 * D), D ** (-0.5)), 'w_o': n(ks[2], (D, D), D ** (-0.5)), 'g1': jnp.ones((D,), jnp.float32), 'b1': jnp.zeros((D,), jnp.float32), 'wg': n(ks[3], (D, E), D ** (-0.5)), 'w1': n(ks[4], (E, D, F), D ** (-0.5)), 'bb1': jnp.zeros((E, F), jnp.float32), 'w2': n(ks[5], (E, F, D), F ** (-0.5)), 'bb2': jnp.zeros((E, D), jnp.float32), 'g2': jnp.ones((D,), jnp.float32), 'b2': jnp.zeros((D,), jnp.float32)}
    _L0_ffn_in = _L0_ffn_setup()
    _d = {'L0_attn_x': _L0_attn_in['x'], 'L0_attn_W_dkv': _L0_attn_in['W_dkv'], 'L0_attn_W_uk': _L0_attn_in['W_uk'], 'L0_attn_W_uv': _L0_attn_in['W_uv'], 'L0_attn_W_dq': _L0_attn_in['W_dq'], 'L0_attn_W_uq': _L0_attn_in['W_uq'], 'L0_attn_W_qr': _L0_attn_in['W_qr'], 'L0_attn_W_kr': _L0_attn_in['W_kr'], 'L0_attn_W_out': _L0_attn_in['W_out'], 'L0_attn_idx_wq': _L0_attn_in['idx_wq'], 'L0_attn_idx_wk': _L0_attn_in['idx_wk'], 'L0_attn_idx_w': _L0_attn_in['idx_w'], 'L0_attn_raw_delta': _L0_attn_in['raw_delta'], 'L0_ffn_w_qkv': _L0_ffn_in['w_qkv'], 'L0_ffn_w_o': _L0_ffn_in['w_o'], 'L0_ffn_g1': _L0_ffn_in['g1'], 'L0_ffn_b1': _L0_ffn_in['b1'], 'L0_ffn_wg': _L0_ffn_in['wg'], 'L0_ffn_w1': _L0_ffn_in['w1'], 'L0_ffn_bb1': _L0_ffn_in['bb1'], 'L0_ffn_w2': _L0_ffn_in['w2'], 'L0_ffn_bb2': _L0_ffn_in['bb2'], 'L0_ffn_g2': _L0_ffn_in['g2'], 'L0_ffn_b2': _L0_ffn_in['b2']}
    _x0 = _d['L0_attn_x']
    _d['L0_attn_x'] = jax.random.normal(jax.random.fold_in(jax.random.key(seed), 1), (2, 1024, 128), dtype=_x0.dtype)
    del _x0
    return _d

def reference(L0_attn_x, L0_attn_W_dkv, L0_attn_W_uk, L0_attn_W_uv, L0_attn_W_dq, L0_attn_W_uq, L0_attn_W_qr, L0_attn_W_kr, L0_attn_W_out, L0_attn_idx_wq, L0_attn_idx_wk, L0_attn_idx_w, L0_attn_raw_delta, L0_ffn_w_qkv, L0_ffn_w_o, L0_ffn_g1, L0_ffn_b1, L0_ffn_wg, L0_ffn_w1, L0_ffn_bb1, L0_ffn_w2, L0_ffn_bb2, L0_ffn_g2, L0_ffn_b2):

    def _L0_attn_ref(x, W_dkv, W_uk, W_uv, W_dq, W_uq, W_qr, W_kr, W_out, idx_wq, idx_wk, idx_w, raw_delta):
        import jax, jax.numpy as jnp
        import numpy as np
        B, L = (2, 128)
        D_MODEL, D_CKV, D_CQ = (128, 32, 64)
        N_HEAD, D_HEAD, D_ROPE = (8, 64, 32)
        N_IDX_HEAD = 4
        K_TS, LW = (96, 64)
        ROPE_BASE = 10000.0

        def _pope(x, angles):
            cos, sin = (jnp.cos(angles), jnp.sin(angles))
            mu1, mu2 = jnp.split(jax.nn.softplus(x), 2, axis=-1)
            return jnp.concatenate([mu1 * cos - mu2 * sin, mu1 * sin + mu2 * cos], axis=-1)

        def _forward(x, W_dkv, W_uk, W_uv, W_dq, W_uq, W_qr, W_kr, W_out, idx_wq, idx_wk, idx_w, raw_delta):
            B_, L_, _ = x.shape
            c_kv = x @ W_dkv
            q_i = (x @ idx_wq).reshape(B_, L_, N_IDX_HEAD, D_HEAD)
            k_i = x @ idx_wk
            s_i = jax.nn.relu(jnp.einsum('bthd,bsd->bths', q_i, k_i))
            I = jnp.einsum('bths,h->bts', s_i, idx_w)
            qpos = jnp.arange(L_)[:, None]
            kpos = jnp.arange(L_)[None, :]
            local = (kpos >= qpos - LW + 1) & (kpos <= qpos)
            causal = kpos > qpos
            I = jnp.where(local[None], jnp.inf, I)
            I = jnp.where(causal[None], -jnp.inf, I)
            kk = min(K_TS, L_)
            _, idx = jax.lax.top_k(I, kk)
            bi = jnp.arange(B_)[:, None, None]
            key_c = (c_kv @ W_uk)[bi, idx].reshape(B_, L_, kk, N_HEAD, D_HEAD)
            value = (c_kv @ W_uv)[bi, idx].reshape(B_, L_, kk, N_HEAD, D_HEAD)
            c_q = x @ W_dq
            query_c = (c_q @ W_uq).reshape(B_, L_, N_HEAD, D_HEAD)
            half = D_ROPE // 2
            theta = 1.0 / ROPE_BASE ** (2.0 * jnp.arange(half, dtype=jnp.float32) / D_ROPE)
            delta = -2.0 * jnp.pi * jax.nn.sigmoid(raw_delta)
            angles_q = jnp.arange(L_, dtype=jnp.float32)[:, None] * theta[None, :] + delta
            query_r = _pope((c_q @ W_qr).reshape(B_, L_, N_HEAD, D_ROPE), angles_q[None, :, None, :])
            kr_sel = (x @ W_kr)[bi, idx]
            angles_k = jnp.arange(kk, dtype=jnp.float32)[:, None] * theta[None, :] + delta
            key_r = _pope(kr_sel, angles_k[None, None, :, :])
            scale = (D_HEAD + D_ROPE) ** (-0.5)
            q_c = query_c.transpose(0, 2, 1, 3)
            q_r = query_r.transpose(0, 2, 1, 3)
            k_c = key_c.transpose(0, 3, 1, 2, 4)
            v = value.transpose(0, 3, 1, 2, 4)
            scores = (jnp.einsum('bhld,bhlkd->bhlk', q_c, k_c) + jnp.einsum('bhld,blkd->bhlk', q_r, key_r)) * scale
            attn = jax.nn.softmax(scores.astype(jnp.float32), axis=-1).astype(v.dtype)
            out = jnp.einsum('bhlk,bhlkd->bhld', attn, v)
            out = out.transpose(0, 2, 1, 3).reshape(B_, L_, N_HEAD * D_HEAD)
            return out @ W_out
        return _forward(x, W_dkv, W_uk, W_uv, W_dq, W_uq, W_qr, W_kr, W_out, idx_wq, idx_wk, idx_w, raw_delta)

    def _L0_ffn_ref(x, w_qkv, w_o, g1, b1, wg, w1, bb1, w2, bb2, g2, b2):
        import jax, jax.numpy as jnp
        import numpy as np
        B, S, D, H, E, K, F = (1, 128, 128, 16, 8, 2, 512)

        def layernorm(x, g, b, eps=1e-05):
            m = x.mean(-1, keepdims=True)
            v = ((x - m) ** 2).mean(-1, keepdims=True)
            return (x - m) * jax.lax.rsqrt(v + eps) * g + b
        b, s, d = x.shape
        hd = d // H
        qkv = x @ w_qkv
        q, k, v = jnp.split(qkv, 3, axis=-1)
        to_heads = lambda t: t.reshape(b, s, H, hd).transpose(0, 2, 1, 3)
        q, k, v = (to_heads(q), to_heads(k), to_heads(v))
        scores = jnp.einsum('bhqd,bhkd->bhqk', q, k) / jnp.sqrt(jnp.float32(hd))
        causal = jnp.tril(jnp.ones((s, s), bool))
        scores = jnp.where(causal, scores, jnp.finfo(scores.dtype).min)
        attn = jax.nn.softmax(scores, axis=-1)
        o = jnp.einsum('bhqk,bhkd->bhqd', attn, v)
        o = o.transpose(0, 2, 1, 3).reshape(b, s, d) @ w_o
        h = layernorm(x + o, g1, b1)
        probs = jax.nn.softmax(h @ wg, axis=-1)
        topv, topi = jax.lax.top_k(probs, K)
        topv = topv / topv.sum(-1, keepdims=True)
        w = (topv[..., None] * jax.nn.one_hot(topi, E, dtype=h.dtype)).sum(-2)
        h1 = jax.nn.gelu(jnp.einsum('bsd,edf->ebsf', h, w1) + bb1[:, None, None, :])
        y = jnp.einsum('ebsf,efd->ebsd', h1, w2) + bb2[:, None, None, :]
        moe = jnp.einsum('ebsd,bse->bsd', y, w)
        return layernorm(h + moe, g2, b2)
    x = L0_attn_x
    x = x + 0.5 * _L0_ffn_ref(_layernorm(x, axis=-1), L0_ffn_w_qkv, L0_ffn_w_o, L0_ffn_g1, L0_ffn_b1, L0_ffn_wg, L0_ffn_w1, L0_ffn_bb1, L0_ffn_w2, L0_ffn_bb2, L0_ffn_g2, L0_ffn_b2)
    x = x + _L0_attn_ref(_layernorm(x, axis=-1), L0_attn_W_dkv, L0_attn_W_uk, L0_attn_W_uv, L0_attn_W_dq, L0_attn_W_uq, L0_attn_W_qr, L0_attn_W_kr, L0_attn_W_out, L0_attn_idx_wq, L0_attn_idx_wk, L0_attn_idx_w, L0_attn_raw_delta)
    x = x + 0.5 * _L0_ffn_ref(_layernorm(x, axis=-1), L0_ffn_w_qkv, L0_ffn_w_o, L0_ffn_g1, L0_ffn_b1, L0_ffn_wg, L0_ffn_w1, L0_ffn_bb1, L0_ffn_w2, L0_ffn_bb2, L0_ffn_g2, L0_ffn_b2)
    return x

_drawn_inputs = setup_inputs


def setup_inputs(seed=0):
    import zlib

    import numpy as np

    out = dict(_drawn_inputs(seed))
    spreads = {'L0_attn_idx_w': (1.0, 0.2),
     'L0_ffn_g1': (1.0, 0.2),
     'L0_ffn_b1': (0.0, 0.1),
     'L0_ffn_bb1': (0.0, 0.1),
     'L0_ffn_bb2': (0.0, 0.1),
     'L0_ffn_g2': (1.0, 0.2),
     'L0_ffn_b2': (0.0, 0.1)}
    factors = {}
    for name, (base, spread) in spreads.items():
        noise = np.random.default_rng([zlib.crc32(name.encode()), seed]).standard_normal(out[name].shape)
        drawn = base * np.exp(spread * noise) if base else spread * noise
        out[name] = jnp.asarray(drawn.astype(out[name].dtype))
    for name, factor in factors.items():
        out[name] = (out[name] * factor).astype(out[name].dtype)
    return out
```

```python
from contextlib import ExitStack

import numpy as np

import concourse.bass as bass
from concourse import mybir

F32 = mybir.dt.float32
BF16 = mybir.dt.bfloat16
U32 = mybir.dt.uint32
ALU = mybir.AluOpType
ACT = mybir.ActivationFunctionType
AX_X = mybir.AxisListType.X

P = 128
B, L, D = 2, 1024, 128
TOK = B * L
NT = TOK // P
TB = L // P
BANK = 512
NG = TOK // BANK

H, HD = 16, 8
PAIRS = B * H // 2
E, F = 8, 512
FC = F // P
FFN_EPS = 1e-5
NEG = -1.0e30
PARTS_Q = (0, 0, 0, 1, 1, 1, 2, 2, 2)
PARTS_K = (0, 1, 2, 0, 1, 2, 0, 1, 2)
NPROD = len(PARTS_Q)
STRIP = 32
MAXROWS = 3
ROWS = MAXROWS + NPROD * HD

NH, DH, DC, DCQ, DR = 8, 64, 32, 64, 32
NIH = 4
LW, KTS = 64, 96
NSEL = KTS - LW
HALF = DR // 2
BT = 16
NB = L // BT
GB = BT // 4
LP = L + P - BT
ROWKV = DC + 2 * DR
SCALE2 = float((DH + DR) ** -0.5)

PT_RING = 8
S_RING = 3
PAIR_LOOPS = ((0, TB // 2), (1, TB // 2 - 1))
UNITS1 = [(s, t, hf) for t in range(TB) for s in range(2) for hf in range(2) if hf * BANK < (t + 1) * P]
UNITS2 = [(s, kc, hf) for kc in range(TB) for hf in range(2) for s in range(2) if (hf + 1) * BANK > kc * P]
N1, N2 = len(UNITS1), len(UNITS2)

ARENA = 136 * 1024


def constants():
    f = np.float32
    q, k = np.arange(P)[:, None], np.arange(P)[None, :]
    sel = LW + np.arange(NSEL)[None, :]
    override = sel > q
    g, h, t = (a.reshape(-1, 1) for a in np.meshgrid(np.arange(GB), np.arange(NH), np.arange(4), indexing="ij"))
    tok = 4 * g + t
    early, main = k < LW, (k >= tok + 1) & (k <= tok + LW)
    own = (k // NSEL) == t
    theta = (1.0 / f(10000.0) ** (f(2.0) * np.arange(HALF, dtype=f) / f(DR))).astype(f).astype(np.float64)
    a_sel = (LW + np.arange(P) % NSEL)[:, None] * theta[None, :]
    sign = np.where(np.arange(P) % DR < HALF, -1.0, 1.0)[:, None]
    c = {"ident": np.eye(P),
         "mask_qk": np.where(k > q, NEG, 0.0),
         "mask_kq": np.where(q > k, NEG, 0.0),
         "iota8": np.broadcast_to(np.arange(E), (P, E)),
         "nonlocal": np.where(k <= q, 3e38, -3e38),
         "keep": np.where(override, 0.0, 1.0),
         "fill": np.where(override, np.broadcast_to(sel, (P, NSEL)), 0.0),
         "mask_early": np.where(np.concatenate([np.broadcast_to(early, (P, P)), own], 1), 0.0, NEG),
         "mask_main": np.where(np.concatenate([main, own], 1), 0.0, NEG),
         "cos_sel": np.concatenate([np.cos(a_sel)] * 2, 1),
         "sin_sel": np.concatenate([-np.sin(a_sel), np.sin(a_sel)], 1),
         "sign_row": np.broadcast_to(sign[:DR].T, (P, DR)),
         "sign": sign}
    return {n: np.ascontiguousarray(v.astype(f)) for n, v in c.items()}


def rotations():
    theta = (1.0 / np.float32(10000.0) ** (np.float32(2.0) * np.arange(HALF, dtype=np.float32) / np.float32(DR))).astype(np.float32)
    th = np.tile(theta.astype(np.float64), P // HALF)[:, None]
    t = np.arange(L)
    sign = np.where(np.arange(P) % DR < HALF, -1.0, 1.0)[:, None]
    tabs = []
    for pos in (t, np.where(t < LW, t, 2 * t - (LW - 1))):
        a = pos[None, :] * th
        tabs += [np.cos(a), sign * np.sin(a)]
    return np.ascontiguousarray(np.stack(tabs, 1).astype(np.float32))


def const_layout():
    at, off = {}, 0
    for n, v in constants().items():
        at[n] = (off, v.shape[1])
        off += v.shape[1]
    return at, off


def build(nc, ins, const_ap, rot_ap, out):
    at, width = const_layout()
    ffn = {n[7:]: a for n, a in ins.items() if n.startswith("L0_ffn_")}
    attn = {n[8:]: a for n, a in ins.items() if n.startswith("L0_attn_")}
    q_rows = nc.dram_tensor("q_rows", (PAIRS, 2, NPROD * HD, L), BF16, kind="Internal").ap()
    k_rows = nc.dram_tensor("k_rows", (PAIRS, 2, NPROD * HD, L), BF16, kind="Internal").ap()
    kv_rows = nc.dram_tensor("kv_rows", (B * LP, ROWKV), F32, kind="Internal").ap()

    with ExitStack() as ctx:
        def sb(name, shape, dt=F32):
            return ctx.enter_context(nc.sbuf_tensor(name, shape, dt))

        def sem(name):
            return ctx.enter_context(nc.semaphore(name))

        bank = [ctx.enter_context(nc.psum_tensor(f"bank{i}", [P, BANK], F32)) for i in range(8)]

        const = sb("const", [P, width])

        def cst(name):
            o, n = at[name]
            return const[:, o:o + n]

        ident = cst("ident")
        ident_b = sb("ident_b", [P, P], BF16)
        mask_qk = sb("mask_qk_b", [P, P], BF16)
        mask_kq = sb("mask_kq_b", [P, P], BF16)

        X = sb("X", [P, NT, D])
        XN = sb("XN", [P, NT, D])
        XT = sb("XT", [P, TOK])
        ATT = sb("ATT", [P, NT, D])
        ACC = ATT
        HN = sb("HN", [P, NT, D])
        stats = sb("stats", [P, NT, 6])
        mv = sb("mv", [P, NT, 2])
        vareps = sb("vareps", [P, NT])
        rstd = sb("rstd", [P, NT])
        neghalf = sb("neghalf", [P, NT])

        w_qkv = sb("w_qkv", [P, 3 * D])
        w_o = sb("w_o", [P, D])
        wg = sb("wg", [P, E])
        gains = sb("gains", [P, 4, D])
        bb1 = sb("bb1", [P, E, FC])
        bb2 = sb("bb2", [E, D])

        bias1 = [sb(f"bias1_{i}", [P, FC]) for i in range(2)]
        WKV = sb("WKV", [P, 2 * DR + DC])
        WIQ = sb("WIQ", [P, NIH * DH])
        WIK = sb("WIK", [P, 2 * DH])
        WDQ = sb("WDQ", [P, DCQ])
        WQR = sb("WQR", [DCQ, 2, NH * DR])
        AQ = sb("AQ", [DCQ, NH * DC])
        MO = sb("MO", [DC, NH, D])
        UQT = sb("UQT", [P, NH // 2, DCQ])
        UKT = sb("UKT", [P, NH // 2, DC])
        UVT = sb("UVT", [P, NH // 2, DC])
        WOUT = sb("WOUT", [P, NH // 2, D])
        idx_w = sb("idx_w", [P, NIH])
        delta_col = sb("delta_col", [P, 6])
        delta_row = sb("delta_row", [P, 6, DR])
        rot_sel = sb("rot_sel", [P, 2 * DR])

        arena = sb("arena", [P, ARENA // 4])
        views = {}

        def view(part, shape, dt=F32, rows=P):
            n = int(np.prod(shape)) * (2 if dt == BF16 else 4) // 4
            off = views.get(part, 0)
            views[part] = off + n
            assert off + n <= ARENA // 4, (part, off + n)
            v = arena[0:rows, off:off + n]
            v = v if dt == F32 else v.bitcast(dt)
            if len(shape) == 1:
                return v
            names = "abcd"[:len(shape)]
            sizes = {x: m for x, m in zip(names, shape)}
            return v.rearrange(f"p ({' '.join(names)}) -> p {' '.join(names)}", **sizes)

        qparts = view("ffn", (3, TOK), BF16)
        kparts = view("ffn", (3, TOK), BF16)
        rest = view("ffn", (2, BANK))
        VA = view("ffn", (PAIRS, 2, TB, STRIP))
        QB = [[view("ffn", (L,), BF16) for h in range(2)] for i in range(2)]
        KB = [[view("ffn", (L,), BF16) for h in range(2)] for i in range(2)]
        VS = [view("ffn", (2, TB, STRIP)) for i in range(2)]
        OT = view("ffn", (BANK,))
        PT = [view("ffn", (BANK,)) for i in range(PT_RING)]
        rowmax = view("ffn", (2, 2, TB))
        maxrest = view("ffn", (2, TB))
        MB = view("ffn", (TB, P), BF16)
        rsum = view("ffn", (2, 2, 4))
        W1 = [view("ffn", (F,)) for i in range(2)]
        W2 = [view("ffn", (FC, D)) for i in range(2)]
        H1 = [view("ffn", (FC, BANK)) for i in range(2)]
        WT = view("ffn", (TOK,), rows=E)

        QALL = view("sel", (NH, TOK), rows=96)
        OA = QALL[0:DC]
        RAW = QALL.rearrange("p h t -> p (h t)")
        KL = view("sel", (B, LP), rows=96)
        KVS = view("sel", (NT, ROWKV))
        G = [view("sel", (GB, ROWKV)) for i in range(4)]
        QS = [view("sel", (P,), rows=96) for i in range(2)]
        GTS = [view("sel", (GB, P), rows=ROWKV) for i in range(2)]
        PRD = view("sel", (GB, 2 * DR))
        SM = [view("sel", (2 * P,)) for i in range(2)]
        PB = [view("sel", (2 * P,)) for i in range(2)]
        PTS = [view("sel", (2 * P,)) for i in range(2)]
        VW = [view("sel", (DC,)) for i in range(4)]
        IDX = view("sel", (NT * P // 4,)).bitcast(U32)
        IB = [view("sel", (GB,)).bitcast(U32) for i in range(4)]
        col = view("sel", (2, 4))
        SC = view("sel", (L,))
        RL = [view("sel", (L,)) for i in range(2)]
        best = view("sel", (4, 8))
        bidx = view("sel", (4, 8)).bitcast(U32)
        bidf = view("sel", (2, NSEL))
        views["sel2"] = views["sel"]
        QI = view("sel", (2, TOK))
        KI = view("sel", (TOK,))
        CQ = view("sel2", (TOK,), rows=DCQ)
        ROT = view("sel2", (4, L))
        ATTf = ATT[:, :, :].rearrange("p t d -> p (t d)")
        HNf = HN[:, :, :].rearrange("p t d -> p (t d)")
        XNf = XN[:, :, :].rearrange("p t d -> p (t d)")
        MU, MUS, QT, T1, QRD, QRL = ATTf[:, 0:L], ATTf[:, L:], HNf[:, 0:L], HNf[:, L:], XNf[:, 0:L], XNf[:, L:]
        lg = sb("lg", [P, NT, E])
        pr = sb("pr", [P, NT, E])
        top8 = sb("top8", [P, NT, 8])
        idx8 = sb("idx8", [P, NT, 8], U32)
        idxf = sb("idxf", [P, NT, 2])
        g16 = sb("g16", [P, 4, NT])
        oh = sb("oh", [P, 2, NT, E])
        W8 = sb("W8", [P, NT, E])
        spare = sb("spare", [P, 20])

        x_loaded, const_loaded, w_loaded, sel_w_loaded = (sem(n) for n in ("x_loaded", "const_loaded", "w_loaded", "sel_w_loaded"))
        setup_done, filled = sem("setup_done"), sem("filled")
        var_ready, rstd_ready = sem("var_ready"), sem("rstd_ready")
        xn_ready, h_ready = sem("xn_ready"), sem("h_ready")
        turned, xt_ready = sem("turned"), sem("xt_ready")
        qk_done, p1_done, r1_done, p2_done, p3_done = (sem(n) for n in ("qk_done", "p1_done", "r1_done", "p2_done", "p3_done"))
        v_done, va_ready = sem("v_done"), sem("va_ready")
        rows_spilled = sem("rows_spilled")
        rows_loaded = [sem(f"rows_loaded{i}") for i in range(2)]
        cleared, s1_done, max_done, mb_ready, mt_done = (sem(n) for n in ("cleared", "s1_done", "max_done", "mb_ready", "mt_done"))
        maxrow0, maxrow1 = sem("maxrow0"), sem("maxrow1")
        st_done, exp_done, pv_done, ot_ready, o_turned, att_done = (sem(n) for n in ("st_done", "exp_done", "pv_done", "ot_ready", "o_turned", "att_done"))
        o_done, r_done, gate_done, lg_ready, eg_ready, w8_ready = (sem(n) for n in ("o_done", "r_done", "gate_done", "lg_ready", "eg_ready", "w8_ready"))
        w8_turned, wt_ready, b2_done, acc0_ready = (sem(n) for n in ("w8_turned", "wt_ready", "b2_done", "acc0_ready"))
        a_done, gelu_done, y_done, acc_done = (sem(n) for n in ("a_done", "gelu_done", "y_done", "acc_done"))
        ew_loaded = [sem(f"ew_loaded{i}") for i in range(2)]
        x_ready = sem("x_ready")
        stored = sem("stored")
        raw_loaded, uqk_turned, uqk_ready, prep_done, prep_ready = (sem(n) for n in ("raw_loaded", "uqk_turned", "uqk_ready", "prep_done", "prep_ready"))
        delta_loaded, sig_ready, ang_ready, trig_ready, rot_sel_ready = (sem(n) for n in ("delta_loaded", "sig_ready", "ang_ready", "trig_ready", "rot_sel_ready"))
        qi_done, qi_ready, ki_done, ki_ready = (sem(n) for n in ("qi_done", "qi_ready", "ki_done", "ki_ready"))
        kv_done, kv_log, kv_ready, kv_stored, kv_padded = (sem(n) for n in ("kv_done", "kv_log", "kv_ready", "kv_stored", "kv_padded"))
        si_done, relu_done, sc_used, best_ready, i_turned, idx_ready = (sem(n) for n in ("si_done", "relu_done", "sc_used", "best_ready", "i_turned", "idx_ready"))
        rot_loaded, rot_ready, cq_done, cq_ready = (sem(n) for n in ("rot_loaded", "rot_ready", "cq_done", "cq_ready"))
        kt_done, kt_log, kt_mu, kt_c, kl_ready = (sem(n) for n in ("kt_done", "kt_log", "kt_mu", "kt_c", "kl_ready"))
        qt_done, qt_ready, mu_done, mu_log, mu_ready, qr_ready = (sem(n) for n in ("qt_done", "qt_ready", "mu_done", "mu_log", "mu_ready", "qr_ready"))
        q_placed = sem("q_placed")
        vw_loaded = [sem(f"vw_loaded{i}") for i in range(4)]
        gathered = [sem(f"gathered{i}") for i in range(4)]
        staged = sem("staged")
        qs_ready, rot_done, gt_done, gts_ready, s_done, sm_ready = (sem(n) for n in ("qs_ready", "rot_done", "gt_done", "gts_ready", "s_done", "sm_ready"))
        pb_exp, pn_ready, tp_done, pts_ready, ob_done, oa_ready = (sem(n) for n in ("pb_exp", "pn_ready", "tp_done", "pts_ready", "ob_done", "oa_ready"))
        mix_done = sem("mix_done")
        C0 = 4

        EXP0, PV0, ATT0, GELU0, Y0, ACC0, MAX0, OTURN0 = S_RING, 2 * TB, 1, 4, 2, 2, S_RING, 1
        block = ctx.enter_context(nc.Block())

        w1_d, w2_d = ffn["w1"], ffn["w2"].rearrange("e (c p) d -> e p c d", p=P)

        def sp_rows(sp, g, it, buf):
            sp.wait_ge(pv_done, PV0 + TB * (g + it - 1))
            for s in range(2):
                for dst, src in ((QB, q_rows), (KB, k_rows)):
                    sp.dma_start(dst[buf][s][MAXROWS:ROWS, :], src[bass.ds(it, 1), s].rearrange("a r t -> (a r) t")
                                 if not isinstance(it, int) else src[it, s]).then_inc(rows_loaded[buf], 16)
            va = VA[:, :, :, :, :].rearrange("p a s k d -> p (a s k d)")
            n = 2 * TB * STRIP
            sp.dma_start(VS[buf][:, :, :, :].rearrange("p s k d -> p (s k d)"), va[:, bass.ds(it * n, n)]).then_inc(rows_loaded[buf], 16)

        def sp_expert(sp, c, e, buf):
            if not isinstance(e, int) or c or e >= 2:
                sp.wait_ge(y_done, Y0 + NG * E * c + NG * (e - 1))
            w1e = w1_d[e] if isinstance(e, int) else w1_d[bass.ds(e, 1)].rearrange("a d f -> (a d) f")
            w2e = w2_d[e] if isinstance(e, int) else w2_d[bass.ds(e, 1)].rearrange("a p c d -> p (a c) d")
            sp.dma_start(W1[buf], w1e).then_inc(ew_loaded[buf], 16)
            sp.dma_start(W2[buf], w2e).then_inc(ew_loaded[buf], 16)

        def sp_ffn(sp, c):
            if c:
                sp.wait_ge(x_ready, 2)
            sp_expert(sp, c, 0, 0)
            sp_expert(sp, c, 1, 1)
            sp.wait_ge(p3_done, 8 * (c + 1))
            for src, pick, dst in ((qparts, PARTS_Q, q_rows), (kparts, PARTS_K, k_rows)):
                for r, part in enumerate(pick):
                    for b in range(B):
                        d = dst[b * (PAIRS // B):(b + 1) * (PAIRS // B), :, r * HD:(r + 1) * HD, :]
                        sp.dma_start(d.rearrange("j s d t -> (j s) d t"), src[:, part, b * L:(b + 1) * L])\
                          .then_inc(rows_spilled, 16)
            sp.wait_ge(rows_spilled, 2 * NPROD * B * 16 * (c + 1))
            sp.wait_ge(va_ready, NG * (c + 1))
            sp.wait_ge(filled, c + 1)
            g = PAIRS * c
            sp_rows(sp, g, 0, 0)
            sp_rows(sp, g, 1, 1)
            with sp.Fori(1, PAIRS // 2) as i:
                sp_rows(sp, g, i * 2, 0)
                sp_rows(sp, g, i * 2 + 1, 1)
            with sp.Fori(1, E // 2) as i:
                sp_expert(sp, c, i * 2, 0)
                sp_expert(sp, c, i * 2 + 1, 1)


        def sp_sel(sp):
            sp.wait_ge(x_ready, 1)
            for dst, src in ((RAW[0:DCQ, 0:NH * DH], attn["W_uq"]), (RAW[0:DC, NH * DH:2 * NH * DH], attn["W_uk"]),
                             (RAW[0:DC, 2 * NH * DH:3 * NH * DH], attn["W_uv"])):
                sp.dma_start(dst, src).then_inc(raw_loaded, 16)
            sp.wait_ge(kv_ready, 4)
            for b in range(B):
                base = b * LP
                sp.dma_start(kv_rows[base + LW:base + LW + L].rearrange("(t p) n -> p t n", p=P),
                             KVS[:, b * TB:(b + 1) * TB, :]).then_inc(kv_stored, 16)
                sp.dma_start(kv_rows[base:base + LW], KVS[0:LW, b * TB, :]).then_inc(kv_stored, 16)
                tail = LP - LW - L
                sp.dma_start(kv_rows[base + LW + L:base + LP], KVS[0:tail, b * TB, :]).then_inc(kv_stored, 16)
            sp.wait_ge(relu_done, NT * NIH)
            sp.wait_ge(si_done, NT * NIH)
            sp.dma_start(ROT, rot_ap).then_inc(rot_loaded, 16)
            for n in range(2 * B):
                g, b = n // B, n % B
                for src, row, ready in ((QT, 0, qt_ready), (QRD, DC, qr_ready), (QRL, DC + DR, qr_ready)):
                    sp.wait_ge(ready, 2 * (n + 1))
                    for h in range(4):
                        sp.dma_start(QALL[row:row + DC, 4 * g + h, b * L:(b + 1) * L], src[h * DC:(h + 1) * DC, :]).then_inc(q_placed, 16)
            sp.wait_ge(kv_stored, 16 * 3 * B)
            with sp.Fori(0, B) as b:
                with sp.Fori(0, NB // 4) as i:
                    for k in range(4):
                        sp.wait_ge(ob_done, C0 + b * NB + i * 4 + k - 3)
                        sp.dma_start(VW[k], kv_rows[bass.ds(b * LP + i * (4 * BT) + k * BT, P), 0:DC]).then_inc(vw_loaded[k], 16)

        def pool_rstd(pool, n):
            pool.wait_ge(var_ready, n + 1)
            pool.tensor_tensor(rstd[:, :], vareps[:, :], neghalf[:, :], ALU.pow).then_inc(rstd_ready, 1)


        def pool_fill(pool, c):
            pool.memset(VA[:, :, :, :, HD:STRIP], 0.0)
            pool.drain()
            pool.memset(VA[:, :, :, :, HD:HD + 1], 1.0)
            pool.memset(MB[:, :, :], 0.0)
            for buf in range(2):
                for s in range(2):
                    m = pool.memset(KB[buf][s][0:MAXROWS, :], 1.0)
            pool.drain()
            pool.memset(spare[:, 3:4], float(c)).then_inc(filled, 1)

        def pool_sel(pool):
            pool_rstd(pool, 3)
            pool.wait_ge(kv_stored, 16 * 3 * B)
            with pool.Fori(0, NT) as i:
                for k in range(P // BT):
                    buf = k % 4
                    pool.wait_ge(ob_done, C0 + i * (P // BT) + k - 3)
                    if k == 0:
                        pool.wait_ge(idx_ready, 4 * (i + 1))
                    pool.tensor_copy(IB[buf], IDX[:, bass.ds(i * (P // 4) + k * GB, GB)]).then_inc(staged, 1)
                    pool.drain()
                    for g in range(GB):
                        pool.indirect_dma_start(G[buf][:, g, :], None, kv_rows, bass.IndirectOffsetOnAxis(ap=IB[buf][:, g:g + 1], axis=0))\
                            .then_inc(gathered[buf], 16)

        def pe_turn(pe, tile, n, ready, base):
            for g in range(NG):
                pe.wait_ge(ready, base + g + 1)
                for t in range(4):
                    m = pe.transpose(bank[g][:, t * P:(t + 1) * P], tile(4 * g + t), ident)
                m.then_inc(turned, 1)

        def pe_pass1(pe, g, it, buf, u, visit):
            s, qt, hf = UNITS1[u]
            if u == 0:
                pe.wait_ge(rows_loaded[buf], 80 * (g // 2 + visit + 1))
                pe.wait_ge(cleared, 2 * (g + it + 1))
            pe.wait_ge(max_done, MAX0 + N1 * (g + it) + u + 1 - S_RING)
            lo, hi = hf * BANK, min((qt + 1) * P, (hf + 1) * BANK)
            o = bank[u % S_RING]
            m = pe.matmul(o[:, 0:hi - lo], QB[buf][s][0:ROWS, qt * P:(qt + 1) * P], KB[buf][s][0:ROWS, lo:hi], start=True, stop=True)
            if hi == (qt + 1) * P:
                m = pe.matmul(o[:, hi - lo - P:hi - lo], ident_b[:, :], mask_qk[:, :], start=False, stop=True, skip_group_check=True)
            m.then_inc(s1_done, 1)

        def pe_maxrows(pe, g, it):
            pe.wait_ge(mb_ready, g + it + 1)
            mt = bank[7][:, :].bitcast(BF16)
            for qt in range(TB):
                m = pe.transpose(mt[:, qt * P:(qt + 1) * P], MB[:, qt, :], ident_b[:, :])
            m.then_inc(mt_done, 1)

        def pe_scores(pe, g, it, buf, w):
            s, kc, hf = UNITS2[w]
            if w < 2:
                pe.wait_ge((maxrow0, maxrow1)[s], g + it + 1)
            pe.wait_ge(exp_done, EXP0 + N2 * (g + it) + w + 1 - S_RING)
            lo, hi = max(kc * P, hf * BANK), (hf + 1) * BANK
            o = bank[S_RING + w % S_RING]
            m = pe.matmul(o[:, 0:hi - lo], KB[buf][s][0:ROWS, kc * P:(kc + 1) * P], QB[buf][s][0:ROWS, lo:hi], start=True, stop=True)
            if lo == kc * P:
                m = pe.matmul(o[:, 0:P], ident_b[:, :], mask_kq[:, :], start=False, stop=True, skip_group_check=True)
            m.then_inc(st_done, 1)

        def pe_values(pe, g, it, buf, kc):
            units = [w for w in range(N2) if UNITS2[w][1] == kc]
            if kc == 0:
                pe.wait_ge(att_done, ATT0 + g + it)
            pe.wait_ge(exp_done, EXP0 + N2 * (g + it) + units[-1] + 1)
            for w in units:
                s, _, hf = UNITS2[w]
                lo = max(kc * P, hf * BANK)
                r = (2 * s + hf) * STRIP
                m = pe.matmul(bank[6][r:r + STRIP, lo - hf * BANK:BANK], VS[buf][:, s, kc, :],
                              PT[w % PT_RING][:, 0:(hf + 1) * BANK - lo], start=(kc == 0), stop=True, skip_group_check=True)
            m.then_inc(pv_done, 1)

        def pe_outputs(pe, g, it):
            pe.wait_ge(ot_ready, g + it + 1)
            for t in range(4):
                m = pe.transpose(bank[6][:, t * P:(t + 1) * P], OT[:, t * P:(t + 1) * P], ident)
            m.then_inc(o_turned, 1)

        LEAD = 1
        PER_TILE = 4

        def pe_step(pe, g, b, it, buf, ahead, visit):
            u = 0
            for kc in range(TB + 1):
                todo = [u + k for k in range(PER_TILE) if u + k < N1] if ahead and kc >= LEAD else []
                u += len(todo)
                for w in [w for w in range(N2) if UNITS2[w][1] == kc]:
                    pe_scores(pe, g, it, buf, w)
                    if todo:
                        pe_pass1(pe, g, it + 1, 1 - buf, todo.pop(0), visit + buf)
                for k in todo:
                    pe_pass1(pe, g, it + 1, 1 - buf, k, visit + buf)
                if kc == TB and ahead:
                    pe_maxrows(pe, g, it + 1)
                if kc >= 1:
                    pe_values(pe, g, it, buf, kc - 1)
            pe_outputs(pe, g, it)

        def pe_ffn(pe, c):
            n_turn = (0, 4)[c]
            pe_turn(pe, lambda t: XN[:, t, :], n_turn, xn_ready, NG * 2 * c)
            for n in range(8):
                if n % 2 == 0:
                    pe.wait_ge(xt_ready, NG * n_turn + n // 2 + 1)
                if n >= 4:
                    pe.wait_ge(r1_done, 8 * c + n - 3)
                pe.matmul(bank[4 + n % 4][:, :], w_qkv[:, (n % 2) * D:(n % 2 + 1) * D],
                          XT[:, (n // 2) * BANK:(n // 2 + 1) * BANK], start=True, stop=True).then_inc(qk_done, 1)
            for g in range(NG):
                for t in range(4):
                    m = pe.matmul(bank[g][:, t * P:(t + 1) * P], XT[:, (4 * g + t) * P:(4 * g + t + 1) * P],
                                  w_qkv[:, 2 * D:3 * D], start=True, stop=True)
                m.then_inc(v_done, 1)
            pe.wait_ge(va_ready, NG * (c + 1))
            pe.wait_ge(r1_done, 8 * (c + 1))
            g = PAIRS * c
            for u in range(N1):
                pe_pass1(pe, g, 0, 0, u, 0)
            pe_maxrows(pe, g, 0)
            for b, n in PAIR_LOOPS:
                with pe.Fori(0, n) as i:
                    pe_step(pe, g, b, i * 2 + b * TB, 0, True, i + b * TB // 2)
                    pe_step(pe, g, b, i * 2 + b * TB + 1, 1, True, i + b * TB // 2)
            pe_step(pe, g, B - 1, PAIRS - 2, 0, True, PAIRS // 2 - 1)
            pe_step(pe, g, B - 1, PAIRS - 1, 1, False, PAIRS // 2 - 1)
            pe.wait_ge(att_done, ATT0 + PAIRS * (c + 1))
            for gq in range(NG):
                for t in range(4):
                    m = pe.transpose(bank[gq][:, t * P:(t + 1) * P], ATT[:, 4 * gq + t, :], ident)
                m.then_inc(turned, 1)
            for gq in range(NG):
                pe.wait_ge(xt_ready, NG * (n_turn + 1) + gq + 1)
                for t in range(4):
                    m = pe.matmul(bank[4 + gq][:, t * P:(t + 1) * P], XT[:, (4 * gq + t) * P:(4 * gq + t + 1) * P],
                                  w_o[:, :], start=True, stop=True)
                m.then_inc(o_done, 1)
            pe_turn(pe, lambda t: HN[:, t, :], n_turn + 2, h_ready, NG * c)
            pe.wait_ge(xt_ready, NG * (n_turn + 3))
            for t in range(NT):
                m = pe.matmul(bank[4][:, t * E:(t + 1) * E], XT[:, t * P:(t + 1) * P], wg[:, :], start=True, stop=True)
            m.then_inc(gate_done, 1)
            pe.wait_ge(w8_ready, c + 1)
            for gq in range(NG):
                for t in range(4):
                    m = pe.transpose(bank[gq][0:E, t * P:(t + 1) * P], W8[:, 4 * gq + t, :], ident)
                m.then_inc(w8_turned, 1)
            for gq in range(NG):
                pe.wait_ge(wt_ready, NG * c + gq + 1)
                for t in range(4):
                    m = pe.matmul(bank[4 + gq][:, t * P:(t + 1) * P], WT[:, (4 * gq + t) * P:(4 * gq + t + 1) * P],
                                  bb2[:, :], start=True, stop=True)
                m.then_inc(b2_done, 1)
            pe.wait_ge(acc0_ready, NG * (c + 1))
            with pe.Fori(0, E // 2) as i:
                pe_expert(pe, c, i * 2, 0, i)
                pe_expert(pe, c, i * 2 + 1, 1, i)

        def pe_expert(pe, c, e, buf, visit):
            pe.wait_ge(ew_loaded[buf], 32 * (E // 2 * c + 1 + visit))
            for tb in range(NG + 1):
                if tb < NG:
                    for f in range(FC):
                        n = E * NG * FC * c + e * (NG * FC) + tb * FC + f
                        pe.wait_ge(gelu_done, GELU0 + n - 3)
                        pe.matmul(bank[f][:, :], W1[buf][:, f * P:(f + 1) * P], XT[:, tb * BANK:(tb + 1) * BANK],
                                  start=True, stop=True).then_inc(a_done, 1)
                if tb >= 1:
                    u = E * NG * c + e * NG + tb - 1
                    pe.wait_ge(gelu_done, GELU0 + (u + 1) * FC)
                    pe.wait_ge(acc_done, ACC0 + u - 1)
                    k = (tb - 1) % 2
                    for t in range(4):
                        for f in range(FC):
                            m = pe.matmul(bank[4 + k][:, t * P:(t + 1) * P], H1[k][:, f, t * P:(t + 1) * P],
                                          W2[buf][:, f, :], start=(f == 0), stop=(f == FC - 1))
                    m.then_inc(y_done, 1)

        def pe_sel(pe):
            pe_turn(pe, lambda t: XN[:, t, :], 3, xn_ready, NG)
            pe.wait_ge(sel_w_loaded, 16 * 13)
            pe.wait_ge(raw_loaded, 16 * 3)
            for j in range(NH // 2):
                pe.transpose(bank[4][:, j * DCQ:(j + 1) * DCQ], RAW[0:DCQ, j * P:(j + 1) * P], ident[0:DCQ, 0:DCQ])
            for k in range(2):
                for j in range(NH // 2):
                    o = (k + 1) * NH * DH + j * P
                    m = pe.transpose(bank[5][:, (4 * k + j) * DC:(4 * k + j + 1) * DC], RAW[0:DC, o:o + P], ident[0:DC, 0:DC])
            m.then_inc(uqk_turned, 1)
            pe.wait_ge(uqk_ready, 3)
            for h in range(NH):
                r, j = slice((h % 2) * DH, (h % 2 + 1) * DH), h // 2
                pe.matmul(bank[6 + h % 2][0:DCQ, j * DC:(j + 1) * DC], UQT[r, j, :], UKT[r, j, :], start=True, stop=True)
            for h in range(NH):
                r, j = slice((h % 2) * DH, (h % 2 + 1) * DH), h // 2
                m = pe.matmul(bank[4 + h % 2][0:DC, j * D:(j + 1) * D], UVT[r, j, :], WOUT[r, j, :], start=True, stop=True)
            m.then_inc(prep_done, 1)
            pe.wait_ge(prep_ready, 4)
            for n in range(8):
                pe.wait_ge(xt_ready, NG * 3 + n // 2 + 1)
                pe.matmul(bank[n][:, :], WIQ[:, (n % 2) * P:(n % 2 + 1) * P], XT[:, (n // 2) * BANK:(n // 2 + 1) * BANK],
                          start=True, stop=True).then_inc(qi_done, 1)
            for n in range(4):
                pe.wait_ge(qi_ready, n + 1)
                pe.matmul(bank[n][:, :], WIK[:, :], XT[:, n * BANK:(n + 1) * BANK], start=True, stop=True).then_inc(ki_done, 1)
            for q in range(4):
                pe.wait_ge(qi_ready, 5 + q)
                for t in range(4):
                    m = pe.matmul(bank[4 + q][:, t * P:t * P + ROWKV], XT[:, (4 * q + t) * P:(4 * q + t + 1) * P], WKV[:, :],
                                  start=True, stop=True)
                m.then_inc(kv_done, 1)
            pe.wait_ge(qi_ready, 8)
            pe.wait_ge(ki_ready, 4)
            pe.wait_ge(kv_ready, 4)
            for tile in range(NT):
                b, w = tile // TB, (tile % TB) * P + LW
                for h in range(NIH):
                    u = tile * NIH + h
                    if u >= 3:
                        pe.wait_ge(relu_done, u - 2)
                    r = slice((h % 2) * DH, (h % 2 + 1) * DH)
                    for half in range((w + BANK - 1) // BANK):
                        lo, hi = half * BANK, min(w, (half + 1) * BANK)
                        m = pe.matmul(bank[2 * (u % 3) + half][:, 0:hi - lo], QI[r, h // 2, tile * P:(tile + 1) * P],
                                      KI[r, b * L + lo:b * L + hi], start=True, stop=True)
                    m.then_inc(si_done, 1)
                if tile >= 1:
                    pe_index(pe, tile - 1)
            pe_index(pe, NT - 1)
            pe.wait_ge(relu_done, NT * NIH)
            pe.wait_ge(idx_ready, 4 * NT)
            for n in range(4):
                pe.matmul(bank[n][0:DCQ, :], WDQ[:, :], XT[:, n * BANK:(n + 1) * BANK], start=True, stop=True).then_inc(cq_done, 1)
            for n in range(4):
                pe.matmul(bank[4 + n][0:ROWKV, :], WKV[:, :], XT[:, n * BANK:(n + 1) * BANK], start=True, stop=True).then_inc(kt_done, 1)
            pe.wait_ge(cq_ready, 4)
            pe.wait_ge(kl_ready, 1)
            for n in range(2 * B):
                g, b = n // B, n % B
                for half in range(2):
                    blk = slice(b * L + half * BANK, b * L + (half + 1) * BANK)
                    if n >= 1:
                        pe.wait_ge(qt_ready, 2 * (n - 1) + half + 1)
                    pe.matmul(bank[half][:, :], AQ[:, g * P:(g + 1) * P], CQ[:, blk], start=True, stop=True).then_inc(qt_done, 1)
                    for sw in range(2):
                        if n >= 1:
                            pe.wait_ge(mu_ready, 4 * (n - 1) + 2 * half + sw + 1)
                        pe.matmul(bank[2 + 2 * half + sw][:, :], WQR[:, sw, g * P:(g + 1) * P], CQ[:, blk], start=True, stop=True)\
                          .then_inc(mu_done, 1)
            pe.wait_ge(mu_ready, 4 * 2 * B)
            pe.wait_ge(qt_ready, 2 * 2 * B)
            run_blocks(pe, pe_ahead, pe_block)
            pe.wait_ge(oa_ready, C0 + B * NB)
            for gq in range(NG):
                for t in range(4):
                    tile = 4 * gq + t
                    for h in range(NH):
                        m = pe.matmul(bank[gq][:, t * P:(t + 1) * P], OA[:, h, tile * P:(tile + 1) * P], MO[:, h, :],
                                      start=(h == 0), stop=(h == NH - 1))
                m.then_inc(mix_done, 1)

        def pe_index(pe, tile):
            pe.wait_ge(best_ready, tile + 1)
            if tile >= 1:
                pe.wait_ge(idx_ready, 4 * tile)
            pe.transpose(bank[6][0:NSEL, 0:P], bidf[:, tile % 2, :], ident).then_inc(i_turned, 1)

        def run_blocks(eng, ahead, block_):
            with eng.Fori(0, B) as b:
                ahead(eng, b, b * NB, 0)
                for k in range(4):
                    block_(eng, b, b * NB + k, k, True, ahead)
                with eng.Fori(1, NB // 4 - 1) as i:
                    for k in range(4):
                        block_(eng, b, b * NB + i * 4 + k, k, False, ahead)
                for k in range(4):
                    block_(eng, b, b * NB + (NB - 4) + k, k, False, ahead if k < 3 else None)

        def pe_ahead(pe, b, n, k):
            pe_local(pe, b, n, k)
            pe_gt(pe, n, k)
            pe_sel_scores(pe, n, k)

        def pe_local(pe, b, n, k):
            pe.wait_ge(qs_ready, n + 1)
            pe.wait_ge(sm_ready, C0 + n - 1)
            keys = KL.rearrange("p b t -> p (b t)")
            pe.matmul(bank[k % 2][:, 0:P], QS[k % 2], keys[:, bass.ds(n * BT + b * (LP - L), P)], start=True, stop=True)

        def pe_gt(pe, n, k):
            pe.wait_ge(rot_done, n + 1)
            pe.wait_ge(gts_ready, C0 + n - 1)
            for g in range(GB):
                m = pe.transpose(bank[2 + k % 2][0:ROWKV, g * P:(g + 1) * P], G[k][:, g, :], ident)
            m.then_inc(gt_done, 1)

        def pe_sel_scores(pe, n, k):
            pe.wait_ge(gts_ready, C0 + n + 1)
            for g in range(GB):
                m = pe.matmul(bank[k % 2][g * STRIP:(g + 1) * STRIP, P:2 * P], QS[k % 2][:, g * STRIP:(g + 1) * STRIP],
                              GTS[k % 2][:, g, :], start=True, stop=True)
            m.then_inc(s_done, 1)

        def pe_block(pe, b, n, k, early, ahead):
            k1 = (k + 1) % 4
            if ahead:
                pe_local(pe, b, n + 1, k1)
                pe_gt(pe, n + 1, k1)
            pe.wait_ge(pn_ready, n + 1)
            pe.wait_ge(pts_ready, C0 + n - 1)
            for x in range(2):
                m = pe.transpose(bank[4 + k % 2][:, x * P:(x + 1) * P], PB[k % 2][:, x * P:(x + 1) * P], ident)
            m.then_inc(tp_done, 1)
            if ahead:
                pe_sel_scores(pe, n + 1, k1)
            pe.wait_ge(vw_loaded[k], visit16(n, k))
            pe.wait_ge(oa_ready, C0 + n - 1)
            pe.wait_ge(pts_ready, C0 + n + 1)
            o = bank[6 + k % 2]
            pe.matmul(o[0:DC, 0:P], VW[k], PTS[k % 2][:, 0:P], start=True, stop=True)
            for g in range(GB):
                m = pe.matmul(o[0:DC, g * STRIP:(g + 1) * STRIP], G[k][:, g, 0:DC], PTS[k % 2][:, P + g * STRIP:P + (g + 1) * STRIP],
                              start=False, stop=True, skip_group_check=True)
            m.then_inc(ob_done, 1)

        def visit16(n, k):
            return n * 4 + (16 - 4 * k)


        def act_turn(act, n):
            for g in range(NG):
                act.wait_ge(turned, NG * n + g + 1)
                act.activation(XT[:, g * BANK:(g + 1) * BANK], bank[g][:, :], ACT.Copy).then_inc(xt_ready, 1)

        def act_exps(act, g, it, w):
            act.wait_ge(st_done, N2 * (g + it) + w + 1)
            k = UNITS2[w - PT_RING][1]
            act.wait_ge(pv_done, PV0 + TB * (g + it) + k + 1 - (TB if w < PT_RING else 0))
            s, kc, hf = UNITS2[w]
            n = (hf + 1) * BANK - max(kc * P, hf * BANK)
            act.activation(PT[w % PT_RING][:, 0:n], bank[S_RING + w % S_RING][:, 0:n], ACT.Exp, scale=float(HD) ** -0.5)\
               .then_inc(exp_done, 1)

        def act_maxrow(act, g, it, buf):
            act.wait_ge(mt_done, g + it + 1)
            act.activation(QB[buf][1][0:MAXROWS, :], bank[7][:, :].bitcast(BF16)[STRIP:STRIP + MAXROWS, :], ACT.Copy)\
               .then_inc(maxrow1, 1)

        def act_step(act, g, b, it, buf, ahead):
            for w in range(N2):
                act_exps(act, g, it, w)
            if ahead:
                act_maxrow(act, g, it + 1, 1 - buf)
            act.wait_ge(pv_done, PV0 + TB * (g + it + 1))
            act.wait_ge(o_turned, OTURN0 + g + it)
            act.activation(OT[:, :], bank[6][:, :], ACT.Copy).then_inc(ot_ready, 1)

        def act_ffn(act, c):
            n_turn = (0, 4)[c]
            act_turn(act, n_turn)
            for n in range(9):
                if n < 8:
                    act.wait_ge(qk_done, 8 * c + n + 1)
                    blk = slice((n // 2) * BANK, (n // 2 + 1) * BANK)
                    act.activation((qparts, kparts)[n % 2][:, 0, blk], bank[4 + n % 4][:, :], ACT.Copy).then_inc(p1_done, 1)
                if n >= 1:
                    m = n - 1
                    act.wait_ge(r1_done, 8 * c + m + 1)
                    blk = slice((m // 2) * BANK, (m // 2 + 1) * BANK)
                    act.activation((qparts, kparts)[m % 2][:, 1, blk], rest[:, m % 2, :], ACT.Copy).then_inc(p2_done, 1)
            for g in range(NG):
                act.wait_ge(v_done, NG * c + g + 1)
                b, t0 = 4 * g // TB, 4 * g % TB
                for t in range(4):
                    dst = VA[:, b * (PAIRS // B):(b + 1) * (PAIRS // B), :, t0 + t, 0:HD].rearrange("p a s d -> p (a s) d")
                    m = act.activation(dst, bank[g][:, t * P:(t + 1) * P].rearrange("p (h d) -> p h d", d=HD), ACT.Copy)
                m.then_inc(va_ready, 1)
            g = PAIRS * c
            act_maxrow(act, g, 0, 0)
            for b, n in PAIR_LOOPS:
                with act.Fori(0, n) as i:
                    act_step(act, g, b, i * 2 + b * TB, 0, True)
                    act_step(act, g, b, i * 2 + b * TB + 1, 1, True)
            act_step(act, g, B - 1, PAIRS - 2, 0, True)
            act_step(act, g, B - 1, PAIRS - 1, 1, False)
            act_turn(act, n_turn + 1)
            act_turn(act, n_turn + 2)
            act.wait_ge(lg_ready, c + 1)
            act.activation(lg[:, :, :], lg[:, :, :], ACT.Exp).then_inc(eg_ready, 1)
            for gq in range(NG):
                act.wait_ge(w8_turned, NG * c + gq + 1)
                act.activation(WT[:, gq * BANK:(gq + 1) * BANK], bank[gq][0:E, :], ACT.Copy).then_inc(wt_ready, 1)
            for gq in range(NG):
                act.wait_ge(b2_done, NG * c + gq + 1)
                act.activation(ACC[:, 4 * gq:4 * gq + 4, :], bank[4 + gq][:, :].rearrange("p (t d) -> p t d", d=D), ACT.Copy)\
                   .then_inc(acc0_ready, 1)
            with act.Fori(0, E // 2) as i:
                act_expert(act, c, i * 2, 0)
                act_expert(act, c, i * 2 + 1, 1)

        def act_expert(act, c, e, buf):
            act.activation(bias1[buf][:, :], bb1[:, :, :].rearrange("p e f -> p (e f)")[:, bass.ds(e * FC, FC)], ACT.Copy)
            act.drain()
            for tb in range(NG):
                u = E * NG * c + e * NG + tb
                act.wait_ge(y_done, Y0 + u - 1)
                for f in range(FC):
                    act.wait_ge(a_done, u * FC + f + 1)
                    act.activation(H1[tb % 2][:, f, :], bank[f][:, :], ACT.Gelu_apprx_tanh,
                                   bias=bias1[buf][:, f:f + 1]).then_inc(gelu_done, 1)

        def act_log(act, dst, src, done):
            act.activation(dst, src, ACT.Abs)
            act.drain()
            act.activation(dst, dst, ACT.Exp, scale=-1.0)
            act.drain()
            act.activation(dst, dst, ACT.Ln, bias=1.0).then_inc(done, 1)

        def act_sel(act):
            act_turn(act, 3)
            act.wait_ge(uqk_turned, 1)
            act.activation(UQT[:, :, :].rearrange("p a b -> p (a b)"), bank[4][:, 0:NH // 2 * DCQ], ACT.Copy).then_inc(uqk_ready, 1)
            act.activation(UKT[:, :, :].rearrange("p a b -> p (a b)"), bank[5][:, 0:NH // 2 * DC], ACT.Copy).then_inc(uqk_ready, 1)
            act.activation(UVT[:, :, :].rearrange("p a b -> p (a b)"), bank[5][:, NH // 2 * DC:NH * DC], ACT.Copy).then_inc(uqk_ready, 1)
            act.wait_ge(prep_done, 1)
            for k in range(2):
                act.activation(AQ[:, :].rearrange("p (j s c) -> p s j c", s=2, c=DC)[:, k],
                               bank[6 + k][0:DCQ, 0:NH // 2 * DC].rearrange("p (j c) -> p j c", c=DC), ACT.Copy).then_inc(prep_ready, 1)
            for k in range(2):
                act.activation(MO[:, :, :].rearrange("p (j s) d -> p s j d", s=2)[:, k],
                               bank[4 + k][0:DC, :].rearrange("p (j d) -> p j d", d=D), ACT.Copy).then_inc(prep_ready, 1)
            for n in range(8):
                act.wait_ge(qi_done, n + 1)
                act.activation(QI[:, n % 2, (n // 2) * BANK:(n // 2 + 1) * BANK], bank[n][:, :], ACT.Copy).then_inc(qi_ready, 1)
            for q in range(4):
                act.wait_ge(kv_done, q + 1)
                src = bank[4 + q][:, :].rearrange("p (t n) -> p t n", n=P)[:, :, 0:2 * DR]
                act_log(act, KVS[:, 4 * q:4 * q + 4, DC:ROWKV], src, kv_log)
            act.wait_ge(delta_loaded, 16 * 9)
            act.activation(delta_row[:, 1, 0:HALF], delta_row[:, 0, 0:HALF], ACT.Exp, scale=-1.0).then_inc(sig_ready, 1)
            act.activation(delta_col[:, 1:2], delta_col[:, 0:1], ACT.Exp, scale=-1.0).then_inc(sig_ready, 1)
            act.wait_ge(ang_ready, 2)
            act.activation(delta_row[:, 3:5, 0:HALF], delta_row[:, 1:3, 0:HALF], ACT.Sin).then_inc(trig_ready, 1)
            act.activation(delta_col[:, 3:5], delta_col[:, 1:3], ACT.Sin).then_inc(trig_ready, 1)
            for tile in range(NT):
                w = (tile % TB) * P + LW
                for h in range(NIH):
                    u = tile * NIH + h
                    act.wait_ge(si_done, u + 1)
                    if u >= 2:
                        act.wait_ge(sc_used, u - 1)
                    for half in range((w + BANK - 1) // BANK):
                        lo, hi = half * BANK, min(w, (half + 1) * BANK)
                        m = act.activation(RL[u % 2][:, lo:hi], bank[2 * (u % 3) + half][:, 0:hi - lo], ACT.Relu)
                    m.then_inc(relu_done, 1)
                if tile >= 1:
                    act_index(act, tile - 1)
            act_index(act, NT - 1)
            for n in range(4):
                act.wait_ge(cq_done, n + 1)
                act.activation(CQ[:, n * BANK:(n + 1) * BANK], bank[n][0:DCQ, :], ACT.Copy).then_inc(cq_ready, 1)
            for n in range(4):
                act.wait_ge(kt_done, n + 1)
                act_log(act, MU[0:2 * DR, 0:BANK] if n % 2 == 0 else MU[0:2 * DR, BANK:L], bank[4 + n][0:2 * DR, :], kt_log)
                b, t = n // 2, (n % 2) * BANK
                act.activation(KL[0:DC, b, LW + t:LW + t + BANK], bank[4 + n][2 * DR:ROWKV, :], ACT.Copy).then_inc(kt_c, 1)
                if n % 2 == 1:
                    act.wait_ge(kt_mu, n + 1)
            act.wait_ge(kl_ready, 1)
            for n in range(2 * B):
                for half in range(2):
                    act.wait_ge(qt_done, 2 * n + half + 1)
                    if n >= 1 and half == 0:
                        act.wait_ge(q_placed, 16 * 12 * n)
                    act.activation(QT[:, half * BANK:(half + 1) * BANK], bank[half][:, :], ACT.Copy).then_inc(qt_ready, 1)
                    for sw in range(2):
                        act.wait_ge(mu_done, 4 * n + 2 * half + sw + 1)
                        if n >= 1:
                            act.wait_ge(qr_ready, 2 * n)
                        act_log(act, (MU, MUS)[sw][:, half * BANK:(half + 1) * BANK], bank[2 + 2 * half + sw][:, :], mu_log)
            act.wait_ge(q_placed, 16 * 12 * 2 * B)
            run_blocks(act, act_ahead, act_block)

        def act_index(act, tile):
            act.wait_ge(i_turned, tile + 1)
            src = bank[6][0:NSEL, 0:P].rearrange("p (g t) -> p t g", t=4)
            for t in range(4):
                act.activation(IDX[t * NSEL:(t + 1) * NSEL, tile * (P // 4):(tile + 1) * (P // 4)], src[:, t, :], ACT.Copy).then_inc(idx_ready, 1)

        def act_ahead(act, b, n, k):
            act_gt(act, n, k)

        def act_gt(act, n, k):
            act.wait_ge(s_done, C0 + n - 1)
            act.wait_ge(gt_done, n + 1)
            act.activation(GTS[k % 2][0:DC + DR].rearrange("p g n -> p (g n)"), bank[2 + k % 2][0:DC + DR, :], ACT.Copy).then_inc(gts_ready, 1)

        def act_block(act, b, n, k, early, ahead):
            act.wait_ge(tp_done, C0 + n - 1)
            act.wait_ge(sm_ready, C0 + n + 1)
            c = col[:, k % 2, :]
            act.activation(PB[k % 2], SM[k % 2], ACT.Exp, scale=SCALE2, bias=c[:, 1:2], accum_out=c[:, 2:3]).then_inc(pb_exp, 1)
            if ahead:
                act_gt(act, n + 1, (k + 1) % 4)

        def dve_norm(dve, src, dst, n, done, per):
            for t in range(NT):
                dve.bn_stats(stats[:, t, :], src[:, t, :])
            dve.drain()
            for t in range(NT):
                dve.bn_aggr(mv[:, t, :], stats[:, t, :])
            dve.drain()
            dve.tensor_scalar(vareps[:, :], mv[:, :, 1], FFN_EPS, None, ALU.add).then_inc(var_ready, 1)
            dve.wait_ge(rstd_ready, n + 1)
            for t in range(NT):
                m = dve.tensor_scalar(dst[:, t, :], src[:, t, :], mv[:, t, 0:1], rstd[:, t:t + 1], ALU.subtract, ALU.mult)
                if done is not None and t % 4 == 3:
                    m.then_inc(done, 1)

        def dve_max(dve, g, it, u):
            s, qt, hf = UNITS1[u]
            dve.wait_ge(s1_done, N1 * (g + it) + u + 1)
            n = min((qt + 1) * P - hf * BANK, BANK)
            dve.tensor_reduce(rowmax[:, hf, s, qt:qt + 1], bank[u % S_RING][:, 0:n], AX_X, ALU.max).then_inc(max_done, 1)

        def dve_maxrows(dve, g, it, buf):
            parts = [MB[:, :, 0:2 * STRIP].rearrange("p t (s r) -> p s t r", s=2)[:, :, :, r] for r in range(MAXROWS)]
            top = rowmax[:, 0, :, :]
            dve.drain()
            dve.tensor_tensor(rowmax[:, 0, :, 4:], rowmax[:, 0, :, 4:], rowmax[:, 1, :, 4:], ALU.max)
            dve.drain()
            dve.tensor_scalar(parts[0], top, -1.0, None, ALU.mult)
            dve.drain()
            dve.scalar_tensor_tensor(maxrest[:, :, :], top, -1.0, parts[0], ALU.mult, ALU.subtract)
            dve.drain()
            dve.tensor_copy(parts[1], maxrest[:, :, :])
            dve.drain()
            dve.tensor_tensor(parts[2], maxrest[:, :, :], parts[1], ALU.subtract).then_inc(mb_ready, 1)
            dve.wait_ge(mt_done, g + it + 1)
            dve.tensor_copy(QB[buf][0][0:MAXROWS, :], bank[7][:, :].bitcast(BF16)[0:MAXROWS, :]).then_inc(maxrow0, 1)

        def dve_clear(dve, g, it, buf):
            dve.wait_ge(pv_done, PV0 + TB * (g + it - 1))
            for s in range(2):
                dve.memset(QB[buf][s][0:MAXROWS, :], 0.0).then_inc(cleared, 1)

        def dve_outputs(dve, g, b, it):
            dve.wait_ge(o_turned, OTURN0 + g + it + 1)
            o = bank[6][:, :].rearrange("p (t s h d) -> p s h t d", t=4, s=2, h=2)
            for s in range(2):
                dve.reciprocal(rsum[:, s, :, :], o[:, s, :, :, HD])
            dve.drain()
            att = ATT[:, :, :].rearrange("p t d -> p (t d)")[:, b * L:(b + 1) * L].rearrange("p (h t d) -> p h t d", h=2, d=D)
            for s in range(2):
                m = dve.tensor_tensor(att[:, :, :, bass.ds((it - b * TB) * (2 * HD) + s * HD, HD)], o[:, s, :, :, 0:HD],
                                      rsum[:, s, :, :].unsqueeze(3).broadcast_to([P, 2, 4, HD]), ALU.mult)
            m.then_inc(att_done, 1)

        def dve_step(dve, g, b, it, buf, ahead):
            if ahead:
                dve_clear(dve, g, it + 1, 1 - buf)
                for u in range(N1):
                    dve_max(dve, g, it + 1, u)
                dve_maxrows(dve, g, it + 1, 1 - buf)
            dve_outputs(dve, g, b, it)

        def dve_expert(dve, c, e):
            for tb in range(NG):
                u = E * NG * c + e * NG + tb
                dve.drain()
                dve.wait_ge(y_done, Y0 + u + 1)
                for t in range(4):
                    tile = 4 * tb + t
                    m = dve.scalar_tensor_tensor(ACC[:, tile, :], bank[4 + tb % 2][:, t * P:(t + 1) * P],
                                                 W8[:, tile, bass.ds(e, 1)], ACC[:, tile, :], ALU.mult, ALU.add)
                m.then_inc(acc_done, 1)

        def affine(dve, t, n, done):
            for k, op in ((0, ALU.mult), (1, ALU.add)):
                dve.drain()
                for g in range(NG):
                    m = dve.tensor_tensor(t[:, 4 * g:4 * g + 4, :], t[:, 4 * g:4 * g + 4, :],
                                          gains[:, 2 * n + k, :].unsqueeze(1).broadcast_to([P, 4, D]), op)
                    if k and done is not None:
                        m.then_inc(done, 1)

        def dve_ffn(dve, c):
            ln = (0, 4)[c]
            dve_norm(dve, X, XN, ln, xn_ready, 4)
            for n in range(9):
                if n < 8:
                    blk = slice((n // 2) * BANK, (n // 2 + 1) * BANK)
                    if n >= 2:
                        dve.wait_ge(p2_done, 8 * c + n - 1)
                    dve.wait_ge(p1_done, 8 * c + n + 1)
                    dve.drain()
                    dve.tensor_tensor(rest[:, n % 2, :], bank[4 + n % 4][:, :], (qparts, kparts)[n % 2][:, 0, blk], ALU.subtract)\
                       .then_inc(r1_done, 1)
                if n >= 1:
                    m = n - 1
                    blk = slice((m // 2) * BANK, (m // 2 + 1) * BANK)
                    dve.wait_ge(p2_done, 8 * c + m + 1)
                    p = (qparts, kparts)[m % 2]
                    dve.tensor_tensor(p[:, 2, blk], rest[:, m % 2, :], p[:, 1, blk], ALU.subtract).then_inc(p3_done, 1)
            g = PAIRS * c
            dve.wait_ge(filled, c + 1)
            dve_clear(dve, g, 0, 0)
            for u in range(N1):
                dve_max(dve, g, 0, u)
            dve_maxrows(dve, g, 0, 0)
            for b, n in PAIR_LOOPS:
                with dve.Fori(0, n) as i:
                    dve_step(dve, g, b, i * 2 + b * TB, 0, True)
                    dve_step(dve, g, b, i * 2 + b * TB + 1, 1, True)
            dve_step(dve, g, B - 1, PAIRS - 2, 0, True)
            dve_step(dve, g, B - 1, PAIRS - 1, 1, False)
            for gq in range(NG):
                dve.wait_ge(o_done, NG * c + gq + 1)
                dve.tensor_tensor(XN[:, 4 * gq:4 * gq + 4, :], XN[:, 4 * gq:4 * gq + 4, :],
                                  bank[4 + gq][:, :].rearrange("p (t d) -> p t d", d=D), ALU.add)
            dve.drain()
            dve_norm(dve, XN, HN, ln + 1, None, 4)
            affine(dve, HN, 0, h_ready)
            dve.wait_ge(gate_done, c + 1)
            gate = bank[4][:, 0:NT * E].rearrange("p (t e) -> p t e", e=E)

            def per_tile(k):
                return g16[:, k, :].unsqueeze(2).broadcast_to([P, NT, E])

            dve.tensor_reduce(g16[:, 0, :], gate, AX_X, ALU.max)
            dve.drain()
            dve.tensor_tensor(lg[:, :, :], gate, per_tile(0), ALU.subtract).then_inc(lg_ready, 1)
            dve.wait_ge(eg_ready, c + 1)
            dve.tensor_reduce(g16[:, 1, :], lg[:, :, :], AX_X, ALU.add)
            dve.drain()
            dve.reciprocal(g16[:, 1, :], g16[:, 1, :])
            dve.drain()
            dve.tensor_tensor(pr[:, :, :], lg[:, :, :], per_tile(1), ALU.mult)
            dve.drain()
            for t in range(NT):
                dve.max(top8[:, t, :], pr[:, t, :])
            dve.drain()
            for t in range(NT):
                dve.max_index(idx8[:, t, :], top8[:, t, :], pr[:, t, :])
            dve.tensor_tensor(g16[:, 2, :], top8[:, :, 0], top8[:, :, 1], ALU.add)
            dve.drain()
            dve.tensor_copy(idxf[:, :, :], idx8[:, :, 0:2])
            dve.reciprocal(g16[:, 2, :], g16[:, 2, :])
            dve.drain()
            for k in range(2):
                dve.tensor_tensor(oh[:, k, :, :], cst("iota8").unsqueeze(1).broadcast_to([P, NT, E]),
                                  idxf[:, :, k:k + 1].broadcast_to([P, NT, E]), ALU.is_equal)
            dve.drain()
            for k in range(2):
                dve.tensor_tensor(oh[:, k, :, :], oh[:, k, :, :], top8[:, :, k:k + 1].broadcast_to([P, NT, E]), ALU.mult)
            dve.drain()
            dve.tensor_tensor(oh[:, 0, :, :], oh[:, 0, :, :], oh[:, 1, :, :], ALU.add)
            dve.drain()
            dve.tensor_tensor(W8[:, :, :], oh[:, 0, :, :], per_tile(2), ALU.mult).then_inc(w8_ready, 1)
            dve.wait_ge(acc0_ready, NG * (c + 1))
            with dve.Fori(0, E // 2) as i:
                dve_expert(dve, c, i * 2)
                dve_expert(dve, c, i * 2 + 1)
            dve.drain()
            for gq in range(NG):
                s = slice(4 * gq, 4 * gq + 4)
                dve.tensor_tensor(HN[:, s, :], HN[:, s, :], ACC[:, s, :], ALU.add)
            dve.drain()
            dve_norm(dve, HN, XN, ln + 2, None, 4)
            affine(dve, XN, 1, None)
            dve.drain()
            dve.scalar_tensor_tensor(X[:, :, :], XN[:, :, :], 0.5, X[:, :, :], ALU.mult, ALU.add).then_inc(x_ready, 1)
            dve.drain()

        def dve_sel(dve):
            dve_norm(dve, X, XN, 3, xn_ready, 4)
            dve.wait_ge(sel_w_loaded, 16 * 13)
            for n in range(4):
                dve.wait_ge(ki_done, n + 1)
                dve.tensor_copy(KI[:, n * BANK:(n + 1) * BANK], bank[n][:, :]).then_inc(ki_ready, 1)
            for q in range(4):
                dve.wait_ge(kv_log, q + 1)
                src = bank[4 + q][:, :].rearrange("p (t n) -> p t n", n=P)
                rows = KVS[:, 4 * q:4 * q + 4, :]
                dve.tensor_copy(rows[:, :, 0:DC], src[:, :, 2 * DR:ROWKV])
                dve.scalar_tensor_tensor(rows[:, :, DC:ROWKV], src[:, :, 0:2 * DR], 0.0, rows[:, :, DC:ROWKV], ALU.max, ALU.add)\
                   .then_inc(kv_ready, 1)
            dve.wait_ge(sig_ready, 2)
            dr, dc = delta_row, delta_col
            for d, at_ in ((dr, lambda k: dr[:, k, 0:HALF]), (dc, lambda k: dc[:, k:k + 1])):
                dve.tensor_scalar(at_(2), at_(1), 1.0, None, ALU.add)
                dve.drain()
                dve.reciprocal(at_(5), at_(2))
                dve.drain()
                dve.tensor_scalar(at_(1), at_(5), -2.0 * np.pi, np.pi, ALU.mult, ALU.add)
                dve.drain()
                dve.tensor_scalar(at_(1), at_(1), 3.1415925, -3.1415925, ALU.min, ALU.max)
                dve.tensor_scalar(at_(2), at_(5), -np.pi, None, ALU.mult).then_inc(ang_ready, 1)
            dve.wait_ge(trig_ready, 2)
            for d, at_ in ((dr, lambda k: dr[:, k, 0:HALF]), (dc, lambda k: dc[:, k:k + 1])):
                dve.tensor_tensor(at_(0), at_(4), at_(4), ALU.mult)
                dve.tensor_scalar(at_(1), at_(3), -1.0, None, ALU.mult)
                dve.drain()
                dve.tensor_scalar(at_(0), at_(0), -2.0, 1.0, ALU.mult, ALU.add)
                dve.drain()
            dve.tensor_tensor(dc[:, 1:2], dc[:, 1:2], cst("sign"), ALU.mult)
            for k in range(2):
                dve.tensor_copy(dr[:, k, HALF:DR], dr[:, k, 0:HALF])
            dve.drain()
            dve.tensor_scalar(dc[:, 2:3], dc[:, 1:2], -1.0, None, ALU.mult)
            dve.tensor_tensor(dr[:, 1, :], dr[:, 1, :], cst("sign_row"), ALU.mult)
            dve.drain()
            dve.tensor_tensor(rot_sel[:, 0:DR], cst("cos_sel"), dr[:, 0, :], ALU.mult)
            dve.tensor_tensor(dr[:, 2, :], cst("sin_sel"), dr[:, 1, :], ALU.mult)
            dve.tensor_tensor(rot_sel[:, DR:], cst("sin_sel"), dr[:, 0, :], ALU.mult)
            dve.tensor_tensor(dr[:, 3, :], cst("cos_sel"), dr[:, 1, :], ALU.mult)
            dve.drain()
            dve.tensor_tensor(rot_sel[:, 0:DR], rot_sel[:, 0:DR], dr[:, 2, :], ALU.subtract)
            dve.tensor_tensor(rot_sel[:, DR:], rot_sel[:, DR:], dr[:, 3, :], ALU.add)
            for tile in range(NT):
                dve_select(dve, tile)
            dve.wait_ge(rot_loaded, 16)
            for k in range(2):
                co, si = ROT[:, 2 * k, :], ROT[:, 2 * k + 1, :]
                dve.tensor_scalar(MUS, si, dc[:, 2:3], None, ALU.mult)
                dve.tensor_scalar(T1, co, dc[:, 1:2], None, ALU.mult)
                dve.drain()
                dve.scalar_tensor_tensor(co, co, dc[:, 0:1], MUS, ALU.mult, ALU.add)
                dve.scalar_tensor_tensor(si, si, dc[:, 0:1], T1, ALU.mult, ALU.add)
                dve.drain()
            for g in range(2):
                dve.memset(GTS[g][DC + DR:ROWKV], 0.0)
            dve.memset(KL[DC:DC + DR, :, :], 0.0)
            for n in range(4):
                b, t = n // 2, slice((n % 2) * BANK, (n % 2 + 1) * BANK)
                dve.wait_ge(kt_log, n + 1)
                m = MU[0:2 * DR, t]
                dve.scalar_tensor_tensor(m, bank[4 + n][0:2 * DR, :], 0.0, m, ALU.max, ALU.add)
                dve.drain()
                dve.tensor_tensor(QRD[0:DR, t], m[0:DR], ROT[0:DR, 0, t], ALU.mult)
                dve.tensor_tensor(QRL[0:DR, t], m[DR:2 * DR], ROT[DR:2 * DR, 1, t], ALU.mult).then_inc(kt_mu, 1)
                dve.drain()
                dve.tensor_tensor(KL[DC + DR:, b, LW + (n % 2) * BANK:LW + (n % 2 + 1) * BANK], QRD[0:DR, t], QRL[0:DR, t], ALU.add)
            dve.wait_ge(kt_c, 4)
            dve.drain()
            dve.tensor_copy(KL[:, :, 0:LW], KL[:, :, LW:2 * LW])
            m = dve.tensor_copy(KL[:, :, LW + L:LP], KL[:, :, LW:LW + LP - L - LW])
            m.then_inc(kl_ready, 1)
            for n in range(2 * B):
                for half in range(2):
                    t = slice(half * BANK, (half + 1) * BANK)
                    for sw in range(2):
                        dve.wait_ge(mu_log, 4 * n + 2 * half + sw + 1)
                        m = (MU, MUS)[sw][:, t]
                        dve.scalar_tensor_tensor(m, bank[2 + 2 * half + sw][:, :], 0.0, m, ALU.max, ALU.add).then_inc(mu_ready, 1)
                dve.drain()
                if n >= 1:
                    dve.wait_ge(q_placed, 16 * 12 * n)
                for k, dst in ((0, QRD), (1, QRL)):
                    dve.tensor_tensor(dst, MU, ROT[:, 2 * k, :], ALU.mult)
                    dve.tensor_tensor(T1, MUS, ROT[:, 2 * k + 1, :], ALU.mult)
                    dve.drain()
                    dve.tensor_tensor(dst, dst, T1, ALU.add).then_inc(qr_ready, 1)
                    dve.drain()
            run_blocks(dve, dve_ahead, dve_block)
            for gq in range(NG):
                dve.wait_ge(mix_done, gq + 1)
                m = dve.tensor_tensor(X[:, 4 * gq:4 * gq + 4, :], X[:, 4 * gq:4 * gq + 4, :],
                                      bank[gq][:, :].rearrange("p (t d) -> p t d", d=D), ALU.add)
            m.then_inc(x_ready, 1)
            dve.drain()

        def dve_select(dve, tile):
            b, tt = tile // TB, tile % TB
            w = tt * P + LW
            for h in range(NIH):
                u = tile * NIH + h
                dve.wait_ge(relu_done, u + 1)
                dve.drain()
                if h == 0:
                    dve.tensor_scalar(SC[:, 0:w], RL[u % 2][:, 0:w], idx_w[:, h:h + 1], None, ALU.mult).then_inc(sc_used, 1)
                else:
                    dve.scalar_tensor_tensor(SC[:, 0:w], RL[u % 2][:, 0:w], idx_w[:, h:h + 1], SC[:, 0:w], ALU.mult, ALU.add)\
                       .then_inc(sc_used, 1)
            dve.drain()
            edge = min(w, P)
            dve.tensor_tensor(SC[:, w - edge:w], SC[:, w - edge:w], cst("nonlocal")[:, P - edge:P], ALU.min)
            for r in range(NSEL // 8):
                dve.drain()
                dve.max(best[:, r, :], SC[:, 0:w])
                dve.drain()
                dve.max_index(bidx[:, r, :], best[:, r, :], SC[:, 0:w])
                if r < NSEL // 8 - 1:
                    dve.match_replace(SC[:, 0:w], best[:, r, :], SC[:, 0:w], -3.3e38)
            dve.drain()
            f = bidf[:, tile % 2, :]
            if tile >= 2:
                dve.wait_ge(i_turned, tile - 1)
            dve.tensor_copy(f, bidx.rearrange("p r k -> p (r k)"))
            dve.drain()
            if tt == 0:
                dve.tensor_tensor(f, f, cst("keep"), ALU.mult)
                dve.drain()
                dve.tensor_tensor(f, f, cst("fill"), ALU.add)
                dve.drain()
            dve.tensor_scalar(f, f, float(b * LP + LW), None, ALU.add).then_inc(best_ready, 1)

        def dve_queries(dve, n, k):
            src = QALL[:, :, bass.ds(n * BT, BT)].rearrange("p h (g t) -> p g h t", t=4)
            dve.wait_ge(s_done, C0 + n - 1)
            dve.tensor_scalar(QS[k % 2].rearrange("p (g h t) -> p g h t", g=GB, h=NH), src, 1.0, None, ALU.mult).then_inc(qs_ready, 1)

        def dve_attended(dve, n, k):
            dst = OA[:, :, bass.ds(n * BT, BT)].rearrange("p h (g t) -> p g h t", t=4)
            dve.wait_ge(ob_done, C0 + n + 1)
            dve.tensor_scalar(dst, bank[6 + k % 2][0:DC, 0:P].rearrange("p (g h t) -> p g h t", g=GB, h=NH), 1.0, None, ALU.mult)\
               .then_inc(oa_ready, 1)

        def dve_ahead(dve, b, n, k):
            dve_queries(dve, n, k)
            dve_rotate(dve, n, k)

        def dve_rotate(dve, n, k):
            dve.drain()
            dve.wait_ge(gathered[k], 4 * visit16(n, k))
            dve.tensor_tensor(PRD, G[k][:, :, DC:], rot_sel[:, :].unsqueeze(1).broadcast_to([P, GB, 2 * DR]), ALU.mult)
            dve.drain()
            dve.tensor_tensor(G[k][:, :, DC:DC + DR], PRD[:, :, 0:DR], PRD[:, :, DR:], ALU.add).then_inc(rot_done, 1)

        def dve_block(dve, b, n, k, early, ahead):
            c = col[:, k % 2, :]
            if ahead:
                dve_queries(dve, n + 1, (k + 1) % 4)
            dve.wait_ge(pb_exp, C0 + n - 1)
            dve.wait_ge(s_done, C0 + n + 1)
            dve.memset(c[:, 3:4], 0.0)
            dve.tensor_tensor_reduce(SM[k % 2], bank[k % 2][:, 0:2 * P], cst("mask_early" if early else "mask_main"), 1.0, -3e38,
                                     ALU.add, ALU.max, c[:, 0:1])
            dve.drain()
            dve.tensor_scalar(c[:, 1:2], c[:, 0:1], -SCALE2, None, ALU.mult).then_inc(sm_ready, 1)
            if not (early and k == 0):
                dve_attended(dve, n - 1, (k + 3) % 4)
            if ahead:
                dve_rotate(dve, n + 1, (k + 1) % 4)
            dve.wait_ge(pb_exp, C0 + n + 1)
            dve.reciprocal(c[:, 3:4], c[:, 2:3])
            dve.drain()
            dve.tensor_scalar(PB[k % 2], PB[k % 2], c[:, 3:4], None, ALU.mult).then_inc(pn_ready, 1)
            dve.wait_ge(ob_done, C0 + n - 1)
            dve.wait_ge(tp_done, C0 + n + 1)
            dve.tensor_copy(PTS[k % 2], bank[4 + k % 2][:, 0:2 * P]).then_inc(pts_ready, 1)
            if not ahead:
                dve_attended(dve, n, k)

        @block.sync
        def _(sp):
            sp.dma_start(X[:, :, :], attn["x"].rearrange("b (t p) d -> p (b t) d", p=P)).then_inc(x_loaded, 16)
            sp_ffn(sp, 0)
            sp_sel(sp)
            sp_ffn(sp, 1)
            sp.wait_ge(x_ready, 3)
            sp.dma_start(out.rearrange("b (t p) d -> p (b t) d", p=P), X[:, :, :]).then_inc(stored, 16)
            sp.wait_ge(stored, 16)

        @block.gpsimd
        def _(pool):
            pool.memset(neghalf[:, :], -0.5)
            pool.memset(spare[:, 0:1], 0.0).then_inc(setup_done, 1)
            pool_fill(pool, 0)
            for n in range(3):
                pool_rstd(pool, n)
            pool_sel(pool)
            pool.wait_ge(x_ready, 2)
            pool_fill(pool, 1)
            for n in range(4, 7):
                pool_rstd(pool, n)

        @block.tensor
        def _(pe):
            pe.wait_ge(const_loaded, 16)
            pe.wait_ge(setup_done, 2)
            pe.wait_ge(w_loaded, 16 * 9)
            pe_ffn(pe, 0)
            pe_sel(pe)
            pe_ffn(pe, 1)

        @block.scalar
        def _(act):
            act.dma_start(const[:, :], const_ap).then_inc(const_loaded, 16)
            for dst, src in ((w_qkv[:, :], ffn["w_qkv"]), (w_o[:, :], ffn["w_o"]), (wg[:, :], ffn["wg"]),
                             (gains[:, 0, :], ffn["g1"].partition_broadcast(P)), (gains[:, 1, :], ffn["b1"].partition_broadcast(P)),
                             (gains[:, 2, :], ffn["g2"].partition_broadcast(P)), (gains[:, 3, :], ffn["b2"].partition_broadcast(P)),
                             (bb2[:, :], ffn["bb2"])):
                act.dma_start(dst, src).then_inc(w_loaded, 16)
            act.dma_start(bb1[:, :, :], ffn["bb1"].rearrange("e (f p) -> p e f", p=P), allow_slow_non_contiguous=True).then_inc(w_loaded, 16)
            for dst, src in ((WKV[:, 0:DR], attn["W_kr"]), (WKV[:, DR:DR + HALF], attn["W_kr"][:, HALF:]),
                             (WKV[:, DR + HALF:2 * DR], attn["W_kr"][:, 0:HALF]), (WKV[:, 2 * DR:], attn["W_dkv"]),
                             (WIQ[:, :], attn["idx_wq"]), (WIK[:, 0:DH], attn["idx_wk"]), (WIK[:, DH:], attn["idx_wk"]),
                             (WDQ[:, :], attn["W_dq"]), (WQR[:, 0, :], attn["W_qr"]),
                             (idx_w[:, :], attn["idx_w"].partition_broadcast(P))):
                act.dma_start(dst, src).then_inc(sel_w_loaded, 16)
            for x in range(2):
                act.dma_start(WQR[:, 1, :].rearrange("p (h x i) -> p h x i", h=NH, x=2)[:, :, x, :],
                              attn["W_qr"].rearrange("p (h x i) -> p h x i", h=NH, x=2)[:, :, 1 - x, :]).then_inc(sel_w_loaded, 16)
            act.dma_start(WOUT[:, :, :], attn["W_out"].rearrange("(j p) d -> p j d", p=P)).then_inc(sel_w_loaded, 16)
            act.dma_start(delta_row[:, 0, 0:HALF], attn["raw_delta"].partition_broadcast(P)).then_inc(delta_loaded, 16)
            for x in range(P // HALF):
                act.dma_start(delta_col[x * HALF:(x + 1) * HALF, 0:1], attn["raw_delta"].rearrange("(i a) -> i a", a=1)).then_inc(delta_loaded, 16)
            act.wait_ge(setup_done, 1)
            act.activation(spare[:, 1:2], spare[:, 0:1], ACT.Copy).then_inc(exp_done, EXP0)
            act.activation(spare[:, 2:3], spare[:, 0:1], ACT.Copy).then_inc(gelu_done, GELU0)
            act_ffn(act, 0)
            act_sel(act)
            act_ffn(act, 1)

        @block.vector
        def _(dve):
            dve.wait_ge(const_loaded, 16)
            dve.wait_ge(w_loaded, 16 * 9)
            dve.wait_ge(setup_done, 1)
            dve.tensor_copy(ident_b[:, :], ident)
            dve.tensor_copy(mask_qk[:, :], cst("mask_qk"))
            dve.tensor_copy(mask_kq[:, :], cst("mask_kq")).then_inc(setup_done, 1)
            dve.memset(spare[:, 4:5], 0.0).then_inc(pv_done, PV0)
            dve.memset(spare[:, 5:6], 0.0).then_inc(o_turned, OTURN0)
            dve.memset(spare[:, 6:7], 0.0).then_inc(att_done, ATT0)
            dve.memset(spare[:, 7:8], 0.0).then_inc(y_done, Y0)
            dve.memset(spare[:, 8:9], 0.0).then_inc(acc_done, ACC0)
            dve.memset(spare[:, 9:10], 0.0).then_inc(max_done, MAX0)
            for x in range(8):
                m = (s_done, sm_ready, gts_ready, pb_exp, tp_done, pts_ready, ob_done, oa_ready)[x]
                dve.memset(spare[:, 10 + x:11 + x], 0.0).then_inc(m, C0)
            dve.wait_ge(x_loaded, 16)
            dve_ffn(dve, 0)
            dve_sel(dve)
            dve_ffn(dve, 1)


_INS = ["L0_attn_x", "L0_attn_W_dkv", "L0_attn_W_uk", "L0_attn_W_uv", "L0_attn_W_dq", "L0_attn_W_uq", "L0_attn_W_qr",
        "L0_attn_W_kr", "L0_attn_W_out", "L0_attn_idx_wq", "L0_attn_idx_wk", "L0_attn_idx_w", "L0_attn_raw_delta",
        "L0_ffn_w_qkv", "L0_ffn_w_o", "L0_ffn_g1", "L0_ffn_b1", "L0_ffn_wg", "L0_ffn_w1", "L0_ffn_bb1", "L0_ffn_w2",
        "L0_ffn_bb2", "L0_ffn_g2", "L0_ffn_b2"]


def kernel(**inputs):
    import concourse.bacc as bacc
    from concourse.bass_utils import run_bass_kernel_spmd

    nc = bacc.Bacc("TRN2", target_bir_lowering=False, num_devices=1)
    arrays, aps = {}, {}
    for name in _INS:
        a = np.ascontiguousarray(inputs[name])
        arrays[f"in_{name}"] = a
        aps[name] = nc.dram_tensor(f"in_{name}", a.shape, mybir.dt.from_np(a.dtype), kind="ExternalInput").ap()
    table = np.ascontiguousarray(np.concatenate(list(constants().values()), axis=1))
    arrays["in_constants"] = table
    const_ap = nc.dram_tensor("in_constants", table.shape, F32, kind="ExternalInput").ap()
    out = nc.dram_tensor("out_x", (B, L, D), F32, kind="ExternalOutput").ap()
    turns = rotations()
    arrays["in_rotations"] = turns
    rot_ap = nc.dram_tensor("in_rotations", turns.shape, F32, kind="ExternalInput").ap()
    build(nc, aps, const_ap, rot_ap, out)
    r = run_bass_kernel_spmd(nc, [arrays], core_ids=[0])
    return r.results[0]["out_x"]
```

```python
from contextlib import ExitStack

import numpy as np

import concourse.bass as bass
from concourse import mybir

F32 = mybir.dt.float32
BF16 = mybir.dt.bfloat16
U32 = mybir.dt.uint32
ALU = mybir.AluOpType
ACT = mybir.ActivationFunctionType
AX_X = mybir.AxisListType.X

P = 128
B, L, D = 2, 1024, 128
TOK = B * L
NT = TOK // P
TB = L // P
BANK = 512
NG = TOK // BANK

H, HD = 16, 8
PAIRS = B * H // 2
E, F = 8, 512
FC = F // P
FFN_EPS = 1e-5
NEG = -1.0e30
NPROD = 3 * 3
STRIP = 32
ROWS = NPROD * HD
MAXROW = 96
MAXROWS = 3
RING = 4

NH, DH, DC, DCQ, DR = 8, 64, 32, 64, 32
NIH = 4
LW, KTS = 64, 96
NSEL = KTS - LW
HALF = DR // 2
BT = 16
NB = L // BT
GB = BT // 4
LP = L + P - BT
ROWKV = DC + 2 * DR
SCALE2 = float((DH + DR) ** -0.5)

PT_RING = 8
S_RING = 3
UNITS1 = [(s, t, hf) for t in range(TB) for s in range(2) for hf in range(2) if hf * BANK < (t + 1) * P]
UNITS2 = [(s, kc, hf) for kc in range(TB) for hf in range(2) for s in range(2) if (hf + 1) * BANK > kc * P]
N1, N2 = len(UNITS1), len(UNITS2)
MAX_AT = 5
ROW_LOADS = 16 * (2 * 2 * 3 + 1)
EARLY = N1 // 2

ARENA = 136 * 1024


def constants():
    f = np.float32
    q, k = np.arange(P)[:, None], np.arange(P)[None, :]
    sel = LW + np.arange(NSEL)[None, :]
    override = sel > q
    g, h, t = (a.reshape(-1, 1) for a in np.meshgrid(np.arange(GB), np.arange(NH), np.arange(4), indexing="ij"))
    tok = 4 * g + t
    early, main = k < LW, (k >= tok + 1) & (k <= tok + LW)
    own = (k // NSEL) == t
    theta = (1.0 / f(10000.0) ** (f(2.0) * np.arange(HALF, dtype=f) / f(DR))).astype(f).astype(np.float64)
    a_sel = (LW + np.arange(P) % NSEL)[:, None] * theta[None, :]
    sign = np.where(np.arange(P) % DR < HALF, -1.0, 1.0)[:, None]
    c = {"ident": np.eye(P),
         "mask_qk": np.where(k > q, NEG, 0.0),
         "mask_kq": np.where(q > k, NEG, 0.0),
         "iota8": np.broadcast_to(np.arange(E), (P, E)),
         "nonlocal": np.where(k <= q, 3e38, -3e38),
         "keep": np.where(override, 0.0, 1.0),
         "fill": np.where(override, np.broadcast_to(sel, (P, NSEL)), 0.0),
         "mask_early": np.where(np.concatenate([np.broadcast_to(early, (P, P)), own], 1), 0.0, NEG),
         "mask_main": np.where(np.concatenate([main, own], 1), 0.0, NEG),
         "cos_sel": np.concatenate([np.cos(a_sel)] * 2, 1),
         "sin_sel": np.concatenate([-np.sin(a_sel), np.sin(a_sel)], 1),
         "sign_row": np.broadcast_to(sign[:DR].T, (P, DR)),
         "swap": np.eye(P)[np.arange(P) ^ HALF],
         "sign": sign}
    return {n: np.ascontiguousarray(v.astype(f)) for n, v in c.items()}


def rotations():
    theta = (1.0 / np.float32(10000.0) ** (np.float32(2.0) * np.arange(HALF, dtype=np.float32) / np.float32(DR))).astype(np.float32)
    th = np.tile(theta.astype(np.float64), P // HALF)[:, None]
    t = np.arange(L)
    sign = np.where(np.arange(P) % DR < HALF, -1.0, 1.0)[:, None]
    tabs = []
    for pos in (t, np.where(t < LW, t, 2 * t - (LW - 1))):
        a = pos[None, :] * th
        tabs += [np.cos(a), sign * np.sin(a)]
    return np.ascontiguousarray(np.stack(tabs, 1).astype(np.float32))


def const_layout():
    at, off = {}, 0
    for n, v in constants().items():
        at[n] = (off, v.shape[1])
        off += v.shape[1]
    return at, off


def build(nc, ins, const_ap, rot_ap, out):
    at, width = const_layout()
    ffn = {n[7:]: a for n, a in ins.items() if n.startswith("L0_ffn_")}
    attn = {n[8:]: a for n, a in ins.items() if n.startswith("L0_attn_")}
    q_rows = nc.dram_tensor("q_rows", (PAIRS, 2, HD, 3, L), BF16, kind="Internal").ap()
    k_rows = nc.dram_tensor("k_rows", (PAIRS, 2, HD, 3, L), BF16, kind="Internal").ap()
    kv_rows = nc.dram_tensor("kv_rows", (B * LP, ROWKV), F32, kind="Internal").ap()

    with ExitStack() as ctx:
        def sb(name, shape, dt=F32):
            return ctx.enter_context(nc.sbuf_tensor(name, shape, dt))

        def sem(name):
            return ctx.enter_context(nc.semaphore(name))

        bank = [ctx.enter_context(nc.psum_tensor(f"bank{i}", [P, BANK], F32)) for i in range(8)]

        const = sb("const", [P, width])

        def cst(name):
            o, n = at[name]
            return const[:, o:o + n]

        ident = cst("ident")
        ident_b = sb("ident_b", [P, P], BF16)
        mask_qk = sb("mask_qk_b", [P, P], BF16)
        mask_kq = sb("mask_kq_b", [P, P], BF16)

        X = sb("X", [P, NT, D])
        XN = sb("XN", [P, NT, D])
        XT = sb("XT", [P, TOK])
        ATT = sb("ATT", [P, NT, D])
        ACC = ATT
        HN = sb("HN", [P, NT, D])
        stats = sb("stats", [P, NT, 6])
        mv = sb("mv", [P, NT, 2])
        vareps = sb("vareps", [P, NT])
        rstd = sb("rstd", [P, NT])
        neghalf = sb("neghalf", [P, NT])

        w_qkv = sb("w_qkv", [P, 3 * D])
        w_o = sb("w_o", [P, D])
        wg = sb("wg", [P, E])
        gains = sb("gains", [P, 4, D])
        bb1 = sb("bb1", [P, E, FC])
        bb2 = sb("bb2", [E, D])

        bias1 = [sb(f"bias1_{i}", [P, FC]) for i in range(2)]
        WKV = sb("WKV", [P, 2 * DR + DC])
        WIQ = sb("WIQ", [P, NIH * DH])
        WIK = sb("WIK", [P, 2 * DH])
        WDQ = sb("WDQ", [P, DCQ])
        WQR = sb("WQR", [DCQ, NH * DR])
        AQ = sb("AQ", [DCQ, NH * DC])
        MO = sb("MO", [P, NH * DC // P, D])
        UQT = sb("UQT", [P, NH // 2, DCQ])
        UKT = sb("UKT", [P, NH // 2, DC])
        UVT = sb("UVT", [P, NH // 2, DC])
        WOUT = sb("WOUT", [P, NH // 2, D])
        idx_w = sb("idx_w", [P, NIH])
        delta_col = sb("delta_col", [P, 6])
        delta_row = sb("delta_row", [P, 6, DR])
        rot_sel = sb("rot_sel", [P, 2 * DR])

        arena = sb("arena", [P, ARENA // 4])
        views = {}

        def view(part, shape, dt=F32, rows=P):
            n = int(np.prod(shape)) * (2 if dt == BF16 else 4) // 4
            off = views.get(part, 0)
            views[part] = off + n
            assert off + n <= ARENA // 4, (part, off + n)
            v = arena[0:rows, off:off + n]
            v = v if dt == F32 else v.bitcast(dt)
            if len(shape) == 1:
                return v
            names = "abcd"[:len(shape)]
            sizes = {x: m for x, m in zip(names, shape)}
            return v.rearrange(f"p ({' '.join(names)}) -> p {' '.join(names)}", **sizes)

        views["experts"] = views.get("ffn", 0)
        qparts = view("ffn", (3, TOK), BF16)
        kparts = view("ffn", (3, TOK), BF16)
        H1 = [view("experts", (FC, BANK)) for i in range(2)]
        WT = view("experts", (TOK,), rows=E)
        assert views["experts"] <= views["ffn"]
        rest = view("ffn", (2, BANK))
        VA = view("ffn", (PAIRS, 2, TB, STRIP))
        QB = [[view("ffn", (L,), BF16) for h in range(2)] for i in range(RING)]
        KB = [[view("ffn", (L,), BF16) for h in range(2)] for i in range(RING)]
        VS = [view("ffn", (2, TB, STRIP)) for i in range(RING)]
        OT = view("ffn", (BANK,))
        PT = [view("ffn", (BANK,)) for i in range(PT_RING)]
        rowmax = view("ffn", (2, 2, TB))
        maxrest = view("ffn", (2, TB))
        MB = view("ffn", (TB, P), BF16)
        rsum = view("ffn", (2, 2, 4))
        W1 = [view("ffn", (F,)) for i in range(2)]
        W2 = [view("ffn", (FC, D)) for i in range(2)]

        QALL = view("sel", (NH, TOK), rows=96)
        OA = QALL[0:DC]
        RAW = QALL.rearrange("p h t -> p (h t)")
        KL = view("sel", (B, LP), rows=96)
        KVS = view("sel", (NT, ROWKV))
        G = [view("sel", (GB, ROWKV)) for i in range(4)]
        QS = [view("sel", (P,), rows=96) for i in range(2)]
        GTS = [view("sel", (GB, P), rows=ROWKV) for i in range(2)]
        PRD = view("sel", (GB, 2 * DR))
        SM = [view("sel", (2 * P,)) for i in range(2)]
        PB = [view("sel", (2 * P,)) for i in range(2)]
        PTS = [view("sel", (2 * P,)) for i in range(2)]
        VW = [view("sel", (DC,)) for i in range(4)]
        IDX = view("sel", (NT * P // 4,)).bitcast(U32)
        col = view("sel", (2, 4))
        SC = view("sel", (L,))
        RL = [view("sel", (L,)) for i in range(2)]
        best = view("sel", (4, 8))
        bidx = view("sel", (4, 8)).bitcast(U32)
        bidf = view("sel", (2, NSEL))
        views["sel2"] = views["sel"]
        QI = view("sel", (2, TOK))
        KI = view("sel", (TOK,))
        views["sel3"] = views["sel2"]
        OAX = view("sel3", (NH * DC // P, TOK))
        CQ = view("sel2", (TOK,), rows=DCQ)
        ROT = view("sel2", (4, L))
        ATTf = ATT[:, :, :].rearrange("p t d -> p (t d)")
        HNf = HN[:, :, :].rearrange("p t d -> p (t d)")
        XNf = XN[:, :, :].rearrange("p t d -> p (t d)")
        MU, QRD, QRL = ([t[:, i * L:(i + 1) * L] for i in range(2)] for t in (ATTf, HNf, XNf))
        QT, T1 = RL, SC
        lg = sb("lg", [P, NT, E])
        pr = sb("pr", [P, NT, E])
        top8 = sb("top8", [P, NT, 8])
        idx8 = sb("idx8", [P, NT, 8], U32)
        idxf = sb("idxf", [P, NT, 2])
        g16 = sb("g16", [P, 4, NT])
        oh = sb("oh", [P, 2, NT, E])
        W8 = sb("W8", [P, NT, E])
        IB = [sb(f"IB{i}", [P, P // 4], U32) for i in range(2)]
        turn = sb("turn", [P, 2, P // BT])
        spare = sb("spare", [P, 20])

        x_loaded, const_loaded, w_loaded, sel_w_loaded = (sem(n) for n in ("x_loaded", "const_loaded", "w_loaded", "sel_w_loaded"))
        setup_done, filled = sem("setup_done"), sem("filled")
        var_ready, rstd_ready = sem("var_ready"), sem("rstd_ready")
        xn_ready, h_ready = sem("xn_ready"), sem("h_ready")
        turned, xt_ready = sem("turned"), sem("xt_ready")
        qk_done, p1_done, r1_done, p2_done, p3_done = (sem(n) for n in ("qk_done", "p1_done", "r1_done", "p2_done", "p3_done"))
        v_done, va_ready = sem("v_done"), sem("va_ready")
        rows_spilled = [sem(f"rows_spilled{b}") for b in range(B)]
        rows_loaded = [sem(f"rows_loaded{i}") for i in range(RING)]
        s1_done, max_done, mb_ready, mt_done, maxrow_ready = (sem(n) for n in ("s1_done", "max_done", "mb_ready", "mt_done", "maxrow_ready"))
        st_done, exp_done, pv_done, ot_ready, o_turned, att_done = (sem(n) for n in ("st_done", "exp_done", "pv_done", "ot_ready", "o_turned", "att_done"))
        o_done, r_done, gate_done, lg_ready, eg_ready, w8_ready = (sem(n) for n in ("o_done", "r_done", "gate_done", "lg_ready", "eg_ready", "w8_ready"))
        w8_turned, wt_ready, b2_done, acc0_ready = (sem(n) for n in ("w8_turned", "wt_ready", "b2_done", "acc0_ready"))
        a_done, gelu_done, y_done, acc_done = (sem(n) for n in ("a_done", "gelu_done", "y_done", "acc_done"))
        ew_loaded = [sem(f"ew_loaded{i}") for i in range(2)]
        x_ready = sem("x_ready")
        stored = sem("stored")
        raw_loaded, uqk_turned, uqk_ready, prep_done, prep_ready = (sem(n) for n in ("raw_loaded", "uqk_turned", "uqk_ready", "prep_done", "prep_ready"))
        delta_loaded, sig_ready, ang_ready, trig_ready, rot_sel_ready = (sem(n) for n in ("delta_loaded", "sig_ready", "ang_ready", "trig_ready", "rot_sel_ready"))
        qi_done, qi_ready, ki_done, ki_ready = (sem(n) for n in ("qi_done", "qi_ready", "ki_done", "ki_ready"))
        kv_done, kv_log, kv_ready, kv_stored, kv_padded = (sem(n) for n in ("kv_done", "kv_log", "kv_ready", "kv_stored", "kv_padded"))
        si_done, relu_done, sc_used, best_ready, i_turned, idx_ready = (sem(n) for n in ("si_done", "relu_done", "sc_used", "best_ready", "i_turned", "idx_ready"))
        rot_loaded, rot_ready, cq_done, cq_ready = (sem(n) for n in ("rot_loaded", "rot_ready", "cq_done", "cq_ready"))
        kt_done, kt_log, kt_c, kl_ready = (sem(n) for n in ("kt_done", "kt_log", "kt_c", "kl_ready"))
        qt_done, qt_ready, mu_done, mu_log, mu_ready = (sem(n) for n in ("qt_done", "qt_ready", "mu_done", "mu_log", "mu_ready"))
        mus_done, qr_ready = sem("mus_done"), sem("qr_ready")
        q_placed = [sem(f"q_placed{i}") for i in range(2)]
        vw_loaded = [sem(f"vw_loaded{i}") for i in range(4)]
        gathered = [sem(f"gathered{i}") for i in range(4)]
        staged = sem("staged")
        qs_ready, rot_done, gt_done, gts_ready, s_done, sm_ready = (sem(n) for n in ("qs_ready", "rot_done", "gt_done", "gts_ready", "s_done", "sm_ready"))
        pb_exp, pn_ready, tp_done, pts_ready, ob_done, oa_ready = (sem(n) for n in ("pb_exp", "pn_ready", "tp_done", "pts_ready", "ob_done", "oa_ready"))
        oa_moved = [sem(f"oa_moved{b}") for b in range(B)]
        mix_done = sem("mix_done")
        C0 = 4

        EXP0, PV0, ATT0, GELU0, Y0, ACC0, MAX0, OTURN0, OT0 = S_RING, 2 * TB, 2, 4, 2, 2, S_RING, 1, 1
        block = ctx.enter_context(nc.Block())

        w1_d, w2_d = ffn["w1"], ffn["w2"].rearrange("e (c p) d -> e p c d", p=P)

        def sp_rows(sp, c, it, buf):
            g = PAIRS * c
            if not isinstance(it, int) or c:
                sp.wait_ge(pv_done, PV0 + TB * (g + it - RING + 1))
            for s in range(2):
                for dst, src, axis in ((QB, q_rows, 1), (KB, k_rows, 0)):
                    rows = src[it:it + 1, s] if isinstance(it, int) else src[bass.ds(it, 1), s]
                    rows = rows.rearrange("a d r t -> r (a d) t").unsqueeze(axis).broadcast_to([3, 3, HD, L])
                    for i in range(3):
                        sp.dma_start(dst[buf][s][i * 3 * HD:(i + 1) * 3 * HD, :], rows[i]).then_inc(rows_loaded[buf], 16)
            va = VA[:, :, :, :, :].rearrange("p a s k d -> p (a s k d)")
            n = 2 * TB * STRIP
            sp.dma_start(VS[buf][:, :, :, :].rearrange("p s k d -> p (s k d)"), va[:, bass.ds(it * n, n)]).then_inc(rows_loaded[buf], 16)

        def sp_expert(sp, c, e, buf):
            if not isinstance(e, int) or c or e >= 2:
                sp.wait_ge(y_done, Y0 + NG * E * c + NG * (e - 1))
            w1e = w1_d[e] if isinstance(e, int) else w1_d[bass.ds(e, 1)].rearrange("a d f -> (a d) f")
            w2e = w2_d[e] if isinstance(e, int) else w2_d[bass.ds(e, 1)].rearrange("a p c d -> p (a c) d")
            sp.dma_start(W1[buf], w1e).then_inc(ew_loaded[buf], 16)
            sp.dma_start(W2[buf], w2e).then_inc(ew_loaded[buf], 16)

        def sp_ffn(sp, c):
            if c:
                sp.wait_ge(x_ready, 2)
            sp_expert(sp, c, 0, 0)
            sp_expert(sp, c, 1, 1)
            for b in range(B):
                sp.wait_ge(p3_done, 8 * c + 8 // B * (b + 1))
                for src, dst in ((qparts, q_rows), (kparts, k_rows)):
                    sp.dma_start(dst[b * (PAIRS // B):(b + 1) * (PAIRS // B)].rearrange("j s d r t -> (j s d) r t"),
                                 src[:, :, b * L:(b + 1) * L]).then_inc(rows_spilled[b], 16)
            sp.wait_ge(rows_spilled[0], 2 * 16 * (c + 1))
            sp.wait_ge(va_ready, NG * (c + 1))
            sp.wait_ge(filled, c + 1)
            for k in range(RING):
                sp_rows(sp, c, k, k)
            sp.wait_ge(rows_spilled[1], 2 * 16 * (c + 1))
            with sp.Fori(1, PAIRS // RING) as i:
                for k in range(RING):
                    sp_rows(sp, c, i * RING + k, k)
            with sp.Fori(1, E // 2) as i:
                sp_expert(sp, c, i * 2, 0)
                sp_expert(sp, c, i * 2 + 1, 1)


        def sp_sel(sp):
            sp.wait_ge(x_ready, 1)
            for dst, src in ((RAW[0:DCQ, 0:NH * DH], attn["W_uq"]), (RAW[0:DC, NH * DH:2 * NH * DH], attn["W_uk"]),
                             (RAW[0:DC, 2 * NH * DH:3 * NH * DH], attn["W_uv"])):
                sp.dma_start(dst, src).then_inc(raw_loaded, 16)
            sp.wait_ge(kv_ready, 4)
            for b in range(B):
                base = b * LP
                sp.dma_start(kv_rows[base + LW:base + LW + L].rearrange("(t p) n -> p t n", p=P),
                             KVS[:, b * TB:(b + 1) * TB, :]).then_inc(kv_stored, 16)
                sp.dma_start(kv_rows[base:base + LW], KVS[0:LW, b * TB, :]).then_inc(kv_stored, 16)
                tail = LP - LW - L
                sp.dma_start(kv_rows[base + LW + L:base + LP], KVS[0:tail, b * TB, :]).then_inc(kv_stored, 16)
            sp.wait_ge(relu_done, NT * NIH)
            sp.wait_ge(si_done, NT * NIH)
            sp.dma_start(ROT, rot_ap).then_inc(rot_loaded, 16)
            for n in range(2 * B):
                g, b = n // B, n % B
                for src, row, ready in ((QT, 0, qt_ready), (QRD, DC, qr_ready), (QRL, DC + DR, qr_ready)):
                    sp.wait_ge(ready, 2 * (n + 1))
                    for h in range(4):
                        sp.dma_start(QALL[row:row + DC, 4 * g + h, b * L:(b + 1) * L], src[n % 2][h * DC:(h + 1) * DC, :]).then_inc(q_placed[n % 2], 16)
            sp.wait_ge(kv_stored, 16 * 3 * B)
            with sp.Fori(0, B) as b:
                with sp.Fori(0, NB // 4) as i:
                    for k in range(4):
                        sp.wait_ge(ob_done, C0 + b * NB + i * 4 + k - 3)
                        sp.dma_start(VW[k], kv_rows[bass.ds(b * LP + i * (4 * BT) + k * BT, P), 0:DC]).then_inc(vw_loaded[k], 16)
            for b in range(B):
                sp.wait_ge(oa_ready, C0 + (b + 1) * NB)
                for h in range(NH):
                    sp.dma_start(OAX[h % 4 * DC:(h % 4 + 1) * DC, h // 4, b * L:(b + 1) * L], OA[:, h, b * L:(b + 1) * L]).then_inc(oa_moved[b], 16)

        def pool_rstd(pool, n):
            pool.wait_ge(var_ready, n + 1)
            pool.tensor_tensor(rstd[:, :], vareps[:, :], neghalf[:, :], ALU.pow).then_inc(rstd_ready, 1)


        def pool_ffn(pool, c):
            ln = (0, 4)[c]
            if c:
                pool.wait_ge(x_ready, 2)
            pool_rstd(pool, ln)
            pool_fill(pool, c)
            for n in (ln + 1, ln + 2):
                pool_rstd(pool, n)

        def pool_fill(pool, c):
            pool.memset(VA[:, :, :, :, HD:STRIP], 0.0)
            pool.drain()
            pool.memset(VA[:, :, :, :, HD:HD + 1], 1.0)
            pool.memset(MB[:, :, :], 0.0)
            for buf in range(RING):
                for s in range(2):
                    pool.drain()
                    pool.memset(QB[buf][s][64:MAXROW, :], 0.0)
                    pool.memset(KB[buf][s][64:MAXROW, :], 0.0)
                    pool.drain()
                    pool.memset(KB[buf][s][MAXROW:MAXROW + MAXROWS, :], 1.0)
            pool.drain()
            pool.memset(spare[:, 3:4], float(c)).then_inc(filled, 1)

        def pool_sel(pool):
            pool_rstd(pool, 3)
            pool.wait_ge(kv_stored, 16 * 3 * B)
            with pool.Fori(0, NT // 2) as i:
                for half in range(2):
                    pool.wait_ge(idx_ready, 8 * i + 4 * (half + 1))
                    pool.tensor_copy(IB[half][:, :], IDX[:, bass.ds((2 * i + half) * (P // 4), P // 4)]).then_inc(staged, 1)
                    pool.drain()
                    for k in range(P // BT):
                        pool.wait_ge(ob_done, C0 + i * (2 * P // BT) + half * (P // BT) + k - 3)
                        pool.tensor_tensor(turn[:, half, k:k + 1], neghalf[:, 0:1], neghalf[:, 0:1], ALU.add)
                        for g in range(GB):
                            pool.indirect_dma_start(G[k % 4][:, g, :], None, kv_rows,
                                                    bass.IndirectOffsetOnAxis(ap=IB[half][:, k * GB + g:k * GB + g + 1], axis=0))\
                                .then_inc(gathered[k % 4], 16)

        def pe_turn(pe, tile, n, ready, base):
            for g in range(NG):
                pe.wait_ge(ready, base + g + 1)
                for t in range(4):
                    m = pe.transpose(bank[g][:, t * P:(t + 1) * P], tile(4 * g + t), ident)
                m.then_inc(turned, 1)

        def pe_pass1(pe, c, it, buf, u, visit):
            s, qt, hf = UNITS1[u]
            n = PAIRS * c + it
            if u == 0:
                pe.wait_ge(rows_loaded[buf], ROW_LOADS * (PAIRS // RING * c + visit + 1))
            pe.wait_ge(max_done, MAX0 + N1 * n + u + 1 - S_RING)
            lo, hi = hf * BANK, min((qt + 1) * P, (hf + 1) * BANK)
            o = bank[u % S_RING]
            m = pe.matmul(o[:, 0:hi - lo], QB[buf][s][0:ROWS, qt * P:(qt + 1) * P], KB[buf][s][0:ROWS, lo:hi], start=True, stop=True)
            if hi == (qt + 1) * P:
                m = pe.matmul(o[:, hi - lo - P:hi - lo], ident_b[:, :], mask_qk[:, :], start=False, stop=True, skip_group_check=True)
            m.then_inc(s1_done, 1)

        def pe_maxrows(pe, c, it):
            n = PAIRS * c + it
            pe.wait_ge(att_done, ATT0 + n - 1)
            pe.wait_ge(mb_ready, n + 1)
            mt = bank[7][:, :].bitcast(BF16)
            for qt in range(TB):
                m = pe.transpose(mt[:, qt * P:(qt + 1) * P], MB[:, qt, :], ident_b[:, :])
            m.then_inc(mt_done, 1)

        def pe_scores(pe, c, it, buf, w):
            s, kc, hf = UNITS2[w]
            n = PAIRS * c + it
            if w == 0:
                pe.wait_ge(maxrow_ready, 2 * n + 2)
            pe.wait_ge(exp_done, EXP0 + N2 * n + w + 1 - S_RING)
            lo, hi = max(kc * P, hf * BANK), (hf + 1) * BANK
            o, rows = bank[S_RING + w % S_RING], MAXROW + MAXROWS
            m = pe.matmul(o[:, 0:hi - lo], KB[buf][s][0:rows, kc * P:(kc + 1) * P], QB[buf][s][0:rows, lo:hi], start=True, stop=True)
            if lo == kc * P:
                m = pe.matmul(o[:, 0:P], ident_b[:, :], mask_kq[:, :], start=False, stop=True, skip_group_check=True)
            m.then_inc(st_done, 1)

        def pe_values(pe, c, it, buf, kc):
            units = [w for w in range(N2) if UNITS2[w][1] == kc]
            n = PAIRS * c + it
            if kc == 0:
                pe.wait_ge(ot_ready, OT0 + n)
            pe.wait_ge(exp_done, EXP0 + N2 * n + units[-1] + 1)
            for w in units:
                s, _, hf = UNITS2[w]
                lo = max(kc * P, hf * BANK)
                r = (2 * s + hf) * STRIP
                m = pe.matmul(bank[6][r:r + STRIP, lo - hf * BANK:BANK], VS[buf][:, s, kc, :],
                              PT[w % PT_RING][:, 0:(hf + 1) * BANK - lo], start=(kc == 0), stop=True, skip_group_check=True)
            m.then_inc(pv_done, 1)

        def pe_outputs(pe, c, it):
            pe.wait_ge(att_done, ATT0 + PAIRS * c + it)
            pe.wait_ge(ot_ready, OT0 + PAIRS * c + it + 1)
            for t in range(4):
                m = pe.transpose(bank[7][:, t * P:(t + 1) * P], OT[:, t * P:(t + 1) * P], ident)
            m.then_inc(o_turned, 1)

        def ahead_units(left):
            return [(1, u) for u in range(EARLY, N1) if left >= 1] + [(2, u) for u in range(EARLY) if left >= 2]

        def pe_step(pe, c, b, it, buf, left, visit):
            todo = ahead_units(left)

            def ahead(n):
                for _ in range(min(n, len(todo))):
                    a, u = todo.pop(0)
                    pe_pass1(pe, c, it + a, (buf + a) % RING, u, visit + (buf + a) // RING)

            for kc in range(1, TB + 1):
                for w in [w for w in range(N2) if UNITS2[w][1] == kc]:
                    pe_scores(pe, c, it, buf, w)
                    ahead(1)
                if kc == MAX_AT and left >= 1:
                    pe_maxrows(pe, c, it + 1)
                pe_values(pe, c, it, buf, kc - 1)
            if left >= 1:
                pe_first_scores(pe, c, it + 1, (buf + 1) % RING, ahead)
            pe_outputs(pe, c, it)

        def pe_first_scores(pe, c, it, buf, ahead):
            for w in [w for w in range(N2) if UNITS2[w][1] == 0]:
                pe_scores(pe, c, it, buf, w)
                ahead(1)

        def pe_ffn(pe, c):
            n_turn = (0, 4)[c]
            pe_turn(pe, lambda t: XN[:, t, :], n_turn, xn_ready, NG * 2 * c)
            for n in range(8):
                if n % 2 == 0:
                    pe.wait_ge(xt_ready, NG * n_turn + n // 2 + 1)
                if n >= 4:
                    pe.wait_ge(r1_done, 8 * c + n - 3)
                pe.matmul(bank[4 + n % 4][:, :], w_qkv[:, (n % 2) * D:(n % 2 + 1) * D],
                          XT[:, (n // 2) * BANK:(n // 2 + 1) * BANK], start=True, stop=True).then_inc(qk_done, 1)
            for g in range(NG):
                for t in range(4):
                    m = pe.matmul(bank[g][:, t * P:(t + 1) * P], XT[:, (4 * g + t) * P:(4 * g + t + 1) * P],
                                  w_qkv[:, 2 * D:3 * D], start=True, stop=True)
                m.then_inc(v_done, 1)
            pe.wait_ge(va_ready, NG * (c + 1))
            pe.wait_ge(r1_done, 8 * (c + 1))
            for u in range(N1):
                pe_pass1(pe, c, 0, 0, u, 0)
            for u in range(EARLY):
                pe_pass1(pe, c, 1, 1, u, 0)
            pe_maxrows(pe, c, 0)
            pe_first_scores(pe, c, 0, 0, lambda n: None)
            run_steps(pe, pe_step, c)
            pe.wait_ge(att_done, ATT0 + PAIRS * (c + 1))
            for gq in range(NG):
                for t in range(4):
                    m = pe.transpose(bank[gq][:, t * P:(t + 1) * P], ATT[:, 4 * gq + t, :], ident)
                m.then_inc(turned, 1)
            for gq in range(NG):
                pe.wait_ge(xt_ready, NG * (n_turn + 1) + gq + 1)
                for t in range(4):
                    m = pe.matmul(bank[4 + gq][:, t * P:(t + 1) * P], XT[:, (4 * gq + t) * P:(4 * gq + t + 1) * P],
                                  w_o[:, :], start=True, stop=True)
                m.then_inc(o_done, 1)
            pe_turn(pe, lambda t: HN[:, t, :], n_turn + 2, h_ready, NG * c)
            pe.wait_ge(xt_ready, NG * (n_turn + 3))
            for t in range(NT):
                m = pe.matmul(bank[4][:, t * E:(t + 1) * E], XT[:, t * P:(t + 1) * P], wg[:, :], start=True, stop=True)
            m.then_inc(gate_done, 1)
            pe.wait_ge(w8_ready, c + 1)
            for gq in range(NG):
                for t in range(4):
                    m = pe.transpose(bank[gq][0:E, t * P:(t + 1) * P], W8[:, 4 * gq + t, :], ident)
                m.then_inc(w8_turned, 1)
            for gq in range(NG):
                pe.wait_ge(wt_ready, NG * c + gq + 1)
                for t in range(4):
                    m = pe.matmul(bank[4 + gq][:, t * P:(t + 1) * P], WT[:, (4 * gq + t) * P:(4 * gq + t + 1) * P],
                                  bb2[:, :], start=True, stop=True)
                m.then_inc(b2_done, 1)
            pe.wait_ge(acc0_ready, NG * (c + 1))
            with pe.Fori(0, E // 2) as i:
                pe_expert(pe, c, i * 2, 0, i)
                pe_expert(pe, c, i * 2 + 1, 1, i)

        def run_steps(eng, step, c):
            per = PAIRS // B // RING
            for b in range(B):
                n = per - (b == B - 1)
                with eng.Fori(0, n) as i:
                    for k in range(RING):
                        step(eng, c, b, i * RING + b * (PAIRS // B) + k, k, PAIRS, i + b * per)
            for k in range(RING):
                step(eng, c, B - 1, PAIRS - RING + k, k, RING - 1 - k, B * per - 1)

        def pe_expert(pe, c, e, buf, visit):
            pe.wait_ge(ew_loaded[buf], 32 * (E // 2 * c + 1 + visit))
            for tb in range(NG + 1):
                if tb < NG:
                    for f in range(FC):
                        n = E * NG * FC * c + e * (NG * FC) + tb * FC + f
                        pe.wait_ge(gelu_done, GELU0 + n - 3)
                        pe.matmul(bank[f][:, :], W1[buf][:, f * P:(f + 1) * P], XT[:, tb * BANK:(tb + 1) * BANK],
                                  start=True, stop=True).then_inc(a_done, 1)
                if tb >= 1:
                    u = E * NG * c + e * NG + tb - 1
                    pe.wait_ge(gelu_done, GELU0 + (u + 1) * FC)
                    pe.wait_ge(acc_done, ACC0 + u - 1)
                    k = (tb - 1) % 2
                    for t in range(4):
                        for f in range(FC):
                            m = pe.matmul(bank[4 + k][:, t * P:(t + 1) * P], H1[k][:, f, t * P:(t + 1) * P],
                                          W2[buf][:, f, :], start=(f == 0), stop=(f == FC - 1))
                    m.then_inc(y_done, 1)

        def pe_sel(pe):
            pe_turn(pe, lambda t: XN[:, t, :], 3, xn_ready, NG)
            pe.wait_ge(sel_w_loaded, 16 * 11)
            pe.wait_ge(raw_loaded, 16 * 3)
            for j in range(NH // 2):
                pe.transpose(bank[4][:, j * DCQ:(j + 1) * DCQ], RAW[0:DCQ, j * P:(j + 1) * P], ident[0:DCQ, 0:DCQ])
            for k in range(2):
                for j in range(NH // 2):
                    o = (k + 1) * NH * DH + j * P
                    m = pe.transpose(bank[5][:, (4 * k + j) * DC:(4 * k + j + 1) * DC], RAW[0:DC, o:o + P], ident[0:DC, 0:DC])
            m.then_inc(uqk_turned, 1)
            pe.wait_ge(uqk_ready, 3)
            for h in range(NH):
                r, j = slice((h % 2) * DH, (h % 2 + 1) * DH), h // 2
                pe.matmul(bank[6 + h % 2][0:DCQ, j * DC:(j + 1) * DC], UQT[r, j, :], UKT[r, j, :], start=True, stop=True)
            for h in range(NH):
                r, j = slice((h % 2) * DH, (h % 2 + 1) * DH), h // 2
                m = pe.matmul(bank[4][h % 4 * DC:(h % 4 + 1) * DC, h // 4 * D:(h // 4 + 1) * D], UVT[r, j, :], WOUT[r, j, :],
                              start=True, stop=True)
            m.then_inc(prep_done, 1)
            pe.wait_ge(prep_ready, 3)
            for n in range(8):
                pe.wait_ge(xt_ready, NG * 3 + n // 2 + 1)
                pe.matmul(bank[n][:, :], WIQ[:, (n % 2) * P:(n % 2 + 1) * P], XT[:, (n // 2) * BANK:(n // 2 + 1) * BANK],
                          start=True, stop=True).then_inc(qi_done, 1)
            for n in range(4):
                pe.wait_ge(qi_ready, n + 1)
                pe.matmul(bank[n][:, :], WIK[:, :], XT[:, n * BANK:(n + 1) * BANK], start=True, stop=True).then_inc(ki_done, 1)
            for q in range(4):
                pe.wait_ge(qi_ready, 5 + q)
                for t in range(4):
                    m = pe.matmul(bank[4 + q][:, t * P:t * P + ROWKV], XT[:, (4 * q + t) * P:(4 * q + t + 1) * P], WKV[:, :],
                                  start=True, stop=True)
                m.then_inc(kv_done, 1)
            pe.wait_ge(qi_ready, 8)
            pe.wait_ge(ki_ready, 4)
            pe.wait_ge(kv_ready, 4)
            for tile in range(NT):
                b, w = tile // TB, (tile % TB) * P + LW
                for h in range(NIH):
                    u = tile * NIH + h
                    if u >= 3:
                        pe.wait_ge(relu_done, u - 2)
                    r = slice((h % 2) * DH, (h % 2 + 1) * DH)
                    for half in range((w + BANK - 1) // BANK):
                        lo, hi = half * BANK, min(w, (half + 1) * BANK)
                        m = pe.matmul(bank[2 * (u % 3) + half][:, 0:hi - lo], QI[r, h // 2, tile * P:(tile + 1) * P],
                                      KI[r, b * L + lo:b * L + hi], start=True, stop=True)
                    m.then_inc(si_done, 1)
                if tile >= 1:
                    pe_index(pe, tile - 1)
            pe_index(pe, NT - 1)
            pe.wait_ge(relu_done, NT * NIH)
            pe.wait_ge(idx_ready, 4 * NT)
            for n in range(4):
                pe.matmul(bank[n][0:DCQ, :], WDQ[:, :], XT[:, n * BANK:(n + 1) * BANK], start=True, stop=True).then_inc(cq_done, 1)
            for n in range(4):
                pe.matmul(bank[4 + n][0:ROWKV, :], WKV[:, :], XT[:, n * BANK:(n + 1) * BANK], start=True, stop=True).then_inc(kt_done, 1)
            pe.wait_ge(cq_ready, 4)
            pe.wait_ge(kl_ready, 1)
            pe_raw_queries(pe, 0)
            for n in range(2 * B):
                if n + 1 < 2 * B:
                    pe_raw_queries(pe, n + 1)
                for half in range(2):
                    if n >= 1:
                        pe.wait_ge(qr_ready, 2 * n)
                    pe.wait_ge(mu_ready, 2 * n + half + 1)
                    pe.matmul(bank[4 + half][:, :], cst("swap"), MU[n % 2][:, half * BANK:(half + 1) * BANK], start=True, stop=True)\
                      .then_inc(mus_done, 1)
            pe.wait_ge(qr_ready, 2 * 2 * B)
            pe.wait_ge(qt_ready, 2 * 2 * B)
            run_blocks(pe, pe_ahead, pe_block)
            for gq in range(NG):
                if gq % (NG // B) == 0:
                    pe.wait_ge(oa_moved[gq // (NG // B)], 16 * NH)
                for t in range(4):
                    tile = 4 * gq + t
                    for x in range(NH * DC // P):
                        m = pe.matmul(bank[gq][:, t * P:(t + 1) * P], OAX[:, x, tile * P:(tile + 1) * P], MO[:, x, :],
                                      start=(x == 0), stop=(x == NH * DC // P - 1))
                m.then_inc(mix_done, 1)

        def pe_raw_queries(pe, n):
            g, b = n // B, n % B
            for half in range(2):
                blk = slice(b * L + half * BANK, b * L + (half + 1) * BANK)
                if n >= 1:
                    pe.wait_ge(qt_ready, 2 * (n - 1) + half + 1)
                pe.matmul(bank[half][:, :], AQ[:, g * P:(g + 1) * P], CQ[:, blk], start=True, stop=True).then_inc(qt_done, 1)
                if n >= 2:
                    pe.wait_ge(mu_ready, 2 * (n - 2) + half + 1)
                pe.matmul(raw_bank(n, half)[:, :], WQR[:, g * P:(g + 1) * P], CQ[:, blk], start=True, stop=True).then_inc(mu_done, 1)

        def raw_bank(n, half):
            return bank[(2, 6)[n % 2] + half]

        def pe_index(pe, tile):
            pe.wait_ge(best_ready, tile + 1)
            if tile >= 1:
                pe.wait_ge(idx_ready, 4 * tile)
            pe.transpose(bank[6][0:NSEL, 0:P], bidf[:, tile % 2, :], ident).then_inc(i_turned, 1)

        def run_blocks(eng, ahead, block_):
            with eng.Fori(0, B) as b:
                ahead(eng, b, b * NB, 0)
                for k in range(4):
                    block_(eng, b, b * NB + k, k, True, ahead)
                with eng.Fori(1, NB // 4 - 1) as i:
                    for k in range(4):
                        block_(eng, b, b * NB + i * 4 + k, k, False, ahead)
                for k in range(4):
                    block_(eng, b, b * NB + (NB - 4) + k, k, False, ahead if k < 3 else None)

        def pe_ahead(pe, b, n, k):
            pe_local(pe, b, n, k)
            pe_gt(pe, n, k)
            pe_sel_scores(pe, n, k)

        def pe_local(pe, b, n, k):
            pe.wait_ge(qs_ready, n + 1)
            pe.wait_ge(sm_ready, C0 + n - 1)
            keys = KL.rearrange("p b t -> p (b t)")
            pe.matmul(bank[k % 2][:, 0:P], QS[k % 2], keys[:, bass.ds(n * BT + b * (LP - L), P)], start=True, stop=True)

        def pe_gt(pe, n, k):
            pe.wait_ge(rot_done, n + 1)
            pe.wait_ge(gts_ready, C0 + n - 1)
            for g in range(GB):
                m = pe.transpose(bank[2 + k % 2][0:ROWKV, g * P:(g + 1) * P], G[k][:, g, :], ident)
            m.then_inc(gt_done, 1)

        def pe_sel_scores(pe, n, k):
            pe.wait_ge(gts_ready, C0 + n + 1)
            for g in range(GB):
                m = pe.matmul(bank[k % 2][g * STRIP:(g + 1) * STRIP, P:2 * P], QS[k % 2][:, g * STRIP:(g + 1) * STRIP],
                              GTS[k % 2][:, g, :], start=True, stop=True)
            m.then_inc(s_done, 1)

        def pe_block(pe, b, n, k, early, ahead):
            k1 = (k + 1) % 4
            if ahead:
                pe_local(pe, b, n + 1, k1)
                pe_gt(pe, n + 1, k1)
            pe.wait_ge(pn_ready, n + 1)
            pe.wait_ge(pts_ready, C0 + n - 1)
            for x in range(2):
                m = pe.transpose(bank[4 + k % 2][:, x * P:(x + 1) * P], PB[k % 2][:, x * P:(x + 1) * P], ident)
            m.then_inc(tp_done, 1)
            if ahead:
                pe_sel_scores(pe, n + 1, k1)
            pe.wait_ge(vw_loaded[k], visit16(n, k))
            pe.wait_ge(oa_ready, C0 + n - 1)
            pe.wait_ge(pts_ready, C0 + n + 1)
            o = bank[6 + k % 2]
            pe.matmul(o[0:DC, 0:P], VW[k], PTS[k % 2][:, 0:P], start=True, stop=True)
            for g in range(GB):
                m = pe.matmul(o[0:DC, g * STRIP:(g + 1) * STRIP], G[k][:, g, 0:DC], PTS[k % 2][:, P + g * STRIP:P + (g + 1) * STRIP],
                              start=False, stop=True, skip_group_check=True)
            m.then_inc(ob_done, 1)

        def visit16(n, k):
            return n * 4 + (16 - 4 * k)


        def act_turn(act, n):
            for g in range(NG):
                act.wait_ge(turned, NG * n + g + 1)
                act.activation(XT[:, g * BANK:(g + 1) * BANK], bank[g][:, :], ACT.Copy).then_inc(xt_ready, 1)

        def act_exps(act, c, it, kcs):
            n = PAIRS * c + it
            for w in range(N2):
                s, kc, hf = UNITS2[w]
                if kc not in kcs:
                    continue
                act.wait_ge(st_done, N2 * n + w + 1)
                k = UNITS2[w - PT_RING][1]
                act.wait_ge(pv_done, PV0 + TB * n + k + 1 - (TB if w < PT_RING else 0))
                m = (hf + 1) * BANK - max(kc * P, hf * BANK)
                act.activation(PT[w % PT_RING][:, 0:m], bank[S_RING + w % S_RING][:, 0:m], ACT.Exp, scale=float(HD) ** -0.5)\
                   .then_inc(exp_done, 1)

        def act_maxrows(act, c, it, buf):
            act.wait_ge(mt_done, PAIRS * c + it + 1)
            for s in range(2):
                act.activation(QB[buf][s][MAXROW:MAXROW + MAXROWS, :],
                               bank[7][:, :].bitcast(BF16)[s * STRIP:s * STRIP + MAXROWS, :], ACT.Copy).then_inc(maxrow_ready, 1)

        def act_step(act, c, b, it, buf, left, visit):
            act_exps(act, c, it, range(1, MAX_AT + 1))
            if left >= 1:
                act_maxrows(act, c, it + 1, (buf + 1) % RING)
            act_exps(act, c, it, range(MAX_AT + 1, TB))
            n = PAIRS * c + it
            act.wait_ge(pv_done, PV0 + TB * (n + 1))
            act.wait_ge(o_turned, OTURN0 + n)
            act.activation(OT[:, :], bank[6][:, :], ACT.Copy).then_inc(ot_ready, 1)
            if left >= 1:
                act_exps(act, c, it + 1, (0,))

        def act_ffn(act, c):
            n_turn = (0, 4)[c]
            act_turn(act, n_turn)
            for n in range(9):
                if n < 8:
                    act.wait_ge(qk_done, 8 * c + n + 1)
                    blk = slice((n // 2) * BANK, (n // 2 + 1) * BANK)
                    act.activation((qparts, kparts)[n % 2][:, 0, blk], bank[4 + n % 4][:, :], ACT.Copy).then_inc(p1_done, 1)
                if n >= 1:
                    m = n - 1
                    act.wait_ge(r1_done, 8 * c + m + 1)
                    blk = slice((m // 2) * BANK, (m // 2 + 1) * BANK)
                    act.activation((qparts, kparts)[m % 2][:, 1, blk], rest[:, m % 2, :], ACT.Copy).then_inc(p2_done, 1)
            for g in range(NG):
                act.wait_ge(v_done, NG * c + g + 1)
                b, t0 = 4 * g // TB, 4 * g % TB
                for t in range(4):
                    dst = VA[:, b * (PAIRS // B):(b + 1) * (PAIRS // B), :, t0 + t, 0:HD].rearrange("p a s d -> p (a s) d")
                    m = act.activation(dst, bank[g][:, t * P:(t + 1) * P].rearrange("p (h d) -> p h d", d=HD), ACT.Copy)
                m.then_inc(va_ready, 1)
            act_maxrows(act, c, 0, 0)
            act_exps(act, c, 0, (0,))
            run_steps(act, act_step, c)
            act_turn(act, n_turn + 1)
            act_turn(act, n_turn + 2)
            act.wait_ge(lg_ready, c + 1)
            act.activation(lg[:, :, :], lg[:, :, :], ACT.Exp).then_inc(eg_ready, 1)
            for gq in range(NG):
                act.wait_ge(w8_turned, NG * c + gq + 1)
                act.activation(WT[:, gq * BANK:(gq + 1) * BANK], bank[gq][0:E, :], ACT.Copy).then_inc(wt_ready, 1)
            for gq in range(NG):
                act.wait_ge(b2_done, NG * c + gq + 1)
                act.activation(ACC[:, 4 * gq:4 * gq + 4, :], bank[4 + gq][:, :].rearrange("p (t d) -> p t d", d=D), ACT.Copy)\
                   .then_inc(acc0_ready, 1)
            with act.Fori(0, E // 2) as i:
                act_expert(act, c, i * 2, 0)
                act_expert(act, c, i * 2 + 1, 1)

        def act_expert(act, c, e, buf):
            act.activation(bias1[buf][:, :], bb1[:, :, :].rearrange("p e f -> p (e f)")[:, bass.ds(e * FC, FC)], ACT.Copy)
            act.drain()
            for tb in range(NG):
                u = E * NG * c + e * NG + tb
                act.wait_ge(y_done, Y0 + u - 1)
                for f in range(FC):
                    act.wait_ge(a_done, u * FC + f + 1)
                    act.activation(H1[tb % 2][:, f, :], bank[f][:, :], ACT.Gelu_apprx_tanh,
                                   bias=bias1[buf][:, f:f + 1]).then_inc(gelu_done, 1)

        def act_log(act, t):
            act.drain()
            act.activation(t, t, ACT.Exp, scale=-1.0)
            act.drain()
            return act.activation(t, t, ACT.Ln, bias=1.0)

        def act_sel(act):
            act_turn(act, 3)
            act.wait_ge(uqk_turned, 1)
            act.activation(UQT[:, :, :].rearrange("p a b -> p (a b)"), bank[4][:, 0:NH // 2 * DCQ], ACT.Copy).then_inc(uqk_ready, 1)
            act.activation(UKT[:, :, :].rearrange("p a b -> p (a b)"), bank[5][:, 0:NH // 2 * DC], ACT.Copy).then_inc(uqk_ready, 1)
            act.activation(UVT[:, :, :].rearrange("p a b -> p (a b)"), bank[5][:, NH // 2 * DC:NH * DC], ACT.Copy).then_inc(uqk_ready, 1)
            act.wait_ge(prep_done, 1)
            for k in range(2):
                act.activation(AQ[:, :].rearrange("p (j s c) -> p s j c", s=2, c=DC)[:, k],
                               bank[6 + k][0:DCQ, 0:NH // 2 * DC].rearrange("p (j c) -> p j c", c=DC), ACT.Copy).then_inc(prep_ready, 1)
            act.activation(MO[:, :, :].rearrange("p a d -> p (a d)"), bank[4][:, 0:NH * DC // P * D], ACT.Copy).then_inc(prep_ready, 1)
            for n in range(8):
                act.wait_ge(qi_done, n + 1)
                act.activation(QI[:, n % 2, (n // 2) * BANK:(n // 2 + 1) * BANK], bank[n][:, :], ACT.Copy).then_inc(qi_ready, 1)
            for q in range(4):
                act.wait_ge(kv_done, q + 1)
                src = bank[4 + q][:, :].rearrange("p (t n) -> p t n", n=P)[:, :, 0:2 * DR]
                act.activation(KVS[:, 4 * q:4 * q + 4, DC:ROWKV], src, ACT.Abs)
            act_log(act, KVS[:, :, DC:ROWKV]).then_inc(kv_log, 1)
            act.wait_ge(delta_loaded, 16 * 9)
            act.activation(delta_row[:, 1, 0:HALF], delta_row[:, 0, 0:HALF], ACT.Exp, scale=-1.0).then_inc(sig_ready, 1)
            act.activation(delta_col[:, 1:2], delta_col[:, 0:1], ACT.Exp, scale=-1.0).then_inc(sig_ready, 1)
            act.wait_ge(ang_ready, 2)
            act.activation(delta_row[:, 3:5, 0:HALF], delta_row[:, 1:3, 0:HALF], ACT.Sin).then_inc(trig_ready, 1)
            act.activation(delta_col[:, 3:5], delta_col[:, 1:3], ACT.Sin).then_inc(trig_ready, 1)
            for tile in range(NT):
                w = (tile % TB) * P + LW
                for h in range(NIH):
                    u = tile * NIH + h
                    act.wait_ge(si_done, u + 1)
                    if u >= 2:
                        act.wait_ge(sc_used, u - 1)
                    for half in range((w + BANK - 1) // BANK):
                        lo, hi = half * BANK, min(w, (half + 1) * BANK)
                        m = act.activation(RL[u % 2][:, lo:hi], bank[2 * (u % 3) + half][:, 0:hi - lo], ACT.Relu)
                    m.then_inc(relu_done, 1)
                if tile >= 1:
                    act_index(act, tile - 1)
            act_index(act, NT - 1)
            for n in range(4):
                act.wait_ge(cq_done, n + 1)
                act.activation(CQ[:, n * BANK:(n + 1) * BANK], bank[n][0:DCQ, :], ACT.Copy).then_inc(cq_ready, 1)
            for n in range(4):
                act.wait_ge(kt_done, n + 1)
                act.activation(ATTf[0:2 * DR, n * BANK:(n + 1) * BANK], bank[4 + n][0:2 * DR, :], ACT.Abs)
                b, t = n // 2, (n % 2) * BANK
                act.activation(KL[0:DC, b, LW + t:LW + t + BANK], bank[4 + n][2 * DR:ROWKV, :], ACT.Copy).then_inc(kt_c, 1)
            act_log(act, ATTf[0:2 * DR, :]).then_inc(kt_log, 1)
            act.wait_ge(kl_ready, 1)
            act.wait_ge(sc_used, NT * NIH)
            for n in range(2 * B):
                if n >= 2:
                    act.wait_ge(q_placed[n % 2], 16 * 12 * (n // 2))
                for half in range(2):
                    act.wait_ge(qt_done, 2 * n + half + 1)
                    act.activation(QT[n % 2][:, half * BANK:(half + 1) * BANK], bank[half][:, :], ACT.Copy).then_inc(qt_ready, 1)
                if n >= 2:
                    act.wait_ge(qr_ready, 2 * (n - 1))
                for half in range(2):
                    act.wait_ge(mu_done, 2 * n + half + 1)
                    act.activation(MU[n % 2][:, half * BANK:(half + 1) * BANK], raw_bank(n, half)[:, :], ACT.Abs)
                act_log(act, MU[n % 2]).then_inc(mu_log, 1)
            run_blocks(act, act_ahead, act_block)

        def act_index(act, tile):
            act.wait_ge(i_turned, tile + 1)
            src = bank[6][0:NSEL, 0:P].rearrange("p (g t) -> p t g", t=4)
            for t in range(4):
                act.activation(IDX[t * NSEL:(t + 1) * NSEL, tile * (P // 4):(tile + 1) * (P // 4)], src[:, t, :], ACT.Copy).then_inc(idx_ready, 1)

        def act_ahead(act, b, n, k):
            act_gt(act, n, k)

        def act_gt(act, n, k):
            act.wait_ge(s_done, C0 + n - 1)
            act.wait_ge(gt_done, n + 1)
            act.activation(GTS[k % 2][0:DC + DR].rearrange("p g n -> p (g n)"), bank[2 + k % 2][0:DC + DR, :], ACT.Copy).then_inc(gts_ready, 1)

        def act_block(act, b, n, k, early, ahead):
            act.wait_ge(tp_done, C0 + n - 1)
            act.wait_ge(sm_ready, C0 + n + 1)
            c = col[:, k % 2, :]
            act.activation(PB[k % 2], SM[k % 2], ACT.Exp, scale=SCALE2, bias=c[:, 1:2], accum_out=c[:, 2:3]).then_inc(pb_exp, 1)
            if ahead:
                act_gt(act, n + 1, (k + 1) % 4)

        def dve_norm(dve, src, dst, n, done, per):
            for t in range(NT):
                dve.bn_stats(stats[:, t, :], src[:, t, :])
            dve.drain()
            for t in range(NT):
                dve.bn_aggr(mv[:, t, :], stats[:, t, :])
            dve.drain()
            dve.tensor_scalar(vareps[:, :], mv[:, :, 1], FFN_EPS, None, ALU.add).then_inc(var_ready, 1)
            dve.wait_ge(rstd_ready, n + 1)
            for t in range(NT):
                m = dve.tensor_scalar(dst[:, t, :], src[:, t, :], mv[:, t, 0:1], rstd[:, t:t + 1], ALU.subtract, ALU.mult)
                if done is not None and t % 4 == 3:
                    m.then_inc(done, 1)

        def dve_max(dve, c, it, u):
            s, qt, hf = UNITS1[u]
            dve.wait_ge(s1_done, N1 * (PAIRS * c + it) + u + 1)
            n = min((qt + 1) * P - hf * BANK, BANK)
            dve.tensor_reduce(rowmax[:, hf, s, qt:qt + 1], bank[u % S_RING][:, 0:n], AX_X, ALU.max).then_inc(max_done, 1)

        def dve_maxrows(dve, c, it):
            parts = [MB[:, :, 0:2 * STRIP].rearrange("p t (s r) -> p s t r", s=2)[:, :, :, r] for r in range(MAXROWS)]
            top = rowmax[:, 0, :, :]
            n = PAIRS * c + it
            dve.drain()
            dve.tensor_tensor(rowmax[:, 0, :, 4:], rowmax[:, 0, :, 4:], rowmax[:, 1, :, 4:], ALU.max)
            dve.drain()
            if not isinstance(n, int) or n:
                dve.wait_ge(mt_done, n)
            dve.tensor_scalar(parts[0], top, -1.0, None, ALU.mult)
            dve.drain()
            dve.scalar_tensor_tensor(maxrest[:, :, :], top, -1.0, parts[0], ALU.mult, ALU.subtract)
            dve.drain()
            dve.tensor_copy(parts[1], maxrest[:, :, :])
            dve.drain()
            dve.tensor_tensor(parts[2], maxrest[:, :, :], parts[1], ALU.subtract).then_inc(mb_ready, 1)

        def dve_outputs(dve, c, b, it):
            dve.wait_ge(o_turned, OTURN0 + PAIRS * c + it + 1)
            o = bank[7][:, :].rearrange("p (t s h d) -> p s h t d", t=4, s=2, h=2)
            for s in range(2):
                dve.reciprocal(rsum[:, s, :, :], o[:, s, :, :, HD])
            dve.drain()
            att = ATT[:, :, :].rearrange("p t d -> p (t d)")[:, b * L:(b + 1) * L].rearrange("p (h t d) -> p h t d", h=2, d=D)
            for s in range(2):
                m = dve.tensor_tensor(att[:, :, :, bass.ds((it - b * TB) * (2 * HD) + s * HD, HD)], o[:, s, :, :, 0:HD],
                                      rsum[:, s, :, :].unsqueeze(3).broadcast_to([P, 2, 4, HD]), ALU.mult)
            m.then_inc(att_done, 1)

        def dve_step(dve, c, b, it, buf, left, visit):
            todo = ahead_units(left)
            for a, u in todo:
                dve_max(dve, c, it + a, u)
                if (a, u) == (1, N1 - 1):
                    dve_maxrows(dve, c, it + 1)
            dve_outputs(dve, c, b, it)

        def dve_expert(dve, c, e):
            for tb in range(NG):
                u = E * NG * c + e * NG + tb
                dve.drain()
                dve.wait_ge(y_done, Y0 + u + 1)
                for t in range(4):
                    tile = 4 * tb + t
                    m = dve.scalar_tensor_tensor(ACC[:, tile, :], bank[4 + tb % 2][:, t * P:(t + 1) * P],
                                                 W8[:, tile, bass.ds(e, 1)], ACC[:, tile, :], ALU.mult, ALU.add)
                m.then_inc(acc_done, 1)

        def affine(dve, t, n, done):
            for k, op in ((0, ALU.mult), (1, ALU.add)):
                dve.drain()
                for g in range(NG):
                    m = dve.tensor_tensor(t[:, 4 * g:4 * g + 4, :], t[:, 4 * g:4 * g + 4, :],
                                          gains[:, 2 * n + k, :].unsqueeze(1).broadcast_to([P, 4, D]), op)
                    if k and done is not None:
                        m.then_inc(done, 1)

        def dve_ffn(dve, c):
            ln = (0, 4)[c]
            dve_norm(dve, X, XN, ln, xn_ready, 4)
            for n in range(9):
                if n < 8:
                    blk = slice((n // 2) * BANK, (n // 2 + 1) * BANK)
                    if n >= 2:
                        dve.wait_ge(p2_done, 8 * c + n - 1)
                    dve.wait_ge(p1_done, 8 * c + n + 1)
                    dve.drain()
                    dve.tensor_tensor(rest[:, n % 2, :], bank[4 + n % 4][:, :], (qparts, kparts)[n % 2][:, 0, blk], ALU.subtract)\
                       .then_inc(r1_done, 1)
                if n >= 1:
                    m = n - 1
                    blk = slice((m // 2) * BANK, (m // 2 + 1) * BANK)
                    dve.wait_ge(p2_done, 8 * c + m + 1)
                    p = (qparts, kparts)[m % 2]
                    dve.tensor_tensor(p[:, 2, blk], rest[:, m % 2, :], p[:, 1, blk], ALU.subtract).then_inc(p3_done, 1)
            dve.wait_ge(filled, c + 1)
            for u in range(N1):
                dve_max(dve, c, 0, u)
            dve_maxrows(dve, c, 0)
            for u in range(EARLY):
                dve_max(dve, c, 1, u)
            run_steps(dve, dve_step, c)
            for gq in range(NG):
                dve.wait_ge(o_done, NG * c + gq + 1)
                dve.tensor_tensor(XN[:, 4 * gq:4 * gq + 4, :], XN[:, 4 * gq:4 * gq + 4, :],
                                  bank[4 + gq][:, :].rearrange("p (t d) -> p t d", d=D), ALU.add)
            dve.drain()
            dve_norm(dve, XN, HN, ln + 1, None, 4)
            affine(dve, HN, 0, h_ready)
            dve.wait_ge(gate_done, c + 1)
            gate = bank[4][:, 0:NT * E].rearrange("p (t e) -> p t e", e=E)

            def per_tile(k):
                return g16[:, k, :].unsqueeze(2).broadcast_to([P, NT, E])

            dve.tensor_reduce(g16[:, 0, :], gate, AX_X, ALU.max)
            dve.drain()
            dve.tensor_tensor(lg[:, :, :], gate, per_tile(0), ALU.subtract).then_inc(lg_ready, 1)
            dve.wait_ge(eg_ready, c + 1)
            dve.tensor_reduce(g16[:, 1, :], lg[:, :, :], AX_X, ALU.add)
            dve.drain()
            dve.reciprocal(g16[:, 1, :], g16[:, 1, :])
            dve.drain()
            dve.tensor_tensor(pr[:, :, :], lg[:, :, :], per_tile(1), ALU.mult)
            dve.drain()
            for t in range(NT):
                dve.max(top8[:, t, :], pr[:, t, :])
            dve.drain()
            for t in range(NT):
                dve.max_index(idx8[:, t, :], top8[:, t, :], pr[:, t, :])
            dve.tensor_tensor(g16[:, 2, :], top8[:, :, 0], top8[:, :, 1], ALU.add)
            dve.drain()
            dve.tensor_copy(idxf[:, :, :], idx8[:, :, 0:2])
            dve.reciprocal(g16[:, 2, :], g16[:, 2, :])
            dve.drain()
            for k in range(2):
                dve.tensor_tensor(oh[:, k, :, :], cst("iota8").unsqueeze(1).broadcast_to([P, NT, E]),
                                  idxf[:, :, k:k + 1].broadcast_to([P, NT, E]), ALU.is_equal)
            dve.drain()
            for k in range(2):
                dve.tensor_tensor(oh[:, k, :, :], oh[:, k, :, :], top8[:, :, k:k + 1].broadcast_to([P, NT, E]), ALU.mult)
            dve.drain()
            dve.tensor_tensor(oh[:, 0, :, :], oh[:, 0, :, :], oh[:, 1, :, :], ALU.add)
            dve.drain()
            dve.tensor_tensor(W8[:, :, :], oh[:, 0, :, :], per_tile(2), ALU.mult).then_inc(w8_ready, 1)
            dve.wait_ge(acc0_ready, NG * (c + 1))
            with dve.Fori(0, E // 2) as i:
                dve_expert(dve, c, i * 2)
                dve_expert(dve, c, i * 2 + 1)
            dve.drain()
            for gq in range(NG):
                s = slice(4 * gq, 4 * gq + 4)
                dve.tensor_tensor(HN[:, s, :], HN[:, s, :], ACC[:, s, :], ALU.add)
            dve.drain()
            dve_norm(dve, HN, XN, ln + 2, None, 4)
            affine(dve, XN, 1, None)
            dve.drain()
            dve.scalar_tensor_tensor(X[:, :, :], XN[:, :, :], 0.5, X[:, :, :], ALU.mult, ALU.add).then_inc(x_ready, 1)
            dve.drain()

        def dve_sel(dve):
            dve_norm(dve, X, XN, 3, xn_ready, 4)
            dve.wait_ge(sel_w_loaded, 16 * 11)
            for n in range(4):
                dve.wait_ge(ki_done, n + 1)
                dve.tensor_copy(KI[:, n * BANK:(n + 1) * BANK], bank[n][:, :]).then_inc(ki_ready, 1)
            for q in range(4):
                dve.wait_ge(kv_log, 1)
                src = bank[4 + q][:, :].rearrange("p (t n) -> p t n", n=P)
                rows = KVS[:, 4 * q:4 * q + 4, :]
                dve.tensor_copy(rows[:, :, 0:DC], src[:, :, 2 * DR:ROWKV])
                dve.scalar_tensor_tensor(rows[:, :, DC:ROWKV], src[:, :, 0:2 * DR], 0.0, rows[:, :, DC:ROWKV], ALU.max, ALU.add)\
                   .then_inc(kv_ready, 1)
            dve.wait_ge(sig_ready, 2)
            dr, dc = delta_row, delta_col
            for d, at_ in ((dr, lambda k: dr[:, k, 0:HALF]), (dc, lambda k: dc[:, k:k + 1])):
                dve.tensor_scalar(at_(2), at_(1), 1.0, None, ALU.add)
                dve.drain()
                dve.reciprocal(at_(5), at_(2))
                dve.drain()
                dve.tensor_scalar(at_(1), at_(5), -2.0 * np.pi, np.pi, ALU.mult, ALU.add)
                dve.drain()
                dve.tensor_scalar(at_(1), at_(1), 3.1415925, -3.1415925, ALU.min, ALU.max)
                dve.tensor_scalar(at_(2), at_(5), -np.pi, None, ALU.mult).then_inc(ang_ready, 1)
            dve.wait_ge(trig_ready, 2)
            for d, at_ in ((dr, lambda k: dr[:, k, 0:HALF]), (dc, lambda k: dc[:, k:k + 1])):
                dve.tensor_tensor(at_(0), at_(4), at_(4), ALU.mult)
                dve.tensor_scalar(at_(1), at_(3), -1.0, None, ALU.mult)
                dve.drain()
                dve.tensor_scalar(at_(0), at_(0), -2.0, 1.0, ALU.mult, ALU.add)
                dve.drain()
            dve.tensor_tensor(dc[:, 1:2], dc[:, 1:2], cst("sign"), ALU.mult)
            for k in range(2):
                dve.tensor_copy(dr[:, k, HALF:DR], dr[:, k, 0:HALF])
            dve.drain()
            dve.tensor_scalar(dc[:, 2:3], dc[:, 1:2], -1.0, None, ALU.mult)
            dve.tensor_tensor(dr[:, 1, :], dr[:, 1, :], cst("sign_row"), ALU.mult)
            dve.drain()
            dve.tensor_tensor(rot_sel[:, 0:DR], cst("cos_sel"), dr[:, 0, :], ALU.mult)
            dve.tensor_tensor(dr[:, 2, :], cst("sin_sel"), dr[:, 1, :], ALU.mult)
            dve.tensor_tensor(rot_sel[:, DR:], cst("sin_sel"), dr[:, 0, :], ALU.mult)
            dve.tensor_tensor(dr[:, 3, :], cst("cos_sel"), dr[:, 1, :], ALU.mult)
            dve.drain()
            dve.tensor_tensor(rot_sel[:, 0:DR], rot_sel[:, 0:DR], dr[:, 2, :], ALU.subtract)
            dve.tensor_tensor(rot_sel[:, DR:], rot_sel[:, DR:], dr[:, 3, :], ALU.add)
            for tile in range(NT):
                dve_select(dve, tile)
            dve.wait_ge(rot_loaded, 16)
            for k in range(2):
                co, si = ROT[:, 2 * k, :], ROT[:, 2 * k + 1, :]
                dve.tensor_scalar(QRD[0], si, dc[:, 2:3], None, ALU.mult)
                dve.tensor_scalar(T1, co, dc[:, 1:2], None, ALU.mult)
                dve.drain()
                dve.scalar_tensor_tensor(co, co, dc[:, 0:1], QRD[0], ALU.mult, ALU.add)
                dve.scalar_tensor_tensor(si, si, dc[:, 0:1], T1, ALU.mult, ALU.add)
                dve.drain()
            for g in range(2):
                dve.memset(GTS[g][DC + DR:ROWKV], 0.0)
            dve.memset(KL[DC:DC + DR, :, :], 0.0)
            for n in range(4):
                b, t = n // 2, slice((n % 2) * BANK, (n % 2 + 1) * BANK)
                dve.wait_ge(kt_log, 1)
                m = ATTf[0:2 * DR, n * BANK:(n + 1) * BANK]
                dve.scalar_tensor_tensor(m, bank[4 + n][0:2 * DR, :], 0.0, m, ALU.max, ALU.add)
                dve.drain()
                dve.tensor_tensor(QRD[0][0:DR, t], m[0:DR], ROT[0:DR, 0, t], ALU.mult)
                dve.tensor_tensor(QRL[0][0:DR, t], m[DR:2 * DR], ROT[DR:2 * DR, 1, t], ALU.mult)
                dve.drain()
                dve.tensor_tensor(KL[DC + DR:, b, LW + (n % 2) * BANK:LW + (n % 2 + 1) * BANK], QRD[0][0:DR, t], QRL[0][0:DR, t], ALU.add)
            dve.wait_ge(kt_c, 4)
            dve.drain()
            dve.tensor_copy(KL[:, :, 0:LW], KL[:, :, LW:2 * LW])
            m = dve.tensor_copy(KL[:, :, LW + L:LP], KL[:, :, LW:LW + LP - L - LW])
            m.then_inc(kl_ready, 1)
            for n in range(2 * B):
                halves = [slice(half * BANK, (half + 1) * BANK) for half in range(2)]
                dve.wait_ge(mu_log, n + 1)
                for half in range(2):
                    m = MU[n % 2][:, halves[half]]
                    dve.scalar_tensor_tensor(m, raw_bank(n, half)[:, :], 0.0, m, ALU.max, ALU.add).then_inc(mu_ready, 1)
                dve.drain()
                if n >= 2:
                    dve.wait_ge(q_placed[n % 2], 16 * 12 * (n // 2))
                for k, dst in ((0, QRD[n % 2]), (1, QRL[n % 2])):
                    dve.tensor_tensor(dst, MU[n % 2], ROT[:, 2 * k, :], ALU.mult)
                    for half in range(2):
                        dve.wait_ge(mus_done, 2 * n + half + 1)
                        dve.tensor_tensor(T1[:, halves[half]], bank[4 + half][:, :], ROT[:, 2 * k + 1, halves[half]], ALU.mult)
                    dve.drain()
                    dve.tensor_tensor(dst, dst, T1, ALU.add).then_inc(qr_ready, 1)
                    dve.drain()
            for i in range(2):
                dve.wait_ge(q_placed[i], 16 * 12 * B)
            run_blocks(dve, dve_ahead, dve_block)
            for gq in range(NG):
                dve.wait_ge(mix_done, gq + 1)
                m = dve.tensor_tensor(X[:, 4 * gq:4 * gq + 4, :], X[:, 4 * gq:4 * gq + 4, :],
                                      bank[gq][:, :].rearrange("p (t d) -> p t d", d=D), ALU.add)
            m.then_inc(x_ready, 1)
            dve.drain()

        def dve_select(dve, tile):
            b, tt = tile // TB, tile % TB
            w = tt * P + LW
            for h in range(NIH):
                u = tile * NIH + h
                dve.wait_ge(relu_done, u + 1)
                dve.drain()
                if h == 0:
                    dve.tensor_scalar(SC[:, 0:w], RL[u % 2][:, 0:w], idx_w[:, h:h + 1], None, ALU.mult).then_inc(sc_used, 1)
                else:
                    dve.scalar_tensor_tensor(SC[:, 0:w], RL[u % 2][:, 0:w], idx_w[:, h:h + 1], SC[:, 0:w], ALU.mult, ALU.add)\
                       .then_inc(sc_used, 1)
            dve.drain()
            edge = min(w, P)
            dve.tensor_tensor(SC[:, w - edge:w], SC[:, w - edge:w], cst("nonlocal")[:, P - edge:P], ALU.min)
            for r in range(NSEL // 8):
                dve.drain()
                dve.max(best[:, r, :], SC[:, 0:w])
                dve.drain()
                dve.max_index(bidx[:, r, :], best[:, r, :], SC[:, 0:w])
                if r < NSEL // 8 - 1:
                    dve.match_replace(SC[:, 0:w], best[:, r, :], SC[:, 0:w], -3.3e38)
            dve.drain()
            f = bidf[:, tile % 2, :]
            if tile >= 2:
                dve.wait_ge(i_turned, tile - 1)
            dve.tensor_copy(f, bidx.rearrange("p r k -> p (r k)"))
            dve.drain()
            if tt == 0:
                dve.tensor_tensor(f, f, cst("keep"), ALU.mult)
                dve.drain()
                dve.tensor_tensor(f, f, cst("fill"), ALU.add)
                dve.drain()
            dve.tensor_scalar(f, f, float(b * LP + LW), None, ALU.add).then_inc(best_ready, 1)

        def dve_queries(dve, n, k):
            src = QALL[:, :, bass.ds(n * BT, BT)].rearrange("p h (g t) -> p g h t", t=4)
            dve.wait_ge(s_done, C0 + n - 1)
            dve.tensor_scalar(QS[k % 2].rearrange("p (g h t) -> p g h t", g=GB, h=NH), src, 1.0, None, ALU.mult).then_inc(qs_ready, 1)

        def dve_attended(dve, n, k):
            dst = OA[:, :, bass.ds(n * BT, BT)].rearrange("p h (g t) -> p g h t", t=4)
            dve.wait_ge(ob_done, C0 + n + 1)
            dve.tensor_scalar(dst, bank[6 + k % 2][0:DC, 0:P].rearrange("p (g h t) -> p g h t", g=GB, h=NH), 1.0, None, ALU.mult)\
               .then_inc(oa_ready, 1)

        def dve_ahead(dve, b, n, k):
            dve_queries(dve, n, k)
            dve_rotate(dve, n, k)

        def dve_rotate(dve, n, k):
            dve.drain()
            dve.wait_ge(gathered[k], 4 * visit16(n, k))
            dve.tensor_tensor(PRD, G[k][:, :, DC:], rot_sel[:, :].unsqueeze(1).broadcast_to([P, GB, 2 * DR]), ALU.mult)
            dve.drain()
            dve.tensor_tensor(G[k][:, :, DC:DC + DR], PRD[:, :, 0:DR], PRD[:, :, DR:], ALU.add).then_inc(rot_done, 1)

        def dve_block(dve, b, n, k, early, ahead):
            c = col[:, k % 2, :]
            if ahead:
                dve_queries(dve, n + 1, (k + 1) % 4)
            dve.wait_ge(pb_exp, C0 + n - 1)
            dve.wait_ge(s_done, C0 + n + 1)
            dve.memset(c[:, 3:4], 0.0)
            dve.tensor_tensor_reduce(SM[k % 2], bank[k % 2][:, 0:2 * P], cst("mask_early" if early else "mask_main"), 1.0, -3e38,
                                     ALU.add, ALU.max, c[:, 0:1])
            dve.drain()
            dve.tensor_scalar(c[:, 1:2], c[:, 0:1], -SCALE2, None, ALU.mult).then_inc(sm_ready, 1)
            if not (early and k == 0):
                dve_attended(dve, n - 1, (k + 3) % 4)
            if ahead:
                dve_rotate(dve, n + 1, (k + 1) % 4)
            dve.wait_ge(pb_exp, C0 + n + 1)
            dve.reciprocal(c[:, 3:4], c[:, 2:3])
            dve.drain()
            dve.tensor_scalar(PB[k % 2], PB[k % 2], c[:, 3:4], None, ALU.mult).then_inc(pn_ready, 1)
            dve.wait_ge(ob_done, C0 + n - 1)
            dve.wait_ge(tp_done, C0 + n + 1)
            dve.tensor_copy(PTS[k % 2], bank[4 + k % 2][:, 0:2 * P]).then_inc(pts_ready, 1)
            if not ahead:
                dve_attended(dve, n, k)

        @block.sync
        def _(sp):
            sp.dma_start(X[:, :, :], attn["x"].rearrange("b (t p) d -> p (b t) d", p=P)).then_inc(x_loaded, 16)
            sp_ffn(sp, 0)
            sp_sel(sp)
            sp_ffn(sp, 1)
            sp.wait_ge(x_ready, 3)
            sp.dma_start(out.rearrange("b (t p) d -> p (b t) d", p=P), X[:, :, :]).then_inc(stored, 16)
            sp.wait_ge(stored, 16)

        @block.gpsimd
        def _(pool):
            pool.memset(neghalf[:, :], -0.5)
            pool.memset(spare[:, 0:1], 0.0).then_inc(setup_done, 1)
            pool_ffn(pool, 0)
            pool_sel(pool)
            pool_ffn(pool, 1)

        @block.tensor
        def _(pe):
            pe.wait_ge(const_loaded, 16)
            pe.wait_ge(setup_done, 2)
            pe.wait_ge(w_loaded, 16 * 9)
            pe_ffn(pe, 0)
            pe_sel(pe)
            pe_ffn(pe, 1)

        @block.scalar
        def _(act):
            act.dma_start(const[:, :], const_ap).then_inc(const_loaded, 16)
            for dst, src in ((w_qkv[:, :], ffn["w_qkv"]), (w_o[:, :], ffn["w_o"]), (wg[:, :], ffn["wg"]),
                             (gains[:, 0, :], ffn["g1"].partition_broadcast(P)), (gains[:, 1, :], ffn["b1"].partition_broadcast(P)),
                             (gains[:, 2, :], ffn["g2"].partition_broadcast(P)), (gains[:, 3, :], ffn["b2"].partition_broadcast(P)),
                             (bb2[:, :], ffn["bb2"])):
                act.dma_start(dst, src).then_inc(w_loaded, 16)
            act.dma_start(bb1[:, :, :], ffn["bb1"].rearrange("e (f p) -> p e f", p=P), allow_slow_non_contiguous=True).then_inc(w_loaded, 16)
            for dst, src in ((WKV[:, 0:DR], attn["W_kr"]), (WKV[:, DR:DR + HALF], attn["W_kr"][:, HALF:]),
                             (WKV[:, DR + HALF:2 * DR], attn["W_kr"][:, 0:HALF]), (WKV[:, 2 * DR:], attn["W_dkv"]),
                             (WIQ[:, :], attn["idx_wq"]), (WIK[:, 0:DH], attn["idx_wk"]), (WIK[:, DH:], attn["idx_wk"]),
                             (WDQ[:, :], attn["W_dq"]), (WQR[:, :], attn["W_qr"]),
                             (idx_w[:, :], attn["idx_w"].partition_broadcast(P))):
                act.dma_start(dst, src).then_inc(sel_w_loaded, 16)
            act.dma_start(WOUT[:, :, :], attn["W_out"].rearrange("(j p) d -> p j d", p=P)).then_inc(sel_w_loaded, 16)
            act.dma_start(delta_row[:, 0, 0:HALF], attn["raw_delta"].partition_broadcast(P)).then_inc(delta_loaded, 16)
            for x in range(P // HALF):
                act.dma_start(delta_col[x * HALF:(x + 1) * HALF, 0:1], attn["raw_delta"].rearrange("(i a) -> i a", a=1)).then_inc(delta_loaded, 16)
            act.wait_ge(setup_done, 1)
            act.activation(spare[:, 1:2], spare[:, 0:1], ACT.Copy).then_inc(exp_done, EXP0)
            act.activation(spare[:, 2:3], spare[:, 0:1], ACT.Copy).then_inc(gelu_done, GELU0)
            act_ffn(act, 0)
            act_sel(act)
            act_ffn(act, 1)

        @block.vector
        def _(dve):
            dve.wait_ge(const_loaded, 16)
            dve.wait_ge(w_loaded, 16 * 9)
            dve.wait_ge(setup_done, 1)
            dve.tensor_copy(ident_b[:, :], ident)
            dve.tensor_copy(mask_qk[:, :], cst("mask_qk"))
            dve.tensor_copy(mask_kq[:, :], cst("mask_kq")).then_inc(setup_done, 1)
            dve.memset(spare[:, 4:5], 0.0).then_inc(pv_done, PV0)
            dve.memset(spare[:, 5:6], 0.0).then_inc(o_turned, OTURN0)
            dve.memset(spare[:, 18:19], 0.0).then_inc(ot_ready, OT0)
            dve.memset(spare[:, 6:7], 0.0).then_inc(att_done, ATT0)
            dve.memset(spare[:, 7:8], 0.0).then_inc(y_done, Y0)
            dve.memset(spare[:, 8:9], 0.0).then_inc(acc_done, ACC0)
            dve.memset(spare[:, 9:10], 0.0).then_inc(max_done, MAX0)
            for x in range(8):
                m = (s_done, sm_ready, gts_ready, pb_exp, tp_done, pts_ready, ob_done, oa_ready)[x]
                dve.memset(spare[:, 10 + x:11 + x], 0.0).then_inc(m, C0)
            dve.wait_ge(x_loaded, 16)
            dve_ffn(dve, 0)
            dve_sel(dve)
            dve_ffn(dve, 1)


_INS = ["L0_attn_x", "L0_attn_W_dkv", "L0_attn_W_uk", "L0_attn_W_uv", "L0_attn_W_dq", "L0_attn_W_uq", "L0_attn_W_qr",
        "L0_attn_W_kr", "L0_attn_W_out", "L0_attn_idx_wq", "L0_attn_idx_wk", "L0_attn_idx_w", "L0_attn_raw_delta",
        "L0_ffn_w_qkv", "L0_ffn_w_o", "L0_ffn_g1", "L0_ffn_b1", "L0_ffn_wg", "L0_ffn_w1", "L0_ffn_bb1", "L0_ffn_w2",
        "L0_ffn_bb2", "L0_ffn_g2", "L0_ffn_b2"]


def kernel(**inputs):
    import concourse.bacc as bacc
    from concourse.bass_utils import run_bass_kernel_spmd

    nc = bacc.Bacc("TRN2", target_bir_lowering=False, num_devices=1)
    arrays, aps = {}, {}
    for name in _INS:
        a = np.ascontiguousarray(inputs[name])
        arrays[f"in_{name}"] = a
        aps[name] = nc.dram_tensor(f"in_{name}", a.shape, mybir.dt.from_np(a.dtype), kind="ExternalInput").ap()
    table = np.ascontiguousarray(np.concatenate(list(constants().values()), axis=1))
    arrays["in_constants"] = table
    const_ap = nc.dram_tensor("in_constants", table.shape, F32, kind="ExternalInput").ap()
    out = nc.dram_tensor("out_x", (B, L, D), F32, kind="ExternalOutput").ap()
    turns = rotations()
    arrays["in_rotations"] = turns
    rot_ap = nc.dram_tensor("in_rotations", turns.shape, F32, kind="ExternalInput").ap()
    build(nc, aps, const_ap, rot_ap, out)
    r = run_bass_kernel_spmd(nc, [arrays], core_ids=[0])
    return r.results[0]["out_x"]
```

```python
from contextlib import ExitStack

import numpy as np

import concourse.bass as bass
from concourse import mybir

F32 = mybir.dt.float32
BF16 = mybir.dt.bfloat16
F32R = mybir.dt.float32r
U32 = mybir.dt.uint32
ALU = mybir.AluOpType
ACT = mybir.ActivationFunctionType
AX_X = mybir.AxisListType.X

P = 128
B, L, D = 2, 1024, 128
TOK = B * L
NT = TOK // P
TB = L // P
BANK = 512
NG = TOK // BANK

H, HD = 16, 8
PAIRS = B * H // 2
E, F = 8, 512
FC = F // P
FFN_EPS = 1e-5
NEG = -1.0e30
NPROD = 3 * 3
STRIP = 32
ROWS = NPROD * HD
MAXROW = 96
MAXROWS = 3
RING = 4

NH, DH, DC, DCQ, DR = 8, 64, 32, 64, 32
NIH = 4
LW, KTS = 64, 96
NSEL = KTS - LW
HALF = DR // 2
BT = 16
NB = L // BT
G_RING = 8
GB = BT // 4
LP = L + P - BT
ROWKV = DC + 2 * DR
SCALE2 = float((DH + DR) ** -0.5)

PT_RING = 8
S_RING = 3
UNITS1 = [(s, t, hf) for t in range(TB) for s in range(2) for hf in range(2) if hf * BANK < (t + 1) * P]
UNITS2 = [(s, kc, hf) for kc in range(TB) for hf in range(2) for s in range(2) if (hf + 1) * BANK > kc * P]
N1, N2 = len(UNITS1), len(UNITS2)
MAX_AT = 5
ROW_LOADS = 16 * (2 * 2 * 3 + 1)
EARLY = N1 // 2

ARENA = 136 * 1024


def constants():
    f = np.float32
    q, k = np.arange(P)[:, None], np.arange(P)[None, :]
    sel = LW + np.arange(NSEL)[None, :]
    override = sel > q
    g, h, t = (a.reshape(-1, 1) for a in np.meshgrid(np.arange(GB), np.arange(NH), np.arange(4), indexing="ij"))
    tok = 4 * g + t
    early, main = k < LW, (k >= tok + 1) & (k <= tok + LW)
    own = (k // NSEL) == t
    theta = (1.0 / f(10000.0) ** (f(2.0) * np.arange(HALF, dtype=f) / f(DR))).astype(f).astype(np.float64)
    a_sel = (LW + np.arange(P) % NSEL)[:, None] * theta[None, :]
    sign = np.where(np.arange(P) % DR < HALF, -1.0, 1.0)[:, None]
    c = {"ident": np.eye(P),
         "mask_qk": np.where(k > q, NEG, 0.0),
         "mask_kq": np.where(q > k, NEG, 0.0),
         "iota8": np.broadcast_to(np.arange(E), (P, E)),
         "nonlocal": np.where(k <= q, 3e38, -3e38),
         "keep": np.where(override, 0.0, 1.0),
         "fill": np.where(override, np.broadcast_to(sel, (P, NSEL)), 0.0),
         "mask_early": np.where(np.concatenate([np.broadcast_to(early, (P, P)), own], 1), 0.0, NEG),
         "mask_main": np.where(np.concatenate([main, own], 1), 0.0, NEG),
         "cos_sel": np.concatenate([np.cos(a_sel)] * 2, 1),
         "sin_sel": np.concatenate([-np.sin(a_sel), np.sin(a_sel)], 1),
         "sign_row": np.broadcast_to(sign[:DR].T, (P, DR)),
         "swap": np.eye(P)[np.arange(P) ^ HALF],
         "sign": sign}
    return {n: np.ascontiguousarray(v.astype(f)) for n, v in c.items()}


def rotations():
    theta = (1.0 / np.float32(10000.0) ** (np.float32(2.0) * np.arange(HALF, dtype=np.float32) / np.float32(DR))).astype(np.float32)
    th = np.tile(theta.astype(np.float64), P // HALF)[:, None]
    t = np.arange(L)
    sign = np.where(np.arange(P) % DR < HALF, -1.0, 1.0)[:, None]
    tabs = []
    for pos in (t, np.where(t < LW, t, 2 * t - (LW - 1))):
        a = pos[None, :] * th
        tabs += [np.cos(a), sign * np.sin(a)]
    return np.ascontiguousarray(np.stack(tabs, 1).astype(np.float32))


def const_layout():
    at, off = {}, 0
    for n, v in constants().items():
        at[n] = (off, v.shape[1])
        off += v.shape[1]
    return at, off


def build(nc, ins, const_ap, rot_ap, out):
    at, width = const_layout()
    ffn = {n[7:]: a for n, a in ins.items() if n.startswith("L0_ffn_")}
    attn = {n[8:]: a for n, a in ins.items() if n.startswith("L0_attn_")}
    q_rows = nc.dram_tensor("q_rows", (PAIRS, 2, HD, 3, L), BF16, kind="Internal").ap()
    k_rows = nc.dram_tensor("k_rows", (PAIRS, 2, HD, 3, L), BF16, kind="Internal").ap()
    wt_rows = nc.dram_tensor("wt_rows", (E, TOK), F32, kind="Internal").ap()
    kv_rows = nc.dram_tensor("kv_rows", (B * LP, ROWKV), F32, kind="Internal").ap()

    with ExitStack() as ctx:
        def sb(name, shape, dt=F32):
            return ctx.enter_context(nc.sbuf_tensor(name, shape, dt))

        def sem(name):
            return ctx.enter_context(nc.semaphore(name))

        bank = [ctx.enter_context(nc.psum_tensor(f"bank{i}", [P, BANK], F32)) for i in range(8)]

        const = sb("const", [P, width])

        def cst(name):
            o, n = at[name]
            return const[:, o:o + n]

        ident = cst("ident")
        ident_b = sb("ident_b", [P, P], BF16)
        mask_qk = sb("mask_qk_b", [P, P], BF16)
        mask_kq = sb("mask_kq_b", [P, P], BF16)

        X = sb("X", [P, NT, D])
        XN = sb("XN", [P, NT, D])
        XT = sb("XT", [P, TOK])
        ATT = sb("ATT", [P, NT, D])
        ACC = ATT[:, :, :].rearrange("p t d -> p (t d)")
        HN = sb("HN", [P, NT, D])
        stats = sb("stats", [P, NT, 6])
        mv = sb("mv", [P, NT, 2])
        vareps = sb("vareps", [P, NT])
        rstd = sb("rstd", [P, NT])
        neghalf = sb("neghalf", [P, NT])

        w_qkv = sb("w_qkv", [P, 3 * D])
        w_o = sb("w_o", [P, D])
        wg = sb("wg", [P, E])
        gains = sb("gains", [P, 4, D])
        gain_col = sb("gain_col", [P, 2])
        bb1 = sb("bb1", [P, E, FC])
        bb2 = sb("bb2", [E, D])

        bias1 = [sb(f"bias1_{i}", [P, FC]) for i in range(2)]
        WKV = sb("WKV", [P, 2 * DR + DC])
        WIQ = sb("WIQ", [P, NIH * DH])
        WIK = sb("WIK", [P, 2 * DH])
        WDQ = sb("WDQ", [P, DCQ])
        WQR = sb("WQR", [DCQ, NH * DR])
        AQ = sb("AQ", [DCQ, NH * DC])
        MO = sb("MO", [P, NH * DC // P, D])
        UQT = sb("UQT", [P, NH // 2, DCQ])
        UKT = sb("UKT", [P, NH // 2, DC])
        UVT = sb("UVT", [P, NH // 2, DC])
        WOUT = sb("WOUT", [P, NH // 2, D])
        idx_w = sb("idx_w", [P, NIH])
        delta_col = sb("delta_col", [P, 6])
        delta_row = sb("delta_row", [P, 6, DR])
        rot_sel = sb("rot_sel", [P, 2 * DR])

        G2 = sb("G2", [P, G_RING - 4, GB, ROWKV])
        arena_at = -(-nc.sbuf_base // 32) * 32
        arena = sb("arena", [P, ARENA // 4])
        views = {}

        def view(part, shape, dt=F32, rows=P):
            n = int(np.prod(shape)) * (2 if dt == BF16 else 4) // 4
            off = views.get(part, 0)
            views[part] = off + n
            assert off + n <= ARENA // 4, (part, off + n)
            if dt == F32R:
                return nc.alloc_sbuf_tensor_at(f"{part}_{off}", [rows] + list(shape), dt, offset=arena_at + 4 * off)
            v = arena[0:rows, off:off + n]
            v = v if dt == F32 else v.bitcast(dt)
            if len(shape) == 1:
                return v
            names = "abcd"[:len(shape)]
            sizes = {x: m for x, m in zip(names, shape)}
            return v.rearrange(f"p ({' '.join(names)}) -> p {' '.join(names)}", **sizes)

        views["experts"] = views.get("ffn", 0)
        qparts = view("ffn", (3, TOK), BF16)
        kparts = view("ffn", (3, TOK), BF16)
        H1 = [view("experts", (FC, BANK)) for i in range(2)]
        H1R = [[view("experts", (FC, BANK), F32R) for part in range(2)] for i in range(2)]
        XR = [view("experts", (TOK,), F32R) for part in range(2)]
        W1R = [[view("experts", (F,), F32R) for part in range(2)] for i in range(2)]
        W2R = [[view("experts", (FC, D), F32R) for part in range(2)] for i in range(2)]
        WT = view("experts", (TOK,), rows=E)
        WB = [view("experts", (TOK,)) for i in range(2)]
        YW = [view("experts", (BANK,)) for i in range(2)]
        rest = view("ffn", (2, BANK))
        VA = view("ffn", (PAIRS, 2, TB, STRIP))
        QB = [[view("ffn", (L,), BF16) for h in range(2)] for i in range(RING)]
        KB = [[view("ffn", (L,), BF16) for h in range(2)] for i in range(RING)]
        VS = [view("ffn", (2, TB, STRIP)) for i in range(RING)]
        OT = view("ffn", (BANK,))
        PT = [view("ffn", (BANK,)) for i in range(PT_RING)]
        rowmax = view("ffn", (2, 2, TB))
        maxrest = view("ffn", (2, TB))
        MB = view("ffn", (TB, P), BF16)
        rsum = view("ffn", (2, 2, 4))
        assert views["experts"] <= views["ffn"]
        W1 = [view("ffn", (F,)) for i in range(2)]
        W2 = [view("ffn", (FC, D)) for i in range(2)]

        QALL_all = view("sel", (NH, TOK))
        QALL = QALL_all[0:96]
        OA = QALL[0:DC]
        RAW = QALL.rearrange("p h t -> p (h t)")
        KL = view("sel", (B, LP), rows=96)
        KVS = view("sel", (NT, ROWKV))
        G = [view("sel", (GB, ROWKV)) for i in range(4)] + [G2[:, i] for i in range(4)]
        views["queries"] = views["sel"]
        QS = [view("sel", (P,), rows=96) for i in range(2)]
        GTS = [view("sel", (GB, P), rows=ROWKV) for i in range(2)]
        PRD = view("sel", (GB, 2 * DR))
        SM = [view("sel", (2 * P,)) for i in range(2)]
        PB = [view("sel", (2 * P,)) for i in range(2)]
        PTS = [view("sel", (2 * P,)) for i in range(2)]
        VW = [view("sel", (DC,)) for i in range(4)]
        IDX = view("sel", (NT * P // 4,)).bitcast(U32)
        col = view("sel", (2, 4))
        SC = view("sel", (L,))
        RL = [view("sel", (L,)) for i in range(2)]
        best = view("sel", (4, 8))
        bidx = view("sel", (4, 8)).bitcast(U32)
        bidf = view("sel", (2, NSEL))
        views["sel2"] = views["sel"]
        QI = view("sel", (2, TOK))
        KI = view("sel", (TOK,))
        views["sel3"] = views["sel2"]
        GE = [view("sel3", (GB, ROWKV)) for i in range(4)]
        OAX = view("sel3", (NH * DC // P, TOK))
        assert views["sel3"] <= views["sel"]
        ROT = QALL_all[:, NH // 2:, L:]
        CQ = QALL_all[0:DCQ, NH // 2:NH // 2 + 2, 0:L]
        ATTf = ATT[:, :, :].rearrange("p t d -> p (t d)")
        HNf = HN[:, :, :].rearrange("p t d -> p (t d)")
        XNf = XN[:, :, :].rearrange("p t d -> p (t d)")
        MU, QRD, QRL = ([t[:, i * L:(i + 1) * L] for i in range(2)] for t in (ATTf, HNf, XNf))
        QT = [view("queries", (L,)) for i in range(2)]
        assert views["queries"] <= views["sel"]
        SCORES = [SC, QT[1]]
        T1 = SC
        lg = sb("lg", [P, NT, E])
        pr = sb("pr", [P, NT, E])
        top8 = sb("top8", [P, NT, 8])
        idx8 = sb("idx8", [P, NT, 8], U32)
        idxf = sb("idxf", [P, NT, 2])
        g16 = sb("g16", [P, 4, NT])
        oh = sb("oh", [P, 2, NT, E])
        W8 = sb("W8", [P, NT, E])
        IB = [sb(f"IB{i}", [P, P // 4], U32) for i in range(2)]
        turn = sb("turn", [P, 2, P // BT])
        spare = sb("spare", [P, 20])

        x_loaded, const_loaded, w_loaded, bb1_loaded, sel_w_loaded = (sem(n) for n in ("x_loaded", "const_loaded", "w_loaded", "bb1_loaded", "sel_w_loaded"))
        setup_done, filled, masks_ready = sem("setup_done"), sem("filled"), sem("masks_ready")
        var_ready, rstd_ready = sem("var_ready"), sem("rstd_ready")
        xn_ready, h_ready = sem("xn_ready"), sem("h_ready")
        turned, xt_ready = sem("turned"), sem("xt_ready")
        qk_done, p1_done, r1_done, p2_done, p3_done = (sem(n) for n in ("qk_done", "p1_done", "r1_done", "p2_done", "p3_done"))
        v_done, va_ready = sem("v_done"), sem("va_ready")
        rows_spilled = [sem(f"rows_spilled{b}") for b in range(B)]
        rows_loaded = [sem(f"rows_loaded{i}") for i in range(RING)]
        s1_done, max_done, mb_ready, mt_done, maxrow_ready = (sem(n) for n in ("s1_done", "max_done", "mb_ready", "mt_done", "maxrow_ready"))
        st_done, exp_done, pv_done, ot_ready, o_turned, att_done = (sem(n) for n in ("st_done", "exp_done", "pv_done", "ot_ready", "o_turned", "att_done"))
        o_done, gate_done, lg_ready, eg_ready, w8_ready = (sem(n) for n in ("o_done", "gate_done", "lg_ready", "eg_ready", "w8_ready"))
        w8_turned, wt_ready, b2_done, acc0_ready = (sem(n) for n in ("w8_turned", "wt_ready", "b2_done", "acc0_ready"))
        a_done, gelu_done, y_done, acc_done = (sem(n) for n in ("a_done", "gelu_done", "y_done", "acc_done"))
        xr1_ready, xr2_ready, split_done, hr2_done, sum_ready, sum_turned = (sem(n) for n in ("xr1_ready", "xr2_ready", "split_done", "hr2_done", "sum_ready", "sum_turned"))
        wt_stored = sem("wt_stored")
        wb_loaded = [sem(f"wb_loaded{i}") for i in range(2)]
        ew_loaded = [sem(f"ew_loaded{i}") for i in range(2)]
        x_ready = sem("x_ready")
        stored = sem("stored")
        raw_loaded, uqk_turned, uqk_ready, prep_done, prep_ready = (sem(n) for n in ("raw_loaded", "uqk_turned", "uqk_ready", "prep_done", "prep_ready"))
        delta_loaded, sig_ready, ang_ready, trig_ready = (sem(n) for n in ("delta_loaded", "sig_ready", "ang_ready", "trig_ready"))
        qi_done, qi_ready, ki_done, ki_ready = (sem(n) for n in ("qi_done", "qi_ready", "ki_done", "ki_ready"))
        kv_done, kv_log, kv_ready, kv_stored = (sem(n) for n in ("kv_done", "kv_log", "kv_ready", "kv_stored"))
        si_done, relu_done, sc_used, best_ready, i_turned, idx_ready = (sem(n) for n in ("si_done", "relu_done", "sc_used", "best_ready", "i_turned", "idx_ready"))
        rot_loaded, cq_done, cq_ready = (sem(n) for n in ("rot_loaded", "cq_done", "cq_ready"))
        kt_done, kt_c, kl_ready = (sem(n) for n in ("kt_done", "kt_c", "kl_ready"))
        qt_done, qt_ready, mu_done, mu_log, mu_ready = (sem(n) for n in ("qt_done", "qt_ready", "mu_done", "mu_log", "mu_ready"))
        mus_done, qr_ready = sem("mus_done"), sem("qr_ready")
        q_placed = [sem(f"q_placed{i}") for i in range(2)]
        vw_loaded = [sem(f"vw_loaded{i}") for i in range(4)]
        gathered = [sem(f"gathered{i}") for i in range(G_RING)]
        same_loaded = [sem(f"same_loaded{i}") for i in range(4)]
        staged = sem("staged")
        qs_ready, rot_done, gt_done, gts_ready, s_done, sm_ready = (sem(n) for n in ("qs_ready", "rot_done", "gt_done", "gts_ready", "s_done", "sm_ready"))
        pb_exp, pn_ready, tp_done, pts_ready, ob_done, oa_ready = (sem(n) for n in ("pb_exp", "pn_ready", "tp_done", "pts_ready", "ob_done", "oa_ready"))
        oa_moved = [sem(f"oa_moved{b}") for b in range(B)]
        mix_done = sem("mix_done")
        C0 = 4

        EXP0, PV0, ATT0, GELU0, Y0, ACC0, MAX0, OTURN0, OT0 = S_RING, 2 * TB, 2, 4, 2, 2, S_RING, 1, 1
        block = ctx.enter_context(nc.Block())

        w1_d, w2_d = ffn["w1"], ffn["w2"].rearrange("e (c p) d -> e p c d", p=P)

        def sp_rows(sp, c, it, buf):
            g = PAIRS * c
            if not isinstance(it, int) or c:
                sp.wait_ge(pv_done, PV0 + TB * (g + it - RING + 1))
            for s in range(2):
                for dst, src, axis in ((QB, q_rows, 1), (KB, k_rows, 0)):
                    rows = src[it:it + 1, s] if isinstance(it, int) else src[bass.ds(it, 1), s]
                    rows = rows.rearrange("a d r t -> r (a d) t").unsqueeze(axis).broadcast_to([3, 3, HD, L])
                    for i in range(3):
                        sp.dma_start(dst[buf][s][i * 3 * HD:(i + 1) * 3 * HD, :], rows[i]).then_inc(rows_loaded[buf], 16)
            va = VA[:, :, :, :, :].rearrange("p a s k d -> p (a s k d)")
            n = 2 * TB * STRIP
            sp.dma_start(VS[buf][:, :, :, :].rearrange("p s k d -> p (s k d)"), va[:, bass.ds(it * n, n)]).then_inc(rows_loaded[buf], 16)

        def sp_expert(sp, c, e, buf):
            if not isinstance(e, int):
                sp.wait_ge(split_done, E * c + e - 1)
            w1e = w1_d[e] if isinstance(e, int) else w1_d[bass.ds(e, 1)].rearrange("a d f -> (a d) f")
            w2e = w2_d[e] if isinstance(e, int) else w2_d[bass.ds(e, 1)].rearrange("a p c d -> p (a c) d")
            sp.dma_start(W1[buf], w1e).then_inc(ew_loaded[buf], 16)
            sp.dma_start(W2[buf], w2e).then_inc(ew_loaded[buf], 16)

        def sp_weights(sp, c, e, buf):
            if not isinstance(e, int):
                sp.wait_ge(acc_done, ACC0 + NG * E * c + NG * (e - 1))
            row = wt_rows[e:e + 1] if isinstance(e, int) else wt_rows[bass.ds(e, 1)]
            sp.dma_start(WB[buf], row.rearrange("a t -> (a t)").partition_broadcast(P)).then_inc(wb_loaded[buf], 16)

        def sp_ffn(sp, c):
            if c:
                sp.wait_ge(x_ready, 2)
                sp_expert(sp, c, 0, 0)
                sp_expert(sp, c, 1, 1)
            for b in range(B):
                sp.wait_ge(p3_done, 8 * c + 8 // B * (b + 1))
                for src, dst in ((qparts, q_rows), (kparts, k_rows)):
                    sp.dma_start(dst[b * (PAIRS // B):(b + 1) * (PAIRS // B)].rearrange("j s d r t -> (j s d) r t"),
                                 src[:, :, b * L:(b + 1) * L]).then_inc(rows_spilled[b], 16)
            sp.wait_ge(rows_spilled[0], 2 * 16 * (c + 1))
            sp.wait_ge(va_ready, NG * (c + 1))
            for k in range(RING):
                sp.wait_ge(filled, RING * c + k + 1)
                sp_rows(sp, c, k, k)
            sp.wait_ge(rows_spilled[1], 2 * 16 * (c + 1))
            with sp.Fori(1, PAIRS // RING) as i:
                for k in range(RING):
                    sp_rows(sp, c, i * RING + k, k)
            sp.wait_ge(wt_ready, NG * (c + 1))
            sp.dma_start(wt_rows, WT).then_inc(wt_stored, 16)
            sp.wait_ge(wt_stored, 16 * (c + 1))
            for e in range(2):
                sp_weights(sp, c, e, e)
            with sp.Fori(1, E // 2) as i:
                for k in range(2):
                    sp_expert(sp, c, i * 2 + k, k)
                    sp_weights(sp, c, i * 2 + k, k)


        def sp_window(sp, b, n, k):
            sp.wait_ge(ob_done, C0 + n - 3)
            sp.dma_start(VW[k], kv_rows[bass.ds(n * BT + b * (LP - L), P), 0:DC]).then_inc(vw_loaded[k], 16)

        def sp_sel_loads(sp):
            sp.wait_ge(w_loaded, 16 * 10)
            for dst, src in ((WKV[:, 0:DR], attn["W_kr"]), (WKV[:, DR:DR + HALF], attn["W_kr"][:, HALF:]),
                             (WKV[:, DR + HALF:2 * DR], attn["W_kr"][:, 0:HALF]), (WKV[:, 2 * DR:], attn["W_dkv"]),
                             (WIQ[:, :], attn["idx_wq"]), (WIK[:, 0:DH], attn["idx_wk"]), (WIK[:, DH:], attn["idx_wk"]),
                             (WDQ[:, :], attn["W_dq"]), (WQR[:, :], attn["W_qr"]),
                             (idx_w[:, :], attn["idx_w"].partition_broadcast(P))):
                sp.dma_start(dst, src).then_inc(sel_w_loaded, 16)
            sp.dma_start(WOUT[:, :, :], attn["W_out"].rearrange("(j p) d -> p j d", p=P)).then_inc(sel_w_loaded, 16)
            sp.dma_start(delta_row[:, 0, 0:HALF], attn["raw_delta"].partition_broadcast(P)).then_inc(delta_loaded, 16)
            for x in range(P // HALF):
                sp.dma_start(delta_col[x * HALF:(x + 1) * HALF, 0:1], attn["raw_delta"].rearrange("(i a) -> i a", a=1)).then_inc(delta_loaded, 16)
            sp.dma_start(bb1[:, :, :], ffn["bb1"].rearrange("e (f p) -> p e f", p=P), allow_slow_non_contiguous=True).then_inc(bb1_loaded, 16)

        def sp_sel(sp):
            sp.wait_ge(x_ready, 1)
            for dst, src in ((RAW[0:DCQ, 0:NH * DH], attn["W_uq"]), (RAW[0:DC, NH * DH:2 * NH * DH], attn["W_uk"]),
                             (RAW[0:DC, 2 * NH * DH:3 * NH * DH], attn["W_uv"])):
                sp.dma_start(dst, src).then_inc(raw_loaded, 16)
            sp.dma_start(ROT, rot_ap).then_inc(rot_loaded, 16)
            sp.wait_ge(kv_ready, 4)
            for b in range(B):
                base = b * LP
                sp.dma_start(kv_rows[base + LW:base + LW + L].rearrange("(t p) n -> p t n", p=P),
                             KVS[:, b * TB:(b + 1) * TB, :]).then_inc(kv_stored, 16)
                sp.dma_start(kv_rows[base:base + LW], KVS[0:LW, b * TB, :]).then_inc(kv_stored, 16)
                tail = LP - LW - L
                sp.dma_start(kv_rows[base + LW + L:base + LP], KVS[0:tail, b * TB, :]).then_inc(kv_stored, 16)
            for n in range(2 * B):
                g, b = n // B, n % B
                if n >= B:
                    sp.wait_ge(qr_ready, 2 * (n + 1))
                for src, row, ready in ((QT, 0, qt_ready), (QRD, DC, qr_ready), (QRL, DC + DR, qr_ready)):
                    sp.wait_ge(ready, 2 * (n + 1))
                    for h in range(4):
                        sp.dma_start(QALL[row:row + DC, 4 * g + h, b * L:(b + 1) * L], src[n % 2][h * DC:(h + 1) * DC, :]).then_inc(q_placed[n % 2], 16)
            sp.wait_ge(kv_stored, 16 * 3 * B)
            sp.wait_ge(si_done, NT * NIH)
            with sp.Fori(0, B) as b:
                for k in range(4):
                    sp_window(sp, b, b * NB + k, k)
                    for t in range(4):
                        same = kv_rows[bass.ds(b * LP + 2 * LW, NSEL)].unsqueeze(1).broadcast_to([NSEL, GB, ROWKV])
                        sp.dma_start(GE[k][t * NSEL:(t + 1) * NSEL, :, :], same).then_inc(same_loaded[k], 16)
                with sp.Fori(1, NB // 4) as i:
                    for k in range(4):
                        sp_window(sp, b, b * NB + i * 4 + k, k)
            for b in range(B):
                sp.wait_ge(oa_ready, C0 + (b + 1) * NB)
                for h in range(NH):
                    sp.dma_start(OAX[h % 4 * DC:(h % 4 + 1) * DC, h // 4, b * L:(b + 1) * L], OA[:, h, b * L:(b + 1) * L]).then_inc(oa_moved[b], 16)

        def pool_rstd(pool, n):
            for k in range(2):
                h = slice(k * NT // 2, (k + 1) * NT // 2)
                pool.wait_ge(var_ready, 2 * n + k + 1)
                pool.tensor_tensor(rstd[:, h], vareps[:, h], neghalf[:, h], ALU.pow).then_inc(rstd_ready, 1)

        def pool_ffn(pool, c):
            ln = (0, 4)[c]
            if c:
                pool.wait_ge(x_ready, 2)
            pool_rstd(pool, ln)
            pool_fill(pool, c)
            for n in (ln + 1, ln + 2):
                pool_rstd(pool, n)

        def pool_fill(pool, c):
            pool.memset(VA[:, :, :, :, HD:STRIP], 0.0)
            pool.drain()
            pool.memset(VA[:, :, :, :, HD:HD + 1], 1.0)
            pool.memset(MB[:, :, :], 0.0)
            for buf in range(RING):
                for s in range(2):
                    pool.drain()
                    pool.memset(QB[buf][s][64:MAXROW, :], 0.0)
                    pool.memset(KB[buf][s][64:MAXROW, :], 0.0)
                    pool.drain()
                    pool.memset(KB[buf][s][MAXROW:MAXROW + MAXROWS, :], 1.0)
                pool.drain()
                pool.memset(spare[:, 3:4], float(c)).then_inc(filled, 1)

        def pool_sel(pool):
            pool_rstd(pool, 3)
            for tile in range(NT):
                w = (tile % TB) * P + LW
                sc = SCORES[tile % 2][:, 0:w]
                if tile == 1:
                    pool.wait_ge(q_placed[1], 16 * 12 * B)
                if tile >= 2:
                    pool.wait_ge(best_ready, tile - 1)
                for h in range(1, NIH):
                    u = tile * NIH + h
                    pool.wait_ge(relu_done, u + 1)
                    pool.drain()
                    pool.tensor_tensor(sc, RL[0][:, 0:w] if h == 1 else sc, RL[u % 2][:, 0:w], ALU.add).then_inc(sc_used, 2 if h == 1 else 1)
            pool.wait_ge(kv_stored, 16 * 3 * B)
            with pool.Fori(0, B) as b:
                pool_gather(pool, b * TB, 0, LW // BT)
                pool_gather(pool, b * TB, 1, 0)
                with pool.Fori(1, TB // 2) as i:
                    for half in range(2):
                        pool_gather(pool, b * TB + 2 * i, half, 0)

        def pool_gather(pool, tile, half, first):
            pool.wait_ge(idx_ready, 4 * tile + 4 * (half + 1))
            pool.tensor_copy(IB[half][:, :], IDX[:, bass.ds(tile * (P // 4) + half * (P // 4), P // 4)]).then_inc(staged, 1)
            for k in range(first, P // BT):
                j = (k - LW // BT) % G_RING
                pool.wait_ge(staged, tile + half + 1)
                pool.wait_ge(ob_done, C0 + tile * (P // BT) + half * (P // BT) + k + 1 - G_RING)
                pool.tensor_tensor(turn[:, half, k:k + 1], neghalf[:, 0:1], neghalf[:, 0:1], ALU.add)
                for g in range(GB):
                    pool.indirect_dma_start(G[j][:, g, :], None, kv_rows,
                                            bass.IndirectOffsetOnAxis(ap=IB[half][:, k * GB + g:k * GB + g + 1], axis=0))\
                        .then_inc(gathered[j], 16)

        def pe_turn(pe, tile, n, ready, base):
            for g in range(NG):
                pe.wait_ge(ready, base + g + 1)
                for t in range(4):
                    m = pe.transpose(bank[g][:, t * P:(t + 1) * P], tile(4 * g + t), ident)
                m.then_inc(turned, 1)

        def pe_pass1(pe, c, it, buf, u, visit):
            s, qt, hf = UNITS1[u]
            n = PAIRS * c + it
            if u == 0:
                pe.wait_ge(rows_loaded[buf], ROW_LOADS * (PAIRS // RING * c + visit + 1))
            pe.wait_ge(max_done, MAX0 + N1 * n + u + 1 - S_RING)
            lo, hi = hf * BANK, min((qt + 1) * P, (hf + 1) * BANK)
            o = bank[u % S_RING]
            m = pe.matmul(o[:, 0:hi - lo], QB[buf][s][0:ROWS, qt * P:(qt + 1) * P], KB[buf][s][0:ROWS, lo:hi], start=True, stop=True)
            if hi == (qt + 1) * P:
                m = pe.matmul(o[:, hi - lo - P:hi - lo], ident_b[:, :], mask_qk[:, :], start=False, stop=True, skip_group_check=True)
            m.then_inc(s1_done, 1)

        def pe_maxrows(pe, c, it):
            n = PAIRS * c + it
            pe.wait_ge(att_done, ATT0 + n - 1)
            pe.wait_ge(mb_ready, n + 1)
            mt = bank[7][:, :].bitcast(BF16)
            for qt in range(TB):
                m = pe.transpose(mt[:, qt * P:(qt + 1) * P], MB[:, qt, :], ident_b[:, :])
            m.then_inc(mt_done, 1)

        def pe_scores(pe, c, it, buf, w):
            s, kc, hf = UNITS2[w]
            n = PAIRS * c + it
            if w == 0:
                pe.wait_ge(maxrow_ready, 2 * n + 2)
            pe.wait_ge(exp_done, EXP0 + N2 * n + w + 1 - S_RING)
            lo, hi = max(kc * P, hf * BANK), (hf + 1) * BANK
            o, rows = bank[S_RING + w % S_RING], MAXROW + MAXROWS
            m = pe.matmul(o[:, 0:hi - lo], KB[buf][s][0:rows, kc * P:(kc + 1) * P], QB[buf][s][0:rows, lo:hi], start=True, stop=True)
            if lo == kc * P:
                m = pe.matmul(o[:, 0:P], ident_b[:, :], mask_kq[:, :], start=False, stop=True, skip_group_check=True)
            m.then_inc(st_done, 1)

        def pe_values(pe, c, it, buf, kc):
            units = [w for w in range(N2) if UNITS2[w][1] == kc]
            n = PAIRS * c + it
            if kc == 0:
                pe.wait_ge(ot_ready, OT0 + n)
            pe.wait_ge(exp_done, EXP0 + N2 * n + units[-1] + 1)
            for w in units:
                s, _, hf = UNITS2[w]
                lo = max(kc * P, hf * BANK)
                r = (2 * s + hf) * STRIP
                m = pe.matmul(bank[6][r:r + STRIP, lo - hf * BANK:BANK], VS[buf][:, s, kc, :],
                              PT[w % PT_RING][:, 0:(hf + 1) * BANK - lo], start=(kc == 0), stop=True, skip_group_check=True)
            m.then_inc(pv_done, 1)

        def pe_outputs(pe, c, it):
            pe.wait_ge(att_done, ATT0 + PAIRS * c + it)
            pe.wait_ge(ot_ready, OT0 + PAIRS * c + it + 1)
            for t in range(4):
                m = pe.transpose(bank[7][:, t * P:(t + 1) * P], OT[:, t * P:(t + 1) * P], ident)
            m.then_inc(o_turned, 1)

        def ahead_units(left):
            return [(1, u) for u in range(EARLY, N1) if left >= 1] + [(2, u) for u in range(EARLY) if left >= 2]

        def pe_step(pe, c, b, it, buf, left, visit):
            todo = ahead_units(left)

            def ahead(n):
                for _ in range(min(n, len(todo))):
                    a, u = todo.pop(0)
                    pe_pass1(pe, c, it + a, (buf + a) % RING, u, visit + (buf + a) // RING)

            for kc in range(1, TB + 1):
                for w in [w for w in range(N2) if UNITS2[w][1] == kc]:
                    pe_scores(pe, c, it, buf, w)
                    ahead(1)
                if kc == MAX_AT and left >= 1:
                    pe_maxrows(pe, c, it + 1)
                pe_values(pe, c, it, buf, kc - 1)
            if left >= 1:
                pe_first_scores(pe, c, it + 1, (buf + 1) % RING, ahead)
            pe_outputs(pe, c, it)

        def pe_first_scores(pe, c, it, buf, ahead):
            for w in [w for w in range(N2) if UNITS2[w][1] == 0]:
                pe_scores(pe, c, it, buf, w)
                ahead(1)

        def pe_ffn(pe, c):
            n_turn = (0, 4)[c]
            pe_turn(pe, lambda t: XN[:, t, :], n_turn, xn_ready, NG * 2 * c)
            for n in range(8):
                if n % 2 == 0:
                    pe.wait_ge(xt_ready, NG * n_turn + n // 2 + 1)
                if n >= 4:
                    pe.wait_ge(r1_done, 8 * c + n - 3)
                pe.matmul(bank[4 + n % 4][:, :], w_qkv[:, (n % 2) * D:(n % 2 + 1) * D],
                          XT[:, (n // 2) * BANK:(n // 2 + 1) * BANK], start=True, stop=True).then_inc(qk_done, 1)
            for g in range(NG):
                for t in range(4):
                    m = pe.matmul(bank[g][:, t * P:(t + 1) * P], XT[:, (4 * g + t) * P:(4 * g + t + 1) * P],
                                  w_qkv[:, 2 * D:3 * D], start=True, stop=True)
                m.then_inc(v_done, 1)
            pe.wait_ge(masks_ready, 1)
            pe.wait_ge(va_ready, NG * (c + 1))
            pe.wait_ge(r1_done, 8 * (c + 1))
            for u in range(N1):
                pe_pass1(pe, c, 0, 0, u, 0)
            pe_maxrows(pe, c, 0)
            todo = list(range(EARLY))

            def ahead(n):
                for _ in range(n * EARLY // 4):
                    pe_pass1(pe, c, 1, 1, todo.pop(0), 0)

            pe_first_scores(pe, c, 0, 0, ahead)
            run_steps(pe, pe_step, c)
            pe.wait_ge(att_done, ATT0 + PAIRS * (c + 1))
            for gq in range(NG):
                for t in range(4):
                    m = pe.transpose(bank[gq][:, t * P:(t + 1) * P], ATT[:, 4 * gq + t, :], ident)
                m.then_inc(turned, 1)
            for gq in range(NG):
                pe.wait_ge(xt_ready, NG * (n_turn + 1) + gq + 1)
                for t in range(4):
                    m = pe.matmul(bank[4 + gq][:, t * P:(t + 1) * P], XT[:, (4 * gq + t) * P:(4 * gq + t + 1) * P],
                                  w_o[:, :], start=True, stop=True)
                m.then_inc(o_done, 1)
            pe_turn(pe, lambda t: HN[:, t, :], n_turn + 2, h_ready, NG * c)
            pe.wait_ge(xt_ready, NG * (n_turn + 3))
            for t in range(NT):
                m = pe.matmul(bank[4][:, t * E:(t + 1) * E], XT[:, t * P:(t + 1) * P], wg[:, :], start=True, stop=True)
            m.then_inc(gate_done, 1)
            pe.wait_ge(w8_ready, c + 1)
            for gq in range(NG):
                for t in range(4):
                    m = pe.transpose(bank[gq][0:E, t * P:(t + 1) * P], W8[:, 4 * gq + t, :], ident)
                m.then_inc(w8_turned, 1)
            for gq in range(NG):
                pe.wait_ge(wt_ready, NG * c + gq + 1)
                pe.matmul(bank[4 + gq][:, :], bb2[:, :], WT[:, gq * BANK:(gq + 1) * BANK], start=True, stop=True).then_inc(b2_done, 1)
            pe.wait_ge(acc0_ready, NG * (c + 1))
            pe.wait_ge(xr2_ready, NG * (c + 1))
            run_experts(pe, pe_expert, c)
            pe.wait_ge(sum_ready, c + 1)
            for gq in range(NG):
                for t in range(4):
                    m = pe.transpose(bank[gq][:, t * P:(t + 1) * P], ACC[:, (4 * gq + t) * P:(4 * gq + t + 1) * P], ident)
                m.then_inc(sum_turned, 1)

        def run_experts(eng, expert, c):
            with eng.Fori(0, E // 2 - 1) as i:
                for k in range(2):
                    expert(eng, c, i * 2 + k, k, i, False)
            for k in range(2):
                expert(eng, c, E - 2 + k, k, E // 2 - 1, k == 1)

        def run_steps(eng, step, c):
            per = PAIRS // B // RING
            for b in range(B):
                n = per - (b == B - 1)
                with eng.Fori(0, n) as i:
                    for k in range(RING):
                        step(eng, c, b, i * RING + b * (PAIRS // B) + k, k, PAIRS, i + b * per)
            for k in range(RING):
                step(eng, c, B - 1, PAIRS - RING + k, k, RING - 1 - k, B * per - 1)

        def pe_expert(pe, c, e, buf, visit, last):
            pairs = ((0, 0), (0, 1), (1, 0))
            pe.wait_ge(split_done, E * c + e + 1)
            for tb in range(NG + 1):
                if tb < NG:
                    for f in range(FC):
                        n = E * NG * FC * c + e * (NG * FC) + tb * FC + f
                        pe.wait_ge(gelu_done, GELU0 + n - 3)
                        for w, x in pairs:
                            m = pe.matmul(bank[f][:, :], W1R[buf][w][:, f * P:(f + 1) * P], XR[x][:, tb * BANK:(tb + 1) * BANK],
                                          start=((w, x) == pairs[0]), stop=((w, x) == pairs[-1]))
                        m.then_inc(a_done, 1)
                if tb >= 1:
                    u = E * NG * c + e * NG + tb - 1
                    k = (tb - 1) % 2
                    pe.wait_ge(acc_done, ACC0 + u - 1)
                    for f in range(FC):
                        pe.wait_ge(hr2_done, u * FC + f + 1)
                        for w, x in pairs:
                            m = pe.matmul(bank[4 + k][:, :], W2R[buf][w][:, f, :], H1R[k][x][:, f, :],
                                          start=(f == 0 and (w, x) == pairs[0]), stop=(f == FC - 1 and (w, x) == pairs[-1]))
                    m.then_inc(y_done, 1)

        def pe_sel(pe):
            pe_turn(pe, lambda t: XN[:, t, :], 3, xn_ready, NG)
            pe.wait_ge(sel_w_loaded, 16 * 11)
            pe.wait_ge(raw_loaded, 16 * 3)
            for j in range(NH // 2):
                pe.transpose(bank[4][:, j * DCQ:(j + 1) * DCQ], RAW[0:DCQ, j * P:(j + 1) * P], ident[0:DCQ, 0:DCQ])
            for k in range(2):
                for j in range(NH // 2):
                    o = (k + 1) * NH * DH + j * P
                    m = pe.transpose(bank[5][:, (4 * k + j) * DC:(4 * k + j + 1) * DC], RAW[0:DC, o:o + P], ident[0:DC, 0:DC])
            m.then_inc(uqk_turned, 1)
            pe.wait_ge(uqk_ready, 3)
            for h in range(NH):
                r, j = slice((h % 2) * DH, (h % 2 + 1) * DH), h // 2
                pe.matmul(bank[6 + h % 2][0:DCQ, j * DC:(j + 1) * DC], UQT[r, j, :], UKT[r, j, :], start=True, stop=True)
            for h in range(NH):
                r, j = slice((h % 2) * DH, (h % 2 + 1) * DH), h // 2
                m = pe.matmul(bank[4][h % 4 * DC:(h % 4 + 1) * DC, h // 4 * D:(h // 4 + 1) * D], UVT[r, j, :], WOUT[r, j, :],
                              start=True, stop=True)
            m.then_inc(prep_done, 1)
            pe.wait_ge(prep_ready, 3)
            for n in range(8):
                pe.wait_ge(xt_ready, NG * 3 + n // 2 + 1)
                pe.matmul(bank[n][:, :], WIQ[:, (n % 2) * P:(n % 2 + 1) * P], XT[:, (n // 2) * BANK:(n // 2 + 1) * BANK],
                          start=True, stop=True).then_inc(qi_done, 1)
            for n in range(4):
                pe.wait_ge(qi_ready, n + 1)
                pe.matmul(bank[n][:, :], WIK[:, :], XT[:, n * BANK:(n + 1) * BANK], start=True, stop=True).then_inc(ki_done, 1)
            for q in range(4):
                pe.wait_ge(qi_ready, 5 + q)
                for t in range(4):
                    m = pe.matmul(bank[4 + q][:, t * P:t * P + ROWKV], XT[:, (4 * q + t) * P:(4 * q + t + 1) * P], WKV[:, :],
                                  start=True, stop=True)
                m.then_inc(kv_done, 1)
            for n in range(4):
                pe.wait_ge(ki_ready, n + 1)
                pe.matmul(bank[n][0:ROWKV, :], WKV[:, :], XT[:, n * BANK:(n + 1) * BANK], start=True, stop=True).then_inc(kt_done, 1)
            for n in range(4):
                pe.wait_ge(kv_ready, n + 1)
                pe.matmul(bank[4 + n][0:DCQ, :], WDQ[:, :], XT[:, n * BANK:(n + 1) * BANK], start=True, stop=True).then_inc(cq_done, 1)
            pe.wait_ge(qi_ready, 8)
            pe.wait_ge(cq_ready, 4)
            pe.wait_ge(kl_ready, 1)
            pe_raw_queries(pe, 0)
            for n in range(2 * B):
                if n + 1 < 2 * B:
                    pe_raw_queries(pe, n + 1)
                for half in range(2):
                    if n >= 1:
                        pe.wait_ge(qr_ready, 2 * n)
                    pe.wait_ge(mu_ready, 2 * n + half + 1)
                    pe.matmul(bank[4 + half][:, :], cst("swap"), MU[n % 2][:, half * BANK:(half + 1) * BANK], start=True, stop=True)\
                      .then_inc(mus_done, 1)
            pe.wait_ge(qr_ready, 2 * 2 * B)
            pe.wait_ge(qt_ready, 2 * 2 * B)
            for tile in range(NT):
                b, w = tile // TB, (tile % TB) * P + LW
                for h in range(NIH):
                    u = tile * NIH + h
                    if u >= 3:
                        pe.wait_ge(relu_done, u - 2)
                    r = slice((h % 2) * DH, (h % 2 + 1) * DH)
                    for half in range((w + BANK - 1) // BANK):
                        lo, hi = half * BANK, min(w, (half + 1) * BANK)
                        m = pe.matmul(bank[2 * (u % 3) + half][:, 0:hi - lo], QI[r, h // 2, tile * P:(tile + 1) * P],
                                      KI[r, b * L + lo:b * L + hi], start=True, stop=True)
                    m.then_inc(si_done, 1)
                if tile >= 2:
                    pe_index(pe, tile - 2)
            for tile in range(NT - 2, NT):
                pe_index(pe, tile)
            pe.wait_ge(relu_done, NT * NIH)
            pe.wait_ge(idx_ready, 4 * NT)
            run_blocks(pe, pe_ahead, pe_block)
            for gq in range(NG):
                if gq % (NG // B) == 0:
                    pe.wait_ge(oa_moved[gq // (NG // B)], 16 * NH)
                for t in range(4):
                    tile = 4 * gq + t
                    for x in range(NH * DC // P):
                        m = pe.matmul(bank[gq][:, t * P:(t + 1) * P], OAX[:, x, tile * P:(tile + 1) * P], MO[:, x, :],
                                      start=(x == 0), stop=(x == NH * DC // P - 1))
                m.then_inc(mix_done, 1)

        def pe_raw_queries(pe, n):
            g, b = n // B, n % B
            for half in range(2):
                blk = slice(half * BANK, (half + 1) * BANK)
                if n >= 1:
                    pe.wait_ge(qt_ready, 2 * (n - 1) + half + 1)
                pe.matmul(bank[half][:, :], AQ[:, g * P:(g + 1) * P], CQ[:, b, blk], start=True, stop=True).then_inc(qt_done, 1)
                if n >= 2:
                    pe.wait_ge(mu_ready, 2 * (n - 2) + half + 1)
                pe.matmul(raw_bank(n, half)[:, :], WQR[:, g * P:(g + 1) * P], CQ[:, b, blk], start=True, stop=True).then_inc(mu_done, 1)

        def raw_bank(n, half):
            return bank[(2, 6)[n % 2] + half]

        def pe_index(pe, tile):
            pe.wait_ge(best_ready, tile + 1)
            if tile >= 1:
                pe.wait_ge(idx_ready, 4 * tile)
            pe.transpose(bank[6][0:NSEL, 0:P], bidf[:, tile % 2, :], ident).then_inc(i_turned, 1)

        def run_blocks(eng, ahead, block_):
            with eng.Fori(0, B) as b:

                def first(k):
                    return GE[k], same_loaded[k], b * (16 * 4) + 16 * 4

                def slot(i, j):
                    per = (NB - 4 - j + G_RING - 1) // G_RING
                    return G[j], gathered[j], b * (per * 16 * GB) + i * (16 * GB) + 16 * GB

                ahead(eng, b, b * NB, 0, first(0))
                for k in range(4):
                    block_(eng, b, b * NB + k, k, first(k), first(k + 1) if k < 3 else slot(0, 0), True)
                rounds = (NB - 4) // G_RING
                with eng.Fori(0, rounds) as i:
                    for j in range(G_RING):
                        block_(eng, b, b * NB + 4 + i * G_RING + j, j % 4, slot(i, j), slot(i + (j + 1) // G_RING, (j + 1) % G_RING), False)
                for k in range(4):
                    block_(eng, b, b * NB + (NB - 4) + k, k, slot(rounds, k), slot(rounds, k + 1) if k < 3 else None, False)

        def pe_ahead(pe, b, n, k, rows):
            pe_local(pe, b, n, k)
            pe_gt(pe, n, k, rows)
            pe_sel_scores(pe, n, k)

        def pe_local(pe, b, n, k):
            pe.wait_ge(qs_ready, n + 1)
            pe.wait_ge(sm_ready, C0 + n - 1)
            keys = KL.rearrange("p b t -> p (b t)")
            pe.matmul(bank[k % 2][:, 0:P], QS[k % 2], keys[:, bass.ds(n * BT + b * (LP - L), P)], start=True, stop=True)

        def pe_gt(pe, n, k, rows):
            pe.wait_ge(rot_done, n + 1)
            pe.wait_ge(gts_ready, C0 + n - 1)
            for g in range(GB):
                m = pe.transpose(bank[2 + k % 2][0:ROWKV, g * P:(g + 1) * P], rows[0][:, g, :], ident)
            m.then_inc(gt_done, 1)

        def pe_sel_scores(pe, n, k):
            pe.wait_ge(gts_ready, C0 + n + 1)
            for g in range(GB):
                m = pe.matmul(bank[k % 2][g * STRIP:(g + 1) * STRIP, P:2 * P], QS[k % 2][:, g * STRIP:(g + 1) * STRIP],
                              GTS[k % 2][:, g, :], start=True, stop=True)
            m.then_inc(s_done, 1)

        def pe_block(pe, b, n, k, rows, ahead, early):
            k1 = (k + 1) % 4
            if ahead:
                pe_local(pe, b, n + 1, k1)
                pe_gt(pe, n + 1, k1, ahead)
            pe.wait_ge(pn_ready, n + 1)
            pe.wait_ge(pts_ready, C0 + n - 1)
            for x in range(2):
                m = pe.transpose(bank[4 + k % 2][:, x * P:(x + 1) * P], PB[k % 2][:, x * P:(x + 1) * P], ident)
            m.then_inc(tp_done, 1)
            if ahead:
                pe_sel_scores(pe, n + 1, k1)
            pe.wait_ge(vw_loaded[k], visit16(n, k))
            pe.wait_ge(oa_ready, C0 + n - 1)
            pe.wait_ge(pts_ready, C0 + n + 1)
            o = bank[6 + k % 2]
            pe.matmul(o[0:DC, 0:P], VW[k], PTS[k % 2][:, 0:P], start=True, stop=True)
            for g in range(GB):
                m = pe.matmul(o[0:DC, g * STRIP:(g + 1) * STRIP], rows[0][:, g, 0:DC], PTS[k % 2][:, P + g * STRIP:P + (g + 1) * STRIP],
                              start=False, stop=True, skip_group_check=True)
            m.then_inc(ob_done, 1)

        def visit16(n, k):
            return n * 4 + (16 - 4 * k)


        def act_turn(act, n, gain=None, bias=None):
            for g in range(NG):
                act.wait_ge(turned, NG * n + g + 1)
                dst = XT[:, g * BANK:(g + 1) * BANK]
                if gain is None:
                    m = act.activation(dst, bank[g][:, :], ACT.Copy)
                else:
                    m = act.activation(dst, bank[g][:, :], ACT.Identity, scale=gain, bias=bias)
                m.then_inc(xt_ready, 1)

        def act_exps(act, c, it, kcs):
            n = PAIRS * c + it
            for w in range(N2):
                s, kc, hf = UNITS2[w]
                if kc not in kcs:
                    continue
                act.wait_ge(st_done, N2 * n + w + 1)
                k = UNITS2[w - PT_RING][1]
                act.wait_ge(pv_done, PV0 + TB * n + k + 1 - (TB if w < PT_RING else 0))
                m = (hf + 1) * BANK - max(kc * P, hf * BANK)
                act.activation(PT[w % PT_RING][:, 0:m], bank[S_RING + w % S_RING][:, 0:m], ACT.Exp, scale=float(HD) ** -0.5)\
                   .then_inc(exp_done, 1)

        def act_maxrows(act, c, it, buf):
            act.wait_ge(mt_done, PAIRS * c + it + 1)
            for s in range(2):
                act.activation(QB[buf][s][MAXROW:MAXROW + MAXROWS, :],
                               bank[7][:, :].bitcast(BF16)[s * STRIP:s * STRIP + MAXROWS, :], ACT.Copy).then_inc(maxrow_ready, 1)

        def act_step(act, c, b, it, buf, left, visit):
            act_exps(act, c, it, range(1, MAX_AT + 1))
            if left >= 1:
                act_maxrows(act, c, it + 1, (buf + 1) % RING)
            act_exps(act, c, it, range(MAX_AT + 1, TB))
            n = PAIRS * c + it
            act.wait_ge(pv_done, PV0 + TB * (n + 1))
            act.wait_ge(o_turned, OTURN0 + n)
            act.activation(OT[:, :], bank[6][:, :], ACT.Copy).then_inc(ot_ready, 1)
            if left >= 1:
                act_exps(act, c, it + 1, (0,))

        def act_ffn(act, c):
            n_turn = (0, 4)[c]
            act_turn(act, n_turn)
            for n in range(9):
                if n < 8:
                    act.wait_ge(qk_done, 8 * c + n + 1)
                    blk = slice((n // 2) * BANK, (n // 2 + 1) * BANK)
                    act.activation((qparts, kparts)[n % 2][:, 0, blk], bank[4 + n % 4][:, :], ACT.Copy).then_inc(p1_done, 1)
                if n >= 1:
                    m = n - 1
                    act.wait_ge(r1_done, 8 * c + m + 1)
                    blk = slice((m // 2) * BANK, (m // 2 + 1) * BANK)
                    act.activation((qparts, kparts)[m % 2][:, 1, blk], rest[:, m % 2, :], ACT.Copy).then_inc(p2_done, 1)
            for g in range(NG):
                act.wait_ge(v_done, NG * c + g + 1)
                b, t0 = 4 * g // TB, 4 * g % TB
                for t in range(4):
                    dst = VA[:, b * (PAIRS // B):(b + 1) * (PAIRS // B), :, t0 + t, 0:HD].rearrange("p a s d -> p (a s) d")
                    m = act.activation(dst, bank[g][:, t * P:(t + 1) * P].rearrange("p (h d) -> p h d", d=HD), ACT.Copy)
                m.then_inc(va_ready, 1)
            act_maxrows(act, c, 0, 0)
            act_exps(act, c, 0, (0,))
            run_steps(act, act_step, c)
            act_turn(act, n_turn + 1)
            act.wait_ge(bb1_loaded, 16)
            act.wait_ge(w_loaded, 16 * 10)
            gain, bias = gain_col[:, 0:1], gain_col[:, 1:2]
            act_turn(act, n_turn + 2, gain, bias)
            for g in range(NG):
                act.activation(XR[0][:, g * BANK:(g + 1) * BANK], bank[g][:, :], ACT.Identity, scale=gain, bias=bias).then_inc(xr1_ready, 1)
            act.wait_ge(lg_ready, c + 1)
            act.activation(lg[:, :, :], lg[:, :, :], ACT.Exp).then_inc(eg_ready, 1)
            for gq in range(NG):
                act.wait_ge(w8_turned, NG * c + gq + 1)
                act.activation(WT[:, gq * BANK:(gq + 1) * BANK], bank[gq][0:E, :], ACT.Copy).then_inc(wt_ready, 1)
            for gq in range(NG):
                act.wait_ge(b2_done, NG * c + gq + 1)
                act.activation(ACC[:, gq * BANK:(gq + 1) * BANK], bank[4 + gq][:, :], ACT.Copy).then_inc(acc0_ready, 1)
            run_experts(act, act_expert, c)

        def act_expert(act, c, e, buf, visit, last):
            act.activation(bias1[buf][:, :], bb1[:, :, :].rearrange("p e f -> p (e f)")[:, bass.ds(e * FC, FC)], ACT.Copy)
            act.drain()
            for tb in range(NG):
                u = E * NG * c + e * NG + tb
                act.wait_ge(y_done, Y0 + u - 1)
                for f in range(FC):
                    act.wait_ge(a_done, u * FC + f + 1)
                    act.activation(H1[tb % 2][:, f, :], bank[f][:, :], ACT.Gelu_apprx_tanh, bias=bias1[buf][:, f:f + 1])
                    act.activation(H1R[tb % 2][0][:, f, :], bank[f][:, :], ACT.Gelu_apprx_tanh,
                                   bias=bias1[buf][:, f:f + 1]).then_inc(gelu_done, 1)

        def act_log(act, tensors):
            act.drain()
            for t in tensors:
                act.activation(t, t, ACT.Exp, scale=-1.0)
            act.drain()
            for t in tensors:
                m = act.activation(t, t, ACT.Ln, bias=1.0)
            return m

        def act_sel(act):
            act.wait_ge(delta_loaded, 16 * 9)
            act.activation(delta_row[:, 1, 0:HALF], delta_row[:, 0, 0:HALF], ACT.Exp, scale=-1.0).then_inc(sig_ready, 1)
            act.activation(delta_col[:, 1:2], delta_col[:, 0:1], ACT.Exp, scale=-1.0).then_inc(sig_ready, 1)
            act_turn(act, 3)
            act.wait_ge(uqk_turned, 1)
            act.activation(UQT[:, :, :].rearrange("p a b -> p (a b)"), bank[4][:, 0:NH // 2 * DCQ], ACT.Copy).then_inc(uqk_ready, 1)
            act.activation(UKT[:, :, :].rearrange("p a b -> p (a b)"), bank[5][:, 0:NH // 2 * DC], ACT.Copy).then_inc(uqk_ready, 1)
            act.activation(UVT[:, :, :].rearrange("p a b -> p (a b)"), bank[5][:, NH // 2 * DC:NH * DC], ACT.Copy).then_inc(uqk_ready, 1)
            act.wait_ge(prep_done, 1)
            for k in range(2):
                act.activation(AQ[:, :].rearrange("p (j s c) -> p s j c", s=2, c=DC)[:, k],
                               bank[6 + k][0:DCQ, 0:NH // 2 * DC].rearrange("p (j c) -> p j c", c=DC), ACT.Copy).then_inc(prep_ready, 1)
            act.activation(MO[:, :, :].rearrange("p a d -> p (a d)"), bank[4][:, 0:NH * DC // P * D], ACT.Copy).then_inc(prep_ready, 1)
            for n in range(8):
                act.wait_ge(qi_done, n + 1)
                act.activation(QI[:, n % 2, (n // 2) * BANK:(n // 2 + 1) * BANK], bank[n][:, :], ACT.Copy).then_inc(qi_ready, 1)
            act.wait_ge(ang_ready, 2)
            act.activation(delta_row[:, 3:5, 0:HALF], delta_row[:, 1:3, 0:HALF], ACT.Sin).then_inc(trig_ready, 1)
            act.activation(delta_col[:, 3:5], delta_col[:, 1:3], ACT.Sin).then_inc(trig_ready, 1)
            for q in range(4):
                act.wait_ge(kv_done, q + 1)
                src = bank[4 + q][:, :].rearrange("p (t n) -> p t n", n=P)[:, :, 0:2 * DR]
                act.activation(KVS[:, 4 * q:4 * q + 4, DC:ROWKV], src, ACT.Abs)
            for n in range(4):
                act.wait_ge(kt_done, n + 1)
                act.activation(ATTf[0:2 * DR, n * BANK:(n + 1) * BANK], bank[n][0:2 * DR, :], ACT.Abs)
                b, t = n // 2, (n % 2) * BANK
                act.activation(KL[0:DC, b, LW + t:LW + t + BANK], bank[n][2 * DR:ROWKV, :], ACT.Copy).then_inc(kt_c, 1)
            act_log(act, (KVS[:, :, DC:ROWKV], ATTf[0:2 * DR, :])).then_inc(kv_log, 1)
            for n in range(4):
                act.wait_ge(cq_done, n + 1)
                act.activation(CQ[:, n // 2, (n % 2) * BANK:(n % 2 + 1) * BANK], bank[4 + n][0:DCQ, :], ACT.Copy).then_inc(cq_ready, 1)
            for n in range(2 * B):
                if n >= 2:
                    act.wait_ge(q_placed[n % 2], 16 * 12 * (n // 2))
                for half in range(2):
                    act.wait_ge(qt_done, 2 * n + half + 1)
                    act.activation(QT[n % 2][:, half * BANK:(half + 1) * BANK], bank[half][:, :], ACT.Copy).then_inc(qt_ready, 1)
                if n >= 2:
                    act.wait_ge(qr_ready, 2 * (n - 1))
                for half in range(2):
                    act.wait_ge(mu_done, 2 * n + half + 1)
                    act.activation(MU[n % 2][:, half * BANK:(half + 1) * BANK], raw_bank(n, half)[:, :], ACT.Abs)
                act_log(act, (MU[n % 2],)).then_inc(mu_log, 1)
            act.wait_ge(sel_w_loaded, 16 * 11)
            for tile in range(NT):
                w = (tile % TB) * P + LW
                for h in range(NIH):
                    u = tile * NIH + h
                    act.wait_ge(si_done, u + 1)
                    if u >= 2:
                        act.wait_ge(sc_used, u - 1)
                    for half in range((w + BANK - 1) // BANK):
                        lo, hi = half * BANK, min(w, (half + 1) * BANK)
                        m = act.activation(RL[u % 2][:, lo:hi], bank[2 * (u % 3) + half][:, 0:hi - lo], ACT.Relu)
                    act.drain()
                    act.activation(RL[u % 2][:, 0:w], RL[u % 2][:, 0:w], ACT.Identity, scale=idx_w[:, h:h + 1]).then_inc(relu_done, 1)
                if tile >= 2:
                    act_index(act, tile - 2)
            for tile in range(NT - 2, NT):
                act_index(act, tile)
            run_blocks(act, act_ahead, act_block)

        def act_index(act, tile):
            act.wait_ge(i_turned, tile + 1)
            src = bank[6][0:NSEL, 0:P].rearrange("p (g t) -> p t g", t=4)
            for t in range(4):
                act.activation(IDX[t * NSEL:(t + 1) * NSEL, tile * (P // 4):(tile + 1) * (P // 4)], src[:, t, :], ACT.Copy).then_inc(idx_ready, 1)

        def act_ahead(act, b, n, k, rows):
            act_gt(act, n, k)

        def act_gt(act, n, k):
            act.wait_ge(s_done, C0 + n - 1)
            act.wait_ge(gt_done, n + 1)
            act.activation(GTS[k % 2][0:DC + DR].rearrange("p g n -> p (g n)"), bank[2 + k % 2][0:DC + DR, :], ACT.Copy).then_inc(gts_ready, 1)

        def act_block(act, b, n, k, rows, ahead, early):
            act.wait_ge(tp_done, C0 + n - 1)
            act.wait_ge(sm_ready, C0 + n + 1)
            c = col[:, k % 2, :]
            act.activation(PB[k % 2], SM[k % 2], ACT.Exp, scale=SCALE2, bias=c[:, 1:2], accum_out=c[:, 2:3]).then_inc(pb_exp, 1)
            if ahead:
                act_gt(act, n + 1, (k + 1) % 4)

        def dve_norm(dve, src, dst, n, done):
            for k, h in enumerate(dve_sums(dve, src)):
                dve.wait_ge(rstd_ready, 2 * n + k + 1)
                for t in h:
                    m = dve.tensor_scalar(dst[:, t, :], src[:, t, :], mv[:, t, 0:1], rstd[:, t:t + 1], ALU.subtract, ALU.mult)
                    if done is not None and t % 4 == 3:
                        m.then_inc(done, 1)

        def dve_sums(dve, src):
            halves = [range(h * NT // 2, (h + 1) * NT // 2) for h in range(2)]
            for h in halves:
                for t in h:
                    dve.bn_stats(stats[:, t, :], src[:, t, :])
                dve.drain()
                for t in h:
                    dve.bn_aggr(mv[:, t, :], stats[:, t, :])
                dve.drain()
                dve.tensor_scalar(vareps[:, h[0]:h[-1] + 1], mv[:, h[0]:h[-1] + 1, 1], FFN_EPS, None, ALU.add).then_inc(var_ready, 1)
            return halves

        def dve_max(dve, c, it, u):
            s, qt, hf = UNITS1[u]
            dve.wait_ge(s1_done, N1 * (PAIRS * c + it) + u + 1)
            n = min((qt + 1) * P - hf * BANK, BANK)
            dve.tensor_reduce(rowmax[:, hf, s, qt:qt + 1], bank[u % S_RING][:, 0:n], AX_X, ALU.max).then_inc(max_done, 1)

        def dve_maxrows(dve, c, it):
            parts = [MB[:, :, 0:2 * STRIP].rearrange("p t (s r) -> p s t r", s=2)[:, :, :, r] for r in range(MAXROWS)]
            top = rowmax[:, 0, :, :]
            n = PAIRS * c + it
            dve.drain()
            dve.tensor_tensor(rowmax[:, 0, :, 4:], rowmax[:, 0, :, 4:], rowmax[:, 1, :, 4:], ALU.max)
            dve.drain()
            if not isinstance(n, int) or n:
                dve.wait_ge(mt_done, n)
            dve.tensor_scalar(parts[0], top, -1.0, None, ALU.mult)
            dve.drain()
            dve.scalar_tensor_tensor(maxrest[:, :, :], top, -1.0, parts[0], ALU.mult, ALU.subtract)
            dve.drain()
            dve.tensor_copy(parts[1], maxrest[:, :, :])
            dve.drain()
            dve.tensor_tensor(parts[2], maxrest[:, :, :], parts[1], ALU.subtract).then_inc(mb_ready, 1)

        def dve_outputs(dve, c, b, it):
            dve.wait_ge(o_turned, OTURN0 + PAIRS * c + it + 1)
            o = bank[7][:, :].rearrange("p (t s h d) -> p s h t d", t=4, s=2, h=2)
            for s in range(2):
                dve.reciprocal(rsum[:, s, :, :], o[:, s, :, :, HD])
            dve.drain()
            att = ATT[:, :, :].rearrange("p t d -> p (t d)")[:, b * L:(b + 1) * L].rearrange("p (h t d) -> p h t d", h=2, d=D)
            for s in range(2):
                m = dve.tensor_tensor(att[:, :, :, bass.ds((it - b * TB) * (2 * HD) + s * HD, HD)], o[:, s, :, :, 0:HD],
                                      rsum[:, s, :, :].unsqueeze(3).broadcast_to([P, 2, 4, HD]), ALU.mult)
            m.then_inc(att_done, 1)

        def dve_step(dve, c, b, it, buf, left, visit):
            todo = ahead_units(left)
            for a, u in todo:
                dve_max(dve, c, it + a, u)
                if (a, u) == (1, N1 - 1):
                    dve_maxrows(dve, c, it + 1)
            dve_outputs(dve, c, b, it)

        def dve_split(dve, c, e, buf, visit):
            dve.wait_ge(ew_loaded[buf], 32 * (E // 2 * c + 1 + visit))
            for w, parts in ((W1[buf], W1R[buf]), (W2[buf], W2R[buf])):
                dve.tensor_scalar(parts[0][...], w, 1.0, None, ALU.mult)
            dve.drain()
            for w, parts in ((W1[buf], W1R[buf]), (W2[buf], W2R[buf])):
                m = dve.tensor_tensor(parts[1][...], w, parts[0][...].bitcast(F32), ALU.subtract)
            m.then_inc(split_done, 1)

        def dve_expert(dve, c, e, buf, visit, last):
            for tb in range(NG + 1):
                u = E * NG * c + e * NG + tb
                if tb < NG:
                    for f in range(FC):
                        dve.wait_ge(gelu_done, GELU0 + u * FC + f + 1)
                        dve.tensor_tensor(H1R[tb % 2][1][:, f, :], H1[tb % 2][:, f, :], H1R[tb % 2][0][:, f, :].bitcast(F32), ALU.subtract)\
                           .then_inc(hr2_done, 1)
                if tb >= 1:
                    t, k = slice((tb - 1) * BANK, tb * BANK), (tb - 1) % 2
                    if tb == 1:
                        dve.wait_ge(wb_loaded[buf], 16 * (E // 2 * c + 1 + visit))
                    dve.wait_ge(y_done, Y0 + u)
                    dve.tensor_tensor(YW[k], bank[4 + k][:, :], WB[buf][:, t], ALU.mult).then_inc(acc_done, 1)
                    dve.drain()
                    m = dve.tensor_tensor(ACC[:, t], ACC[:, t], YW[k], ALU.add)
                    if last and tb == NG:
                        m.then_inc(sum_ready, 1)
                    if tb == 2 and not last:
                        dve_split(dve, c, e + 1, 1 - buf, visit + buf)

        def dve_ffn(dve, c):
            ln = (0, 4)[c]
            dve_norm(dve, X, XN, ln, xn_ready)
            if c == 0:
                dve.wait_ge(const_loaded, 16)
                dve.tensor_copy(ident_b[:, :], ident)
                dve.tensor_copy(mask_qk[:, :], cst("mask_qk"))
                dve.tensor_copy(mask_kq[:, :], cst("mask_kq")).then_inc(masks_ready, 1)
            for n in range(9):
                if n < 8:
                    blk = slice((n // 2) * BANK, (n // 2 + 1) * BANK)
                    if n >= 2:
                        dve.wait_ge(p2_done, 8 * c + n - 1)
                    dve.wait_ge(p1_done, 8 * c + n + 1)
                    dve.drain()
                    dve.tensor_tensor(rest[:, n % 2, :], bank[4 + n % 4][:, :], (qparts, kparts)[n % 2][:, 0, blk], ALU.subtract)\
                       .then_inc(r1_done, 1)
                if n >= 1:
                    m = n - 1
                    blk = slice((m // 2) * BANK, (m // 2 + 1) * BANK)
                    dve.wait_ge(p2_done, 8 * c + m + 1)
                    p = (qparts, kparts)[m % 2]
                    dve.tensor_tensor(p[:, 2, blk], rest[:, m % 2, :], p[:, 1, blk], ALU.subtract).then_inc(p3_done, 1)
            dve.wait_ge(filled, RING * c + 1)
            for u in range(N1):
                dve_max(dve, c, 0, u)
            dve_maxrows(dve, c, 0)
            for u in range(EARLY):
                dve_max(dve, c, 1, u)
            run_steps(dve, dve_step, c)
            dve_split(dve, c, 0, 0, 0)
            for gq in range(NG):
                dve.wait_ge(o_done, NG * c + gq + 1)
                dve.tensor_tensor(XN[:, 4 * gq:4 * gq + 4, :], XN[:, 4 * gq:4 * gq + 4, :],
                                  bank[4 + gq][:, :].rearrange("p (t d) -> p t d", d=D), ALU.add)
            dve.drain()
            dve_norm(dve, XN, HN, ln + 1, h_ready)
            dve.wait_ge(w_loaded, 16 * 10)
            if c == 0:
                dve.tensor_scalar(gains[:, 2:, :], gains[:, 2:, :], 0.5, None, ALU.mult)
                dve.drain()
            for g in range(NG):
                t = slice(4 * g, 4 * g + 4)
                dve.tensor_tensor(X[:, t, :], X[:, t, :], gains[:, 3, :].unsqueeze(1).broadcast_to([P, 4, D]), ALU.add)
            for g in range(NG):
                t = slice(g * BANK, (g + 1) * BANK)
                dve.wait_ge(xr1_ready, NG * c + g + 1)
                dve.tensor_tensor(XR[1][:, t], XT[:, t], XR[0][:, t].bitcast(F32), ALU.subtract).then_inc(xr2_ready, 1)
            dve.wait_ge(gate_done, c + 1)
            gate = bank[4][:, 0:NT * E].rearrange("p (t e) -> p t e", e=E)

            def per_tile(k):
                return g16[:, k, :].unsqueeze(2).broadcast_to([P, NT, E])

            dve.tensor_reduce(g16[:, 0, :], gate, AX_X, ALU.max)
            dve.drain()
            dve.tensor_tensor(lg[:, :, :], gate, per_tile(0), ALU.subtract).then_inc(lg_ready, 1)
            dve.wait_ge(eg_ready, c + 1)
            dve.tensor_reduce(g16[:, 1, :], lg[:, :, :], AX_X, ALU.add)
            dve.drain()
            dve.reciprocal(g16[:, 1, :], g16[:, 1, :])
            dve.drain()
            dve.tensor_tensor(pr[:, :, :], lg[:, :, :], per_tile(1), ALU.mult)
            dve.drain()
            for t in range(NT):
                dve.max(top8[:, t, :], pr[:, t, :])
            dve.drain()
            for t in range(NT):
                dve.max_index(idx8[:, t, :], top8[:, t, :], pr[:, t, :])
            dve.tensor_tensor(g16[:, 2, :], top8[:, :, 0], top8[:, :, 1], ALU.add)
            dve.drain()
            dve.tensor_copy(idxf[:, :, :], idx8[:, :, 0:2])
            dve.reciprocal(g16[:, 2, :], g16[:, 2, :])
            dve.drain()
            for k in range(2):
                dve.tensor_tensor(oh[:, k, :, :], cst("iota8").unsqueeze(1).broadcast_to([P, NT, E]),
                                  idxf[:, :, k:k + 1].broadcast_to([P, NT, E]), ALU.is_equal)
            dve.drain()
            for k in range(2):
                dve.tensor_tensor(oh[:, k, :, :], oh[:, k, :, :], top8[:, :, k:k + 1].broadcast_to([P, NT, E]), ALU.mult)
            dve.drain()
            dve.tensor_tensor(oh[:, 0, :, :], oh[:, 0, :, :], oh[:, 1, :, :], ALU.add)
            dve.drain()
            dve.tensor_tensor(W8[:, :, :], oh[:, 0, :, :], per_tile(2), ALU.mult).then_inc(w8_ready, 1)
            dve.wait_ge(acc0_ready, NG * (c + 1))
            for k, op in ((0, ALU.mult), (1, ALU.add)):
                dve.drain()
                for g in range(NG):
                    dve.tensor_tensor(HN[:, 4 * g:4 * g + 4, :], HN[:, 4 * g:4 * g + 4, :],
                                      gains[:, k, :].unsqueeze(1).broadcast_to([P, 4, D]), op)
            run_experts(dve, dve_expert, c)
            dve.drain()
            for gq in range(NG):
                s = slice(4 * gq, 4 * gq + 4)
                dve.wait_ge(sum_turned, NG * c + gq + 1)
                dve.tensor_tensor(HN[:, s, :], HN[:, s, :], bank[gq][:, :].rearrange("p (t d) -> p t d", d=D), ALU.add)
            dve.drain()
            halves = dve_sums(dve, HN)
            for t in range(NT):
                dve.scalar_tensor_tensor(XN[:, t, :], HN[:, t, :], mv[:, t, 0:1], gains[:, 2, :], ALU.subtract, ALU.mult)
            for k, h in enumerate(halves):
                dve.wait_ge(rstd_ready, 2 * (ln + 2) + k + 1)
                dve.drain()
                for t in h:
                    m = dve.scalar_tensor_tensor(X[:, t, :], XN[:, t, :], rstd[:, t:t + 1], X[:, t, :], ALU.mult, ALU.add)
            m.then_inc(x_ready, 1)
            dve.drain()

        def dve_sel(dve):
            dve_norm(dve, X, XN, 3, xn_ready)
            dve.wait_ge(sig_ready, 2)
            dr, dc = delta_row, delta_col
            for d, at_ in ((dr, lambda k: dr[:, k, 0:HALF]), (dc, lambda k: dc[:, k:k + 1])):
                dve.tensor_scalar(at_(2), at_(1), 1.0, None, ALU.add)
                dve.drain()
                dve.reciprocal(at_(5), at_(2))
                dve.drain()
                dve.tensor_scalar(at_(1), at_(5), -2.0 * np.pi, np.pi, ALU.mult, ALU.add)
                dve.drain()
                dve.tensor_scalar(at_(1), at_(1), 3.1415925, -3.1415925, ALU.min, ALU.max)
                dve.tensor_scalar(at_(2), at_(5), -np.pi, None, ALU.mult).then_inc(ang_ready, 1)
            dve.memset(KL[DC:DC + DR, :, :], 0.0)
            dve.wait_ge(sel_w_loaded, 16 * 11)
            for n in range(4):
                dve.wait_ge(ki_done, n + 1)
                dve.tensor_copy(KI[:, n * BANK:(n + 1) * BANK], bank[n][:, :]).then_inc(ki_ready, 1)
            dve.wait_ge(trig_ready, 2)
            for d, at_ in ((dr, lambda k: dr[:, k, 0:HALF]), (dc, lambda k: dc[:, k:k + 1])):
                dve.tensor_tensor(at_(0), at_(4), at_(4), ALU.mult)
                dve.tensor_scalar(at_(1), at_(3), -1.0, None, ALU.mult)
                dve.drain()
                dve.tensor_scalar(at_(0), at_(0), -2.0, 1.0, ALU.mult, ALU.add)
                dve.drain()
            dve.tensor_tensor(dc[:, 1:2], dc[:, 1:2], cst("sign"), ALU.mult)
            for k in range(2):
                dve.tensor_copy(dr[:, k, HALF:DR], dr[:, k, 0:HALF])
            dve.drain()
            dve.tensor_scalar(dc[:, 2:3], dc[:, 1:2], -1.0, None, ALU.mult)
            dve.tensor_tensor(dr[:, 1, :], dr[:, 1, :], cst("sign_row"), ALU.mult)
            dve.drain()
            dve.tensor_tensor(rot_sel[:, 0:DR], cst("cos_sel"), dr[:, 0, :], ALU.mult)
            dve.tensor_tensor(dr[:, 2, :], cst("sin_sel"), dr[:, 1, :], ALU.mult)
            dve.tensor_tensor(rot_sel[:, DR:], cst("sin_sel"), dr[:, 0, :], ALU.mult)
            dve.tensor_tensor(dr[:, 3, :], cst("cos_sel"), dr[:, 1, :], ALU.mult)
            dve.drain()
            dve.tensor_tensor(rot_sel[:, 0:DR], rot_sel[:, 0:DR], dr[:, 2, :], ALU.subtract)
            dve.tensor_tensor(rot_sel[:, DR:], rot_sel[:, DR:], dr[:, 3, :], ALU.add)
            dve.wait_ge(rot_loaded, 16)
            for k in range(2):
                co, si = ROT[:, 2 * k, :], ROT[:, 2 * k + 1, :]
                dve.tensor_scalar(QRD[0], si, dc[:, 2:3], None, ALU.mult)
                dve.tensor_scalar(T1, co, dc[:, 1:2], None, ALU.mult)
                dve.drain()
                dve.scalar_tensor_tensor(co, co, dc[:, 0:1], QRD[0], ALU.mult, ALU.add)
                dve.scalar_tensor_tensor(si, si, dc[:, 0:1], T1, ALU.mult, ALU.add)
                dve.drain()
            for q in range(4):
                dve.wait_ge(kv_log, 1)
                src = bank[4 + q][:, :].rearrange("p (t n) -> p t n", n=P)
                rows = KVS[:, 4 * q:4 * q + 4, :]
                dve.tensor_copy(rows[:, :, 0:DC], src[:, :, 2 * DR:ROWKV])
                dve.scalar_tensor_tensor(rows[:, :, DC:ROWKV], src[:, :, 0:2 * DR], 0.0, rows[:, :, DC:ROWKV], ALU.max, ALU.add)\
                   .then_inc(kv_ready, 1)
            for n in range(4):
                b, t = n // 2, slice((n % 2) * BANK, (n % 2 + 1) * BANK)
                dve.wait_ge(kv_log, 1)
                m = ATTf[0:2 * DR, n * BANK:(n + 1) * BANK]
                dve.scalar_tensor_tensor(m, bank[n][0:2 * DR, :], 0.0, m, ALU.max, ALU.add)
                dve.drain()
                dve.tensor_tensor(QRD[0][0:DR, t], m[0:DR], ROT[0:DR, 0, t], ALU.mult)
                dve.tensor_tensor(QRL[0][0:DR, t], m[DR:2 * DR], ROT[DR:2 * DR, 1, t], ALU.mult)
                dve.drain()
                dve.tensor_tensor(KL[DC + DR:, b, LW + (n % 2) * BANK:LW + (n % 2 + 1) * BANK], QRD[0][0:DR, t], QRL[0][0:DR, t], ALU.add)
            dve.wait_ge(kt_c, 4)
            dve.drain()
            dve.tensor_copy(KL[:, :, 0:LW], KL[:, :, LW:2 * LW])
            m = dve.tensor_copy(KL[:, :, LW + L:LP], KL[:, :, LW:LW + LP - L - LW])
            m.then_inc(kl_ready, 1)
            for n in range(2 * B):
                halves = [slice(half * BANK, (half + 1) * BANK) for half in range(2)]
                dve.wait_ge(mu_log, n + 1)
                for half in range(2):
                    m = MU[n % 2][:, halves[half]]
                    dve.scalar_tensor_tensor(m, raw_bank(n, half)[:, :], 0.0, m, ALU.max, ALU.add).then_inc(mu_ready, 1)
                dve.drain()
                if n >= 2:
                    dve.wait_ge(q_placed[n % 2], 16 * 12 * (n // 2))
                for k, dst in ((0, QRD[n % 2]), (1, QRL[n % 2])):
                    dve.tensor_tensor(dst, MU[n % 2], ROT[:, 2 * k, :], ALU.mult)
                    for half in range(2):
                        dve.wait_ge(mus_done, 2 * n + half + 1)
                        dve.tensor_tensor(T1[:, halves[half]], bank[4 + half][:, :], ROT[:, 2 * k + 1, halves[half]], ALU.mult)
                    dve.drain()
                    dve.tensor_tensor(dst, dst, T1, ALU.add).then_inc(qr_ready, 1)
                    dve.drain()
            for tile in range(NT):
                dve_select(dve, tile)
            for i in range(2):
                dve.wait_ge(q_placed[i], 16 * 12 * B)
            for g in range(2):
                dve.memset(GTS[g][DC + DR:ROWKV], 0.0)
            run_blocks(dve, dve_ahead, dve_block)
            for gq in range(NG):
                dve.wait_ge(mix_done, gq + 1)
                m = dve.tensor_tensor(X[:, 4 * gq:4 * gq + 4, :], X[:, 4 * gq:4 * gq + 4, :],
                                      bank[gq][:, :].rearrange("p (t d) -> p t d", d=D), ALU.add)
            m.then_inc(x_ready, 1)
            dve.drain()

        def dve_select(dve, tile):
            b, tt = tile // TB, tile % TB
            w = tt * P + LW
            SC = SCORES[tile % 2]
            dve.wait_ge(sc_used, (tile + 1) * NIH)
            edge = min(w, P)
            dve.tensor_tensor(SC[:, w - edge:w], SC[:, w - edge:w], cst("nonlocal")[:, P - edge:P], ALU.min)
            for r in range(NSEL // 8):
                dve.drain()
                dve.max(best[:, r, :], SC[:, 0:w])
                dve.drain()
                dve.max_index(bidx[:, r, :], best[:, r, :], SC[:, 0:w])
                if r < NSEL // 8 - 1:
                    dve.match_replace(SC[:, 0:w], best[:, r, :], SC[:, 0:w], -3.3e38)
            dve.drain()
            f = bidf[:, tile % 2, :]
            if tile >= 2:
                dve.wait_ge(i_turned, tile - 1)
            dve.tensor_copy(f, bidx.rearrange("p r k -> p (r k)"))
            dve.drain()
            if tt == 0:
                dve.tensor_tensor(f, f, cst("keep"), ALU.mult)
                dve.drain()
                dve.tensor_tensor(f, f, cst("fill"), ALU.add)
                dve.drain()
            dve.tensor_scalar(f, f, float(b * LP + LW), None, ALU.add).then_inc(best_ready, 1)

        def dve_queries(dve, n, k):
            src = QALL[:, :, bass.ds(n * BT, BT)].rearrange("p h (g t) -> p g h t", t=4)
            dve.wait_ge(s_done, C0 + n - 1)
            dve.tensor_scalar(QS[k % 2].rearrange("p (g h t) -> p g h t", g=GB, h=NH), src, 1.0, None, ALU.mult).then_inc(qs_ready, 1)

        def dve_attended(dve, n, k):
            dst = OA[:, :, bass.ds(n * BT, BT)].rearrange("p h (g t) -> p g h t", t=4)
            dve.wait_ge(ob_done, C0 + n + 1)
            dve.tensor_scalar(dst, bank[6 + k % 2][0:DC, 0:P].rearrange("p (g h t) -> p g h t", g=GB, h=NH), 1.0, None, ALU.mult)\
               .then_inc(oa_ready, 1)

        def dve_ahead(dve, b, n, k, rows):
            dve_queries(dve, n, k)
            dve_rotate(dve, rows)

        def dve_rotate(dve, slot):
            rows, loaded, count = slot
            dve.drain()
            dve.wait_ge(loaded, count)
            dve.tensor_tensor(PRD, rows[:, :, DC:], rot_sel[:, :].unsqueeze(1).broadcast_to([P, GB, 2 * DR]), ALU.mult)
            dve.drain()
            dve.tensor_tensor(rows[:, :, DC:DC + DR], PRD[:, :, 0:DR], PRD[:, :, DR:], ALU.add).then_inc(rot_done, 1)

        def dve_block(dve, b, n, k, rows, ahead, early):
            c = col[:, k % 2, :]
            if ahead:
                dve_queries(dve, n + 1, (k + 1) % 4)
                dve_rotate(dve, ahead)
            dve.wait_ge(pb_exp, C0 + n - 1)
            dve.wait_ge(s_done, C0 + n + 1)
            dve.memset(c[:, 3:4], 0.0)
            dve.tensor_tensor_reduce(SM[k % 2], bank[k % 2][:, 0:2 * P], cst("mask_early" if early else "mask_main"), 1.0, -3e38,
                                     ALU.add, ALU.max, c[:, 0:1])
            dve.drain()
            dve.tensor_scalar(c[:, 1:2], c[:, 0:1], -SCALE2, None, ALU.mult).then_inc(sm_ready, 1)
            if not (early and k == 0):
                dve_attended(dve, n - 1, (k + 3) % 4)
            dve.wait_ge(pb_exp, C0 + n + 1)
            dve.reciprocal(c[:, 3:4], c[:, 2:3])
            dve.drain()
            dve.tensor_scalar(PB[k % 2], PB[k % 2], c[:, 3:4], None, ALU.mult).then_inc(pn_ready, 1)
            dve.wait_ge(ob_done, C0 + n - 1)
            dve.wait_ge(tp_done, C0 + n + 1)
            dve.tensor_copy(PTS[k % 2], bank[4 + k % 2][:, 0:2 * P]).then_inc(pts_ready, 1)
            if not ahead:
                dve_attended(dve, n, k)

        @block.sync
        def _(sp):
            sp.dma_start(X[:, :, :], attn["x"].rearrange("b (t p) d -> p (b t) d", p=P)).then_inc(x_loaded, 16)
            sp_expert(sp, 0, 0, 0)
            sp_expert(sp, 0, 1, 1)
            sp_sel_loads(sp)
            sp_ffn(sp, 0)
            sp_sel(sp)
            sp_ffn(sp, 1)
            sp.wait_ge(x_ready, 3)
            sp.dma_start(out.rearrange("b (t p) d -> p (b t) d", p=P), X[:, :, :]).then_inc(stored, 16)
            sp.wait_ge(stored, 16)

        @block.gpsimd
        def _(pool):
            pool.memset(neghalf[:, :], -0.5)
            pool.memset(spare[:, 0:1], 0.0).then_inc(setup_done, 1)
            pool.drain()
            pool_ffn(pool, 0)
            pool_sel(pool)
            pool_ffn(pool, 1)

        @block.tensor
        def _(pe):
            pe.wait_ge(const_loaded, 16)
            pe.wait_ge(w_loaded, 16 * 10)
            pe_ffn(pe, 0)
            pe_sel(pe)
            pe_ffn(pe, 1)

        @block.scalar
        def _(act):
            act.dma_start(const[:, :], const_ap).then_inc(const_loaded, 16)
            for dst, src in ((w_qkv[:, :], ffn["w_qkv"]), (w_o[:, :], ffn["w_o"]), (wg[:, :], ffn["wg"]),
                             (gains[:, 0, :], ffn["g1"].partition_broadcast(P)), (gains[:, 1, :], ffn["b1"].partition_broadcast(P)),
                             (gains[:, 2, :], ffn["g2"].partition_broadcast(P)), (gains[:, 3, :], ffn["b2"].partition_broadcast(P)),
                             (gain_col[:, 0:1], ffn["g1"].rearrange("(p a) -> p a", a=1)),
                             (gain_col[:, 1:2], ffn["b1"].rearrange("(p a) -> p a", a=1)), (bb2[:, :], ffn["bb2"])):
                act.dma_start(dst, src).then_inc(w_loaded, 16)
            act.wait_ge(setup_done, 1)
            act.activation(spare[:, 1:2], spare[:, 0:1], ACT.Copy).then_inc(exp_done, EXP0)
            act.activation(spare[:, 2:3], spare[:, 0:1], ACT.Copy).then_inc(gelu_done, GELU0)
            act_ffn(act, 0)
            act_sel(act)
            act_ffn(act, 1)

        @block.vector
        def _(dve):
            dve.memset(spare[:, 4:5], 0.0).then_inc(pv_done, PV0)
            dve.memset(spare[:, 5:6], 0.0).then_inc(o_turned, OTURN0)
            dve.memset(spare[:, 18:19], 0.0).then_inc(ot_ready, OT0)
            dve.memset(spare[:, 6:7], 0.0).then_inc(att_done, ATT0)
            dve.memset(spare[:, 7:8], 0.0).then_inc(y_done, Y0)
            dve.memset(spare[:, 8:9], 0.0).then_inc(acc_done, ACC0)
            dve.memset(spare[:, 9:10], 0.0).then_inc(max_done, MAX0)
            for x in range(8):
                m = (s_done, sm_ready, gts_ready, pb_exp, tp_done, pts_ready, ob_done, oa_ready)[x]
                dve.memset(spare[:, 10 + x:11 + x], 0.0).then_inc(m, C0)
            dve.wait_ge(x_loaded, 16)
            dve_ffn(dve, 0)
            dve_sel(dve)
            dve_ffn(dve, 1)


_INS = ["L0_attn_x", "L0_attn_W_dkv", "L0_attn_W_uk", "L0_attn_W_uv", "L0_attn_W_dq", "L0_attn_W_uq", "L0_attn_W_qr",
        "L0_attn_W_kr", "L0_attn_W_out", "L0_attn_idx_wq", "L0_attn_idx_wk", "L0_attn_idx_w", "L0_attn_raw_delta",
        "L0_ffn_w_qkv", "L0_ffn_w_o", "L0_ffn_g1", "L0_ffn_b1", "L0_ffn_wg", "L0_ffn_w1", "L0_ffn_bb1", "L0_ffn_w2",
        "L0_ffn_bb2", "L0_ffn_g2", "L0_ffn_b2"]


def kernel(**inputs):
    import concourse.bacc as bacc
    from concourse.bass_utils import run_bass_kernel_spmd

    nc = bacc.Bacc("TRN2", target_bir_lowering=False, num_devices=1)
    arrays, aps = {}, {}
    for name in _INS:
        a = np.ascontiguousarray(inputs[name])
        arrays[f"in_{name}"] = a
        aps[name] = nc.dram_tensor(f"in_{name}", a.shape, mybir.dt.from_np(a.dtype), kind="ExternalInput").ap()
    table = np.ascontiguousarray(np.concatenate(list(constants().values()), axis=1))
    arrays["in_constants"] = table
    const_ap = nc.dram_tensor("in_constants", table.shape, F32, kind="ExternalInput").ap()
    out = nc.dram_tensor("out_x", (B, L, D), F32, kind="ExternalOutput").ap()
    turns = rotations()
    arrays["in_rotations"] = turns
    rot_ap = nc.dram_tensor("in_rotations", turns.shape, F32, kind="ExternalInput").ap()
    build(nc, aps, const_ap, rot_ap, out)
    r = run_bass_kernel_spmd(nc, [arrays], core_ids=[0])
    return r.results[0]["out_x"]
```
